# Optimizing a Trainium2 kernel written in Bass

```python
import numpy as np
import jax
import jax.numpy as jnp

def _softmax(x, axis=-1):
    return jax.nn.softmax(x, axis=axis)

def _gelu(x):
    return jax.nn.gelu(x, approximate=True)

def _silu(x):
    return jax.nn.silu(x)

def _sigmoid(x):
    return jax.nn.sigmoid(x)

def _layernorm(x, axis=-1, eps=1e-05):
    m = jnp.mean(x, axis=axis, keepdims=True)
    v = jnp.var(x, axis=axis, keepdims=True)
    return (x - m) / jnp.sqrt(v + eps)

def _scatter_add(tgt, idx, src, axis=0):
    return tgt.at[idx].add(src)

def _segment_sum(src, seg, n):
    return jax.ops.segment_sum(src, seg, n)
kernel_name = 'mk_gps_d1_gnn_r8_5e74c3'

def setup_inputs(seed: int=0):
    np.random.seed(seed)
    _w = jnp.asarray

    def _rec_inputs():
        import jax
        import jax.numpy as jnp
        _gk = jax.random.key(seed)
        x = -8.776e-05 + 1 * jax.random.normal(jax.random.fold_in(_gk, 1), (6250, 256), jnp.float32)
        _s = jax.random.randint(jax.random.fold_in(_gk, 2), (50000,), 0, 6250, jnp.int32)
        _d = jax.random.randint(jax.random.fold_in(_gk, 3), (50000,), 0, 6250, jnp.int32)
        _loop = jnp.arange(6250, dtype=jnp.int32)
        src = jnp.concatenate([_s, _d, _loop])
        dst = jnp.concatenate([_d, _s, _loop])
        _o = jnp.argsort(dst, stable=True)
        src = src[_o]
        dst = dst[_o]
        edge_attr_64 = 0.000279952 + 1.00013 * jax.random.normal(jax.random.fold_in(_gk, 11), (106250, 64), jnp.float32)
        return (x, src, dst, edge_attr_64)
    x, src, dst, edge_attr_64 = _rec_inputs()

    def _L0_gnn_setup():
        import jax, jax.numpy as jnp
        import numpy as np
        N, E, H, ED = (2500, 40000, 256, 64)
        key = jax.random.key(seed)
        ks = jax.random.split(key, 12)

        def init_w(k, shape, fan_in):
            return (jax.random.normal(k, shape, jnp.float32) / np.sqrt(fan_in)).astype(jnp.float32)
        h = jax.random.normal(ks[0], (N, H), jnp.float32)
        edge_indices = jax.random.randint(ks[1], (2, E), 0, N, jnp.int32)
        edge_attr = jax.random.normal(ks[2], (E, ED), jnp.float32)
        din = 2 * H + ED
        W1 = init_w(ks[3], (H, din), din)
        b1 = jnp.zeros((H,), jnp.float32)
        W2 = init_w(ks[4], (H, H), H)
        b2 = jnp.zeros((H,), jnp.float32)
        W_ih = init_w(ks[5], (3 * H, H), H)
        b_ih = jnp.zeros((3 * H,), jnp.float32)
        W_hh = init_w(ks[6], (3 * H, H), H)
        b_hh = jnp.zeros((3 * H,), jnp.float32)
        return {'h': h, 'edge_indices': edge_indices, 'edge_attr': edge_attr, 'W1': W1, 'b1': b1, 'W2': W2, 'b2': b2, 'W_ih': W_ih, 'b_ih': b_ih, 'W_hh': W_hh, 'b_hh': b_hh}
    _L0_gnn_all = _L0_gnn_setup()
    _L0_gnn_in = {k: v for k, v in _L0_gnn_all.items() if k in ('W1', 'b1', 'W2', 'b2', 'W_ih', 'b_ih', 'W_hh', 'b_hh')}
    del _L0_gnn_all

    def _L0_mix_setup():
        import jax, jax.numpy as jnp
        import numpy as np
        HEADS = 8
        DIM_HEAD = 32
        SCALE = DIM_HEAD ** (-0.5)
        EPS = 1e-05

        def _layernorm_gamma(x, gamma):
            mu = jnp.mean(x, axis=-1, keepdims=True)
            var = jnp.var(x, axis=-1, keepdims=True)
            return (x - mu) * jax.lax.rsqrt(var + EPS) * gamma
        key = jax.random.key(seed)
        k1, k2, k3 = jax.random.split(key, 3)
        B, N, D = (8, 2048, 256)
        hidden = HEADS * DIM_HEAD
        x = jax.random.normal(k1, (B, N, D), dtype=jnp.float32)
        Wqkv = jax.random.normal(k2, (D, 3 * hidden), dtype=jnp.float32) * D ** (-0.5)
        Wout = jax.random.normal(k3, (hidden, D), dtype=jnp.float32) * hidden ** (-0.5)
        gamma = jnp.ones((D,), dtype=jnp.float32)
        return {'x': x, 'Wqkv': Wqkv, 'Wout': Wout, 'gamma': gamma}
    _L0_mix_all = _L0_mix_setup()
    _L0_mix_in = {k: v for k, v in _L0_mix_all.items() if k in ('Wqkv', 'Wout', 'gamma')}
    del _L0_mix_all

    def _L0_ffn_setup():
        import math
        import jax, jax.numpy as jnp
        import numpy as np
        CAPACITY_FACTOR = 1.25
        key = jax.random.key(seed)
        ks = jax.random.split(key, 5)
        B, L, D, F, E = (8, 1024, 256, 1024, 8)
        h = jax.random.normal(ks[0], (B, L, D), dtype=jnp.float32)
        gate_w = jax.random.normal(ks[1], (D, E), dtype=jnp.float32) * 0.02
        gate_b = jnp.zeros((E,), dtype=jnp.float32)
        w1 = jax.random.normal(ks[2], (E, D, F), dtype=jnp.float32) * (1.0 / math.sqrt(D))
        b1 = jnp.zeros((E, F), dtype=jnp.float32)
        w2 = jax.random.normal(ks[3], (E, F, D), dtype=jnp.float32) * (1.0 / math.sqrt(F))
        b2 = jnp.zeros((E, D), dtype=jnp.float32)
        return {'h': h, 'gate_w': gate_w, 'gate_b': gate_b, 'w1': w1, 'b1': b1, 'w2': w2, 'b2': b2}
    _L0_ffn_all = _L0_ffn_setup()
    _L0_ffn_in = {k: v for k, v in _L0_ffn_all.items() if k in ('gate_w', 'gate_b', 'w1', 'b1', 'w2', 'b2')}
    del _L0_ffn_all
    return {'x': x, 'src': src, 'dst': dst, 'edge_attr_64': edge_attr_64, 'L0_gnn_W1': _L0_gnn_in['W1'], 'L0_gnn_b1': _L0_gnn_in['b1'], 'L0_gnn_W2': _L0_gnn_in['W2'], 'L0_gnn_b2': _L0_gnn_in['b2'], 'L0_gnn_W_ih': _L0_gnn_in['W_ih'], 'L0_gnn_b_ih': _L0_gnn_in['b_ih'], 'L0_gnn_W_hh': _L0_gnn_in['W_hh'], 'L0_gnn_b_hh': _L0_gnn_in['b_hh'], 'L0_mix_Wqkv': _L0_mix_in['Wqkv'], 'L0_mix_Wout': _L0_mix_in['Wout'], 'L0_mix_gamma': _L0_mix_in['gamma'], 'L0_ffn_gate_w': _L0_ffn_in['gate_w'], 'L0_ffn_gate_b': _L0_ffn_in['gate_b'], 'L0_ffn_w1': _L0_ffn_in['w1'], 'L0_ffn_b1': _L0_ffn_in['b1'], 'L0_ffn_w2': _L0_ffn_in['w2'], 'L0_ffn_b2': _L0_ffn_in['b2']}

def reference(x, src, dst, edge_attr_64, L0_gnn_W1, L0_gnn_b1, L0_gnn_W2, L0_gnn_b2, L0_gnn_W_ih, L0_gnn_b_ih, L0_gnn_W_hh, L0_gnn_b_hh, L0_mix_Wqkv, L0_mix_Wout, L0_mix_gamma, L0_ffn_gate_w, L0_ffn_gate_b, L0_ffn_w1, L0_ffn_b1, L0_ffn_w2, L0_ffn_b2):
    import jax
    import jax.numpy as jnp

    def _L0_gnn_ref(h, edge_indices, edge_attr, W1, b1, W2, b2, W_ih, b_ih, W_hh, b_hh):
        import jax, jax.numpy as jnp
        import numpy as np
        N, E, H, ED = (2500, 40000, 256, 64)
        row, col = (edge_indices[0], edge_indices[1])
        edge_in = jnp.concatenate([h[row], h[col], edge_attr], axis=-1)
        msg = jax.nn.relu(edge_in @ W1.T + b1) @ W2.T + b2
        agg = jax.ops.segment_sum(msg, row, num_segments=h.shape[0])
        gx = agg @ W_ih.T + b_ih
        gh = h @ W_hh.T + b_hh
        xr, xz, xn = jnp.split(gx, 3, axis=-1)
        hr, hz, hn = jnp.split(gh, 3, axis=-1)
        r = jax.nn.sigmoid(xr + hr)
        z = jax.nn.sigmoid(xz + hz)
        n = jnp.tanh(xn + r * hn)
        h_new = (1.0 - z) * n + z * h
        return h_new

    def _L0_mix_ref(x, Wqkv, Wout, gamma):
        import jax, jax.numpy as jnp
        import numpy as np
        HEADS = 8
        DIM_HEAD = 32
        SCALE = DIM_HEAD ** (-0.5)
        EPS = 1e-05

        def _layernorm_gamma(x, gamma):
            mu = jnp.mean(x, axis=-1, keepdims=True)
            var = jnp.var(x, axis=-1, keepdims=True)
            return (x - mu) * jax.lax.rsqrt(var + EPS) * gamma
        B, N, D = x.shape
        qkv = x @ Wqkv
        q, k, v = jnp.split(qkv, 3, axis=-1)

        def to_heads(t):
            return t.reshape(B, N, HEADS, DIM_HEAD).transpose(0, 2, 1, 3)
        q, k, v = map(to_heads, (q, k, v))
        q = jax.nn.softmax(q, axis=-1) * SCALE
        k = jax.nn.softmax(k, axis=2)
        context = jnp.einsum('bhnd,bhne->bhde', k, v)
        out = jnp.einsum('bhde,bhnd->bhne', context, q)
        out = out.transpose(0, 2, 1, 3).reshape(B, N, HEADS * DIM_HEAD)
        out = out @ Wout
        return _layernorm_gamma(out, gamma)

    def _L0_ffn_ref(h, gate_w, gate_b, w1, b1, w2, b2):
        import math
        import jax, jax.numpy as jnp
        import numpy as np
        CAPACITY_FACTOR = 1.25
        B, L, D = h.shape
        E = gate_w.shape[1]
        T = B * L
        C = max(1, math.ceil(CAPACITY_FACTOR * T / E))
        x = h.reshape(T, D)
        logits = x @ gate_w + gate_b
        probs = jax.nn.softmax(logits, axis=-1)
        idx = jnp.argmax(probs, axis=-1)
        prb = jnp.take_along_axis(probs, idx[:, None], axis=1)[:, 0]
        one_hot = jax.nn.one_hot(idx, E, dtype=jnp.float32)
        pos = (jnp.cumsum(one_hot, axis=0) * one_hot).sum(-1).astype(jnp.int32) - 1
        kept = pos < C
        pos_safe = jnp.where(kept, pos, C)
        buf = jnp.zeros((E, C, D), dtype=h.dtype).at[idx, pos_safe].set(x, mode='drop')
        hmid = jax.nn.relu(jnp.einsum('ecd,edf->ecf', buf, w1) + b1[:, None, :])
        ybuf = jnp.einsum('ecf,efd->ecd', hmid, w2) + b2[:, None, :]
        pos_g = jnp.minimum(pos, C - 1)
        y_tok = ybuf[idx, pos_g] * (prb * kept)[:, None]
        y = y_tok.reshape(B, L, D)
        y = jnp.nan_to_num(y, nan=0.0, posinf=10000.0, neginf=-10000.0)
        return y
    edge_index = jnp.stack([src, dst])
    xn = _layernorm(x, axis=-1)
    x = x + _L0_gnn_ref(xn, edge_index, edge_attr_64, L0_gnn_W1, L0_gnn_b1, L0_gnn_W2, L0_gnn_b2, L0_gnn_W_ih, L0_gnn_b_ih, L0_gnn_W_hh, L0_gnn_b_hh) + _L0_mix_ref(xn[None], L0_mix_Wqkv, L0_mix_Wout, L0_mix_gamma)[0]
    x = x + _L0_ffn_ref(_layernorm(x, axis=-1)[None], L0_ffn_gate_w, L0_ffn_gate_b, L0_ffn_w1, L0_ffn_b1, L0_ffn_w2, L0_ffn_b2)[0]
    return x

_drawn_inputs = setup_inputs


def setup_inputs(seed=0):
    import zlib

    import numpy as np

    out = dict(_drawn_inputs(seed))
    spreads = {'L0_gnn_b1': (0.0, 0.1),
     'L0_gnn_b2': (0.0, 0.1),
     'L0_gnn_b_ih': (0.0, 0.529),
     'L0_gnn_b_hh': (0.0, 0.591),
     'L0_mix_gamma': (1.0, 0.2),
     'L0_ffn_gate_b': (0.0, 0.1),
     'L0_ffn_b1': (0.0, 0.8),
     'L0_ffn_b2': (0.0, 0.8)}
    factors = {}
    for name, (base, spread) in spreads.items():
        noise = np.random.default_rng([zlib.crc32(name.encode()), seed]).standard_normal(out[name].shape)
        drawn = base * np.exp(spread * noise) if base else spread * noise
        out[name] = jnp.asarray(drawn.astype(out[name].dtype))
    for name, factor in factors.items():
        out[name] = (out[name] * factor).astype(out[name].dtype)
    return out
```

```python
from contextlib import ExitStack

import concourse.bass as bass
import concourse.mybir as mybir
from concourse.alu_op_type import AluOpType as ALU

F32, BF16, I32, U16 = mybir.dt.float32, mybir.dt.bfloat16, mybir.dt.int32, mybir.dt.uint16
ACT = mybir.ActivationFunctionType
AX = mybir.AxisListType
OFF = bass.IndirectOffsetOnAxis
ds = bass.ds

P = 128
N, H, E, ED = 6250, 256, 106250, 64
H3 = 3 * H
HEADS, DH = 8, 32
NX, FF = 8, 1024
EPS = 1e-5
REAL = -(-N // P)
NT = REAL + REAL % 2
NTX = NT + 2
TAIL = N - (REAL - 1) * P
NB = REAL
EC = E // P
EREM = E - EC * P
CHUNKS = 3
CW = (EC + 1) // CHUNKS
HALF = 5
NS = EC // (2 * HALF)
PAIR = 2 * P
RING = 8
NG = -(-((E + NB * (PAIR - 1)) // PAIR) // RING) * RING
SLOTS = NG * PAIR
PR = 8
EW = ED + 2
SW = H + 1
CAP = -(-(5 * N) // (4 * NX))
CT = -(-CAP // P)
CLAST = CAP - (CT - 1) * P
XW = H + 1
ZERO_DMAS = NX * CAP // (8 * P) + (NX * CAP % (8 * P) >= P) + (NX * CAP % P > 0)
FMAX = 3.4028235e38
assert CHUNKS * CW == EC + 1 and NS * 2 * HALF == EC and SLOTS % (P * PR) == 0


class Shared:
    pass


class Arrays:

    def __init__(self, x, src, dst, edge_attr, W1, b1, W2, b2, W_ih, b_ih, W_hh, b_hh, Wqkv, Wout, gamma,
                 gate_w, gate_b, fw1, fb1, fw2, fb2, out):
        self.x, self.src, self.dst, self.edge_attr = x, src, dst, edge_attr
        self.W1, self.b1, self.W2, self.b2 = W1, b1, W2, b2
        self.W_ih, self.b_ih, self.W_hh, self.b_hh = W_ih, b_ih, W_hh, b_hh
        self.Wqkv, self.Wout, self.gamma = Wqkv, Wout, gamma
        self.gate_w, self.gate_b, self.fw1, self.fb1, self.fw2, self.fb2 = gate_w, gate_b, fw1, fb1, fw2, fb2
        self.out = out


class Chain:

    def __init__(self, eng, sem, n=0):
        self.eng, self.sem, self.n = eng, sem, n

    def then(self, ins):
        ins.then_inc(self.sem, 1)
        self.n = self.n + 1
        self.eng.wait_ge(self.sem, self.n)


def apart(s, eng):
    eng.sem_inc(s.carried, 1)


def credit(s, eng, sem, n):
    k = s.credits
    s.credits += 1
    eng.dma_start(s.credit_d[k:k + 1, :], s.zerob[0:1, :]).then_inc(sem, n)


def batch_norm_factors(v, ch, st, mean, var, tmp):
    me, qe, mo, qo = st[:, :, 1], st[:, :, 2], st[:, :, 4], st[:, :, 5]
    ch.then(v.tensor_tensor(mean, me, mo, ALU.add))
    ch.then(v.tensor_tensor(tmp, me, mo, ALU.subtract))
    ch.then(v.tensor_scalar(mean, mean, 0.5, None, ALU.mult))
    ch.then(v.tensor_tensor(tmp, tmp, tmp, ALU.mult))
    ch.then(v.tensor_tensor(var, qe, qo, ALU.add))
    ch.then(v.tensor_scalar(tmp, tmp, 0.25, EPS, ALU.mult, ALU.add))
    ch.then(v.tensor_scalar(var, var, 1.0 / H, None, ALU.mult))
    ch.then(v.tensor_tensor(var, var, tmp, ALU.add))


def prepare(nc, s, a):
    with ExitStack() as ctx:
        def sb(name, shape, dt=F32):
            return ctx.enter_context(nc.sbuf_tensor(name, shape, dt))

        sem = s.sem
        raw1 = s.big_s[:, 0:1152].rearrange("p (c f) -> p c f", c=2)
        raw_hh = s.big_s[:, 1152:2688].rearrange("p (c f) -> p c f", c=6)
        raw_ih = s.big_s[:, 2688:4224].rearrange("p (c f) -> p c f", c=6)
        raw2 = s.big_s[:, 4224:4736].rearrange("p (c f) -> p c f", c=2)
        raw1c = s.big_s[:, 4736:4992].rearrange("p (c f) -> p c f", c=2)
        prefill = s.big_s[:, 4992:4992 + PR * EW].rearrange("p (r w) -> p r w", w=EW)
        zrow = s.big_s[:, 5600:5856]
        x_all = s.big_p[:, 0:2 * NT * H].bitcast(F32)
        wihT = sb("wihT", [P, 2, H3])
        b2col = sb("b2col", [P, 2])
        src_i = sb("src_i", [P, EC + 1], I32)
        tmp_i = sb("tmp_i", [P, EC + 1], I32)
        bkt = sb("bkt", [P, EC + 1], BF16)
        eqm = sb("eqm", [P, EC + 1], BF16)
        slots = sb("slots", [P, CW])
        onesb = sb("onesb", [P, CW], BF16)
        cnt = sb("cnt", [P, NB])
        pairs_i = sb("pairs_i", [P, NB], I32)
        pairs = sb("pairs", [P, NB])
        incl = sb("incl", [P, NB])
        carry = sb("carry", [P, NB])
        inclT = sb("inclT", [NB, 1])
        iota_g = sb("iota_g", [P, NG])
        st = sb("st", [P, NT, 6])
        var = sb("var", [P, NT])
        tmp = sb("tmp", [P, NT])

        p_step = sem("p_step")
        masks, edges_in, filler = sem("masks_made"), sem("edges_in"), sem("filler_made")
        w_in, x_in, pad_out = sem("weights_in"), sem("x_in"), sem("padding_out")
        tr, ev = sem("weights_transposed"), sem("weights_evacuated")
        fold, folded = sem("fold_products"), sem("fold_evacuated")
        counted, sums, incl_ok, inclT_mm = sem("counted"), sem("sums"), sem("incl_made"), sem("inclT_mm")
        inclT_ok, ind_ok, blk_mm, varred, rooted = (sem("inclT_made"), sem("ind_made"), sem("blk_mm"),
                                                    sem("var_made"), sem("roots_made"))

        jobs = []
        for c in range(2):
            k = slice(c * P, (c + 1) * P)
            jobs.append((s.fused_w[:, c, 0:H], [raw1[:, m, k] for m in range(2)]))
            jobs.append((s.fused_w[:, c, 2 * H:3 * H], [raw1[:, m, H + c * P:H + (c + 1) * P] for m in range(2)]))
            for raw, wt in ((raw_hh, s.whhT), (raw_ih, wihT)):
                jobs.append((wt[:, c, 0:512], [raw[:, m, k] for m in range(4)]))
                jobs.append((wt[:, c, 512:H3], [raw[:, m, k] for m in range(4, 6)]))
        jobs.append((s.w1c[:, :], [raw1c[:, m, :] for m in range(2)]))
        folds = [(s.wg[:, jc, lo:hi], [(raw2[:, oc, jc * P:(jc + 1) * P], wihT[:, oc, lo:hi]) for oc in range(2)])
                 for jc in range(2) for lo, hi in ((0, 512), (512, H3))]
        folds += [(s.bg[0:1, lo:hi], [(b2col[:, oc:oc + 1], wihT[:, oc, lo:hi]) for oc in range(2)])
                  for lo, hi in ((0, 512), (512, H3))]

        with nc.Block() as block:
            @block.gpsimd
            def _(g):
                ch = Chain(g, p_step)
                g.memset(src_i[:, EC:EC + 1], NB * P)
                g.memset(s.dst_i[:, EC:EC + 1], 0).then_inc(masks, 1)
                g.memset(s.zerob[:, :], 0.0)
                ch.then(g.memset(prefill, 0.0))
                ch.then(g.memset(prefill[:, :, EW - 1:EW], -1.0))
                g.memset(zrow, 0.0).then_inc(filler, 1)
                ch.then(g.memset(s.ident[:, :], 0.0))
                ch.then(g.affine_select(out=s.ident[:, :], in_=s.ident[:, :], compare_op=ALU.not_equal, fill=1.0,
                                        base=0, pattern=[[-1, P]], channel_multiplier=1))
                ch.then(g.memset(s.ones[:, :], 1.0))
                g.affine_select(out=s.upper[:, :], in_=s.ones[:, :], compare_op=ALU.is_gt, fill=0.0,
                                base=0, pattern=[[1, P]], channel_multiplier=-1)
                g.memset(onesb[:, :], 1.0)
                g.iota(s.iota_f[:, :], pattern=[[1, P]], base=0, channel_multiplier=0,
                       allow_small_or_imprecise_dtypes=True)
                g.iota(s.node_f[:, :], pattern=[[P, NT]], base=0, channel_multiplier=1,
                       allow_small_or_imprecise_dtypes=True)
                g.iota(iota_g[:, :], pattern=[[1, NG]], base=0, channel_multiplier=0,
                       allow_small_or_imprecise_dtypes=True).then_inc(masks, 1)

            @block.sync
            def _(sp):
                sp.dma_start(src_i[:, 0:EC], a.src[0:EC * P].rearrange("(p c) -> p c", p=P)).then_inc(edges_in, 16)
                sp.dma_start(s.dst_i[:, 0:EC], a.dst[0:EC * P].rearrange("(p c) -> p c", p=P)).then_inc(edges_in, 16)
                sp.wait_ge(masks, 1)
                for to, of in ((src_i, a.src), (s.dst_i, a.dst)):
                    sp.dma_start(to[0:EREM, EC:EC + 1],
                                 of[EC * P:E].rearrange("(p c) -> p c", c=1)).then_inc(edges_in, 16)
                sp.dma_start(raw1, a.W1.rearrange("(c p) f -> p c f", p=P)).then_inc(w_in, 16)
                for k in range(2):
                    sp.dma_start(raw1c[:, :, k * ED:(k + 1) * ED],
                                 a.W1[:, 2 * H:2 * H + ED].rearrange("(c p) f -> p c f", p=P)).then_inc(w_in, 16)
                sp.dma_start(raw_hh, a.W_hh.rearrange("(c p) f -> p c f", p=P)).then_inc(w_in, 16)
                sp.dma_start(raw_ih, a.W_ih.rearrange("(c p) f -> p c f", p=P)).then_inc(w_in, 16)
                sp.dma_start(raw2, a.W2.rearrange("(c p) f -> p c f", p=P)).then_inc(w_in, 16)
                sp.dma_start(b2col[:, :], a.b2.rearrange("(c p) -> p c", p=P), allow_slow_non_contiguous=True).then_inc(w_in, 16)
                sp.dma_start(s.bg[1:2, :], a.b_ih.rearrange("(a f) -> a f", a=1)).then_inc(w_in, 16)
                qkv = a.Wqkv.rearrange("(c p) f -> p c f", p=P)
                sp.dma_start(s.fused_w[:, :, H:2 * H], qkv[:, :, 0:H]).then_inc(w_in, 16)
                sp.dma_start(s.wk[:, :, :], qkv[:, :, H:2 * H]).then_inc(w_in, 16)
                sp.dma_start(s.fused_w[:, :, 3 * H:4 * H], qkv[:, :, 2 * H:3 * H]).then_inc(w_in, 16)
                sp.dma_start(s.wout[:, :, :], a.Wout.rearrange("(c p) f -> p c f", p=P)).then_inc(w_in, 16)
                for to, of in ((s.b1b, a.b1), (s.bhhb, a.b_hh), (s.gammab, a.gamma), (s.gateb, a.gate_b)):
                    sp.dma_start(to[:, :], of.partition_broadcast(P)).then_inc(w_in, 16)
                sp.dma_start(s.gatew[:, :, :], a.gate_w.rearrange("(c p) e -> p c e", p=P)).then_inc(w_in, 16)
                x_rows = s.x_pad.rearrange("t p f -> (t p) f")
                sp.dma_start(x_rows[0:N, :], a.x).then_inc(pad_out, 16)
                sp.wait_ge(filler, 1)
                sp.dma_start(x_rows[N:REAL * P, :], zrow[0:REAL * P - N, :]).then_inc(pad_out, 16)
                for t in range(REAL, NTX):
                    sp.dma_start(s.x_pad[t], zrow).then_inc(pad_out, 16)
                sorted_v = s.sorted_d.rearrange("(k p r) w -> k p r w", p=P, r=PR)
                fills = SLOTS // (P * PR)
                with sp.Fori(0, fills) as k:
                    sp.dma_start(sorted_v[ds(k, 1)].rearrange("k p r w -> p (k r) w"), prefill).then_inc(pad_out, 16)
                sp.wait_ge(pad_out, 16 * (2 + NTX - REAL + fills))
                sp.dma_start(x_all.rearrange("p (t f) -> p t f", f=H),
                             s.x_pad[0:NT].rearrange("t p f -> p t f")).then_inc(x_in, 16)

            @block.tensor
            def _(pe):
                pe.wait_ge(w_in, 16 * 17)
                pe.wait_ge(masks, 2)
                for q, (to, ins) in enumerate(jobs):
                    if q >= 4:
                        pe.wait_ge(ev, q - 3)
                    for m, i in enumerate(ins):
                        last = nc.tensor.transpose(s.bank[q % 4][:, m * P:(m + 1) * P], i, s.ident[:, :])
                    last.then_inc(tr, 1)
                pe.wait_ge(ev, len(jobs))
                for q, (to, terms) in enumerate(folds):
                    if q >= 4:
                        pe.wait_ge(folded, q - 3)
                    rows, cols = to.shape
                    for n, (left, right) in enumerate(terms):
                        last = nc.tensor.matmul(s.bank[q % 4][0:rows, 0:cols], left, right,
                                                start=n == 0, stop=n == len(terms) - 1)
                    last.then_inc(fold, 1)
                pe.wait_ge(counted, 1)
                nc.tensor.matmul(s.bank[4][:, 0:NB], s.ones[:, :], cnt[:, :], start=True, stop=True)
                nc.tensor.matmul(s.bank[5][:, 0:NB], s.upper[:, :], cnt[:, :], start=True,
                                 stop=True).then_inc(sums, 1)
                pe.wait_ge(incl_ok, 1)
                nc.tensor.matmul(s.bank[4][0:NB, 0:1], incl[0:1, :], s.ones[0:1, 0:1], start=True,
                                 stop=True).then_inc(inclT_mm, 1)
                pe.wait_ge(ind_ok, 1)
                nc.tensor.matmul(s.bank[4][0:1, 0:NG], s.ones[0:NB, 0:1], iota_g[0:NB, :], start=True,
                                 stop=True).then_inc(blk_mm, 1)

            @block.scalar
            def _(act):
                for q, (to, ins) in enumerate(jobs):
                    act.wait_ge(tr, q + 1)
                    nc.scalar.copy(to, s.bank[q % 4][:, 0:P * len(ins)]).then_inc(ev, 1)
                for q, (to, terms) in enumerate(folds):
                    act.wait_ge(fold, q + 1)
                    rows, cols = to.shape
                    nc.scalar.copy(to, s.bank[q % 4][0:rows, 0:cols]).then_inc(folded, 1)
                act.wait_ge(varred, 1)
                nc.scalar.activation(s.rstd[:, :], var[:, :], ACT.Sqrt).then_inc(rooted, 1)

            @block.vector
            def _(v):
                ch = Chain(v, s.v_step, s.v_steps)
                v.wait_ge(edges_in, 64)
                v.wait_ge(masks, 2)
                ch.then(v.tensor_scalar(tmp_i[:, :], src_i[:, :], 7, None, ALU.arith_shift_right))
                ch.then(v.tensor_copy(bkt[:, :], tmp_i[:, :]))
                ch.then(v.tensor_scalar(tmp_i[:, :], src_i[:, :], P - 1, None, ALU.bitwise_and))
                ch.then(v.tensor_copy(s.rowl[:, :], tmp_i[:, :]))
                base = ch.n
                with v.Fori(0, NB) as b:
                    ch.n = base + b
                    ch.then(v.tensor_scalar(eqm[:, :], bkt[:, :], s.iota_f[:, ds(b, 1)], 0.0, ALU.is_equal, ALU.add,
                                            accum_out=cnt[:, ds(b, 1)]))
                ch.n = base + NB
                v.tensor_copy(pairs[:, :], cnt[:, :]).then_inc(counted, 1)
                v.wait_ge(sums, 1)
                ch.then(v.tensor_scalar(pairs_i[:, :], s.bank[4][:, 0:NB], float(PAIR - 1), None, ALU.add))
                ch.then(v.tensor_scalar(pairs_i[:, :], pairs_i[:, :], PAIR.bit_length() - 1, None, ALU.arith_shift_right))
                ch.then(v.tensor_copy(pairs[:, :], pairs_i[:, :]))
                ch.then(v.tensor_tensor_scan(incl[:, :], s.ones[:, 0:NB], pairs[:, :], 0.0, ALU.mult, ALU.add))
                v.tensor_tensor(carry[:, :], incl[:, :], pairs[:, :], ALU.subtract).then_inc(incl_ok, 1)
                v.wait_ge(incl_ok, 1)
                ch.then(v.tensor_scalar(carry[:, :], carry[:, :], float(PAIR), -1.0, ALU.mult, ALU.add))
                ch.then(v.tensor_tensor(carry[:, :], carry[:, :], s.bank[5][:, 0:NB], ALU.add))
                v.wait_ge(inclT_mm, 1)
                ch.then(v.tensor_copy(inclT[:, :], s.bank[4][0:NB, 0:1]))
                v.tensor_scalar(iota_g[0:NB, :], iota_g[0:NB, :], inclT[:, 0:1], None, ALU.is_ge).then_inc(ind_ok, 1)
                v.wait_ge(blk_mm, 1)
                ch.then(v.tensor_scalar(s.blk_i[0:1, :], s.bank[4][0:1, 0:NG], float(NB - 1), None, ALU.min))
                ch.then(v.memset(slots[:, :], 0.0))
                base = ch.n
                with v.Fori(0, CHUNKS) as k:
                    part = ds(k * CW, CW)
                    with v.Fori(0, NB) as b:
                        ch.n = base + (k * NB + b) * 3 + k
                        ch.then(v.tensor_scalar(eqm[:, 0:CW], bkt[:, part], s.iota_f[:, ds(b, 1)], None, ALU.is_equal))
                        ch.then(v.tensor_tensor_scan(s.bank[6][:, 0:CW], onesb[:, :], eqm[:, 0:CW],
                                                     carry[:, ds(b, 1)], ALU.mult, ALU.add))
                        apart(s, v)
                        v.copy_predicated(slots[:, :], eqm[:, 0:CW].bitcast(U16), s.bank[6][:, 0:CW])
                        ch.then(v.tensor_copy(carry[:, ds(b, 1)], s.bank[6][:, CW - 1:CW]))
                    ch.n = base + ((k + 1) * NB) * 3 + k
                    ch.then(v.tensor_copy(s.pos[:, part], slots[:, :]))
                ch.n = base + CHUNKS * (NB * 3 + 1)
                v.wait_ge(x_in, 16)
                base = ch.n
                with v.Fori(0, NT) as t:
                    ch.n = base + t
                    ch.then(v.bn_stats(st[:, ds(t, 1), :].rearrange("p a b -> p (a b)"), x_all[:, ds(t * H, H)]))
                ch.n = base + NT
                batch_norm_factors(v, ch, st, s.mean[:, :], var[:, :], tmp[:, :])
                v.tensor_copy(tmp[:, :], var[:, :]).then_inc(varred, 1)
                v.wait_ge(rooted, 1)
                ch.then(v.reciprocal(s.rstd[:, :], s.rstd[:, :]))
                s.v_steps = ch.n


def nodes(nc, s, a):
    with ExitStack() as ctx:
        def sb(name, shape, dt=F32):
            return ctx.enter_context(nc.sbuf_tensor(name, shape, dt))

        sem = s.sem

        ea = sb("ea", [P, 2, HALF, EW])
        slot_i = sb("slot_i", [P, 2, HALF], I32)
        rem = sb("rem", [16, EW])
        rem_i = sb("rem_i", [16, 1], I32)
        xt = sb("xt", [P, 2, H])
        xn = sb("xn", [P, 2, H])
        xnT = sb("xnT", [P, 2, 2, P])
        qt = sb("qt", [P, 2, H])
        vt = sb("vt", [P, 2, H])
        gh = sb("gh", [P, 2, H3])
        pf = sb("pf", [P, H])
        rest = sb("rest", [P, H])
        qe = sb("qe", [P, H])
        qs = sb("qs", [P, 2, H])
        qred = sb("qred", [P, 2, HEADS])
        kmax = sb("kmax", [P, 2])
        et, etok = (x[:, :, :].rearrange("p j (c n) -> p j c n", c=2) for x in (qt, vt))
        v1 = sb("v1", [P, 2, 2, P + 1])
        zero = sb("zero", [P, P + 1])
        blockmask = sb("blockmask", [P, P])
        den = sb("den", [P, 2])
        cx = sb("cx", [P, 2, P])
        cxT = sb("cxT", [P, 2, P])
        mix = sb("mix", [P, 2, H])
        qsl = sb("qsl", [P, 2, H])
        qsT, ot = xnT, qs
        st = sb("st2", [P, 6])
        mvt = sb("mvt", [P, 2])
        rs = sb("rs", [P, 1])
        kT = s.big_s[:, 0:2 * NT * P].rearrange("p (c n) -> p c n", c=2)

        p_step = sem("p2_step")
        ea_in, meta, scattered = sem("ea_in", 2), sem("meta_made"), sem("scattered", 2)
        rem_in, rem_meta, rem_out = sem("rem_in"), sem("rem_meta"), sem("rem_out")
        xt_in, xn_st = sem("xt_in", 2), sem("xn_stored", 2)
        xn_ok, x_tr, xnT_ok = sem("xn_made"), sem("xn_transposed"), sem("xnT_made")
        mm_pq, mm_qv, mm_ga, mm_gb, mm_k = (sem("mm_pq"), sem("mm_qv"), sem("mm_ga"), sem("mm_gb"), sem("mm_k"))
        fr_pq, fr_ga, fr_gb = sem("pq_used"), sem("ga_used"), sem("gb_used")
        q_ok, v_ok, k_ok = sem("q_evacuated"), sem("v_evacuated"), sem("k_evacuated")
        qv_st, gh_st, qs_st = sem("qv_stored", 2), sem("gh_stored", 2), sem("qs_stored", 2)
        gh_ok, qsub, qexp, qs_ok = sem("gh_made"), sem("q_shifted"), sem("q_exp"), sem("qs_made")
        const_ok, kmax_ok = sem("const_made"), sem("kmax_made")
        v_in, et_ok, e_tr, etok_ok, ctx_mm = sem("v_in", 2), sem("e_made"), sem("e_transposed"), sem("etok_made"), sem("context_mm")
        cx_ok, cx_tr, cxT_ok, m_mm, m_ok = sem("cx_made"), sem("cx_transposed"), sem("cxT_made"), sem("m_mm"), sem("m_made")
        qs_in, x2_in, qs_tr, qsT_ok, o_mm = sem("qs_in", 2), sem("x2_in", 2), sem("qs_transposed"), sem("qsT_made"), sem("o_mm")
        o_fr, o_var, o_root, ot_ok, ot_st = sem("o_used"), sem("o_var"), sem("o_root"), sem("ot_made"), sem("ot_stored", 2)

        ea_head = a.edge_attr[0:EC * P, :].rearrange("(p c) f -> p c f", p=P)

        def load_edges(sp, k):
            for h in range(2):
                sp.wait_ge(scattered[h], 16 * HALF * (k + 1))
                sp.dma_start(ea[:, h, :, 0:ED],
                             ea_head[:, ds((2 * k + h) * HALF, HALF), :]).then_inc(ea_in[h], 16)

        def make_meta(v, k):
            for h in range(2):
                v.wait_ge(scattered[h], 16 * HALF * (k + 1))
                cols = ds((2 * k + h) * HALF, HALF)
                v.tensor_copy(ea[:, h, :, ED:ED + 1].bitcast(I32).rearrange("p a b -> p (a b)"), s.dst_i[:, cols])
                v.tensor_copy(ea[:, h, :, ED + 1:EW].rearrange("p a b -> p (a b)"), s.rowl[:, cols])
                v.tensor_copy(slot_i[:, h, :], s.pos[:, cols]).then_inc(meta, 1)

        with nc.Block() as block:
            @block.gpsimd
            def _(g):
                for h in range(2):
                    credit(s, g, scattered[h], 16 * HALF)
                ch = Chain(g, p_step)
                g.memset(zero[:, :], 0.0)
                g.memset(v1[:, :, :, P:P + 1], 1.0)
                ch.then(g.memset(blockmask[:, :], 1.0))
                view = blockmask[:, :].rearrange("p (h e) -> p h e", e=DH)
                ch.then(g.affine_select(out=view, in_=view, compare_op=ALU.is_ge, fill=0.0, base=0,
                                        pattern=[[-DH, P // DH], [0, DH]], channel_multiplier=1))
                g.affine_select(out=view, in_=view, compare_op=ALU.is_ge, fill=0.0, base=DH - 1,
                                pattern=[[DH, P // DH], [0, DH]], channel_multiplier=-1).then_inc(const_ok, 1)
                with g.Fori(0, NS) as k:
                    for h in range(2):
                        g.wait_ge(ea_in[h], 16 * k + 16)
                        g.wait_ge(meta, 2 * k + h + 1)
                        apart(s, g)
                        for j in range(HALF):
                            g.indirect_dma_start(out=s.sorted_d, out_offset=OFF(ap=slot_i[:, h, j:j + 1], axis=0),
                                                 in_=ea[:, h, j, :], in_offset=None).then_inc(scattered[h], 16)
                g.wait_ge(rem_in, 16)
                g.wait_ge(rem_meta, 1)
                g.indirect_dma_start(out=s.sorted_d, out_offset=OFF(ap=rem_i[0:EREM, :], axis=0),
                                     in_=rem[0:EREM, :], in_offset=None).then_inc(rem_out, 16)
                g.wait_ge(rem_out, 16)
                for h in range(2):
                    g.wait_ge(scattered[h], 16 * HALF * (NS + 1))

            @block.sync
            def _(sp):
                for j in range(2):
                    sp.dma_start(xt[:, j, :], s.x_pad[j]).then_inc(xt_in[j], 16)
                    credit(s, sp, xn_st[j], 16)
                    credit(s, sp, qv_st[j], 32)
                    credit(s, sp, gh_st[j], 16)
                    credit(s, sp, qs_st[j], 16)
                    credit(s, sp, ot_st[j], 16)
                sp.dma_start(rem[0:EREM, 0:ED], a.edge_attr[EC * P:E, :]).then_inc(rem_in, 16)
                with sp.Fori(0, NT // 2) as i:
                    load_edges(sp, i)
                    for j in range(2):
                        t = 2 * i + j
                        one = ds(t, 1)
                        sp.wait_ge(xn_ok, t + 3)
                        sp.dma_start(s.xn_d[one].rearrange("t p f -> p (t f)"), xn[:, j, :]).then_inc(xn_st[j], 16)
                        sp.dma_start(xt[:, j, :], s.x_pad[ds(t + 2, 1)].rearrange("t p f -> p (t f)")).then_inc(xt_in[j], 16)
                        sp.wait_ge(v_ok, t + 3)
                        sp.dma_start(s.q_tiles[one].rearrange("t p f -> p (t f)"), qt[:, j, :]).then_inc(qv_st[j], 16)
                        sp.dma_start(s.v_d[one].rearrange("t p f -> p (t f)"), vt[:, j, :]).then_inc(qv_st[j], 16)
                        sp.wait_ge(qs_ok, t + 3)
                        sp.dma_start(s.qs_d[one].rearrange("t p f -> p (t f)"), qs[:, j, :]).then_inc(qs_st[j], 16)
                        sp.wait_ge(gh_ok, t + 3)
                        sp.dma_start(s.gh_d[one].rearrange("t p f -> p (t f)"), gh[:, j, :]).then_inc(gh_st[j], 16)
                for j in range(2):
                    sp.wait_ge(qv_st[j], 16 * NT + 32)
                with sp.Fori(0, NT // 2) as i:
                    load_edges(sp, i + NT // 2)
                    for j in range(2):
                        t = 2 * i + j
                        sp.wait_ge(ctx_mm, t + 1)
                        sp.dma_start(v1[:, j, :, 0:P],
                                     s.v_d[ds(t, 1)].rearrange("t p (c f) -> p (t c) f", c=2)).then_inc(v_in[j], 16)
                for j in range(2):
                    sp.wait_ge(qs_st[j], 8 * NT + 16)
                    sp.wait_ge(ctx_mm, NT + 2)
                with sp.Fori(0, NT // 2) as i:
                    load_edges(sp, i + NT)
                    for j in range(2):
                        t = 2 * i + j
                        sp.wait_ge(ot_ok, t + 1)
                        sp.wait_ge(qsT_ok, t + 1)
                        one = ds(t, 1)
                        sp.dma_start(qsl[:, j, :], s.qs_d[one].rearrange("t p f -> p (t f)")).then_inc(qs_in[j], 16)
                        sp.dma_start(xt[:, j, :], s.x_pad[one].rearrange("t p f -> p (t f)")).then_inc(x2_in[j], 16)
                with sp.Fori(0, NS - 3 * NT // 2) as i:
                    load_edges(sp, i + 3 * NT // 2)
                for j in range(2):
                    sp.wait_ge(xn_st[j], 8 * NT + 16)
                    sp.wait_ge(gh_st[j], 8 * NT + 16)

            @block.tensor
            def _(pe):
                pe.sem_inc(x_tr, 2)
                pe.sem_inc(mm_k, 2)
                with pe.Fori(0, NT // 2) as i:
                    for j in range(2):
                        t = 2 * i + j
                        pe.wait_ge(xn_ok, t + 3)
                        pe.wait_ge(xnT_ok, t + 1)
                        for c in range(2):
                            last = nc.tensor.transpose(s.bank[j][:, c * P:(c + 1) * P],
                                                       xn[:, j, c * P:(c + 1) * P], s.ident[:, :])
                        last.then_inc(x_tr, 1)
                    for j in range(2):
                        t = 2 * i + j
                        pe.wait_ge(xnT_ok, t + 3)

                        def product(bank, right, free, value, signal):
                            pe.wait_ge(free, value)
                            for c in range(2):
                                last = nc.tensor.matmul(s.bank[bank][:, 0:right.shape[2]], xnT[:, j, c, :],
                                                        right[:, c, :], start=c == 0, stop=c == 1)
                            last.then_inc(signal, 1)

                        product(2, s.fused_w[:, :, 0:512], fr_pq, t + 1, mm_pq)
                        product(3, s.fused_w[:, :, 512:1024], v_ok, t + 2, mm_qv)
                        product(4, s.whhT[:, :, 0:512], fr_ga, t + 1, mm_ga)
                        product(5, s.whhT[:, :, 512:H3], fr_gb, t + 1, mm_gb)
                        pe.wait_ge(k_ok, t + 1)
                        for m in range(2):
                            for c in range(2):
                                last = nc.tensor.matmul(s.bank[6][:, m * P:(m + 1) * P], s.wk[:, c, m * P:(m + 1) * P],
                                                        xnT[:, j, c, :], start=c == 0, stop=c == 1)
                        last.then_inc(mm_k, 1)
                pe.sem_inc(ctx_mm, 2)
                pe.sem_inc(e_tr, 2)
                pe.wait_ge(const_ok, 1)
                pe.wait_ge(fr_pq, NT + 1)
                pe.wait_ge(v_ok, NT + 2)
                for m in range(2):
                    nc.tensor.matmul(s.bank[2 + m][:, 0:P + 1], zero[:, 0:P], zero[:, :], start=True, stop=True)
                with pe.Fori(0, NT // 2) as i:
                    for j in range(2):
                        t = 2 * i + j
                        pe.wait_ge(et_ok, t + 3)
                        pe.wait_ge(etok_ok, t + 1)
                        for m in range(2):
                            last = nc.tensor.transpose(s.bank[j][:, m * P:(m + 1) * P], et[:, j, m, :], s.ident[:, :])
                        last.then_inc(e_tr, 1)
                    for j in range(2):
                        t = 2 * i + j
                        pe.wait_ge(etok_ok, t + 3)
                        pe.wait_ge(v_in[j], 16 * i + 16)
                        for m in range(2):
                            last = nc.tensor.matmul(s.bank[2 + m][:, 0:P + 1], etok[:, j, m, :], v1[:, j, m, :],
                                                    start=False, stop=True, skip_group_check=True)
                        last.then_inc(ctx_mm, 1)
                pe.wait_ge(cx_ok, 1)
                for m in range(2):
                    last = nc.tensor.transpose(s.bank[4][:, m * P:(m + 1) * P], cx[:, m, :], s.ident[:, :])
                last.then_inc(cx_tr, 1)
                pe.wait_ge(cxT_ok, 1)
                for m in range(2):
                    last = nc.tensor.matmul(s.bank[5][:, m * H:(m + 1) * H], cxT[:, m, :], s.wout[:, m, :],
                                            start=True, stop=True)
                last.then_inc(m_mm, 1)
                pe.wait_ge(m_ok, 1)
                pe.sem_inc(qs_tr, 2)
                pe.sem_inc(o_mm, 2)
                with pe.Fori(0, NT // 2) as i:
                    for j in range(2):
                        t = 2 * i + j
                        pe.wait_ge(qs_in[j], 16 * i + 16)
                        pe.wait_ge(qsT_ok, t + 1)
                        for m in range(2):
                            last = nc.tensor.transpose(s.bank[j][:, m * P:(m + 1) * P], qsl[:, j, m * P:(m + 1) * P],
                                                       s.ident[:, :])
                        last.then_inc(qs_tr, 1)
                    for j in range(2):
                        t = 2 * i + j
                        pe.wait_ge(qsT_ok, t + 3)
                        pe.wait_ge(o_fr, t + 1)
                        for m in range(2):
                            last = nc.tensor.matmul(s.bank[6 + j][:, 0:H], qsT[:, j, m, :], mix[:, m, :],
                                                    start=m == 0, stop=m == 1)
                        last.then_inc(o_mm, 1)

            @block.scalar
            def _(act):
                act.sem_inc(xnT_ok, 2)
                act.sem_inc(q_ok, 2)
                act.sem_inc(v_ok, 2)
                act.sem_inc(k_ok, 1)
                act.sem_inc(qexp, 1)
                with act.Fori(0, NT // 2) as i:
                    for j in range(2):
                        t = 2 * i + j
                        act.wait_ge(x_tr, t + 3)
                        act.wait_ge(mm_k, t + 1)
                        nc.scalar.copy(xnT[:, j, :, :], s.bank[j][:, 0:H].rearrange("p (c n) -> p c n", c=2)).then_inc(xnT_ok, 1)
                    for j in range(2):
                        t = 2 * i + j
                        act.wait_ge(mm_qv, t + 1)
                        act.wait_ge(qv_st[j], 32 * i + 32)
                        nc.scalar.copy(qt[:, j, :], s.bank[3][:, 0:H]).then_inc(q_ok, 1)
                        act.wait_ge(q_ok, t + 3)
                        nc.scalar.copy(vt[:, j, :], s.bank[3][:, H:2 * H]).then_inc(v_ok, 1)
                        act.wait_ge(qsub, t + 1)
                        nc.scalar.activation(qe[:, :], qe[:, :], ACT.Exp).then_inc(qexp, 1)
                        act.wait_ge(mm_k, t + 3)
                        nc.scalar.copy(kT[:, :, ds(t * P, P)], s.bank[6][:, 0:H].rearrange("p (c n) -> p c n", c=2)).then_inc(k_ok, 1)
                act.sem_inc(et_ok, 2)
                act.sem_inc(etok_ok, 2)
                act.wait_ge(kmax_ok, 1)
                for j in range(2):
                    act.wait_ge(qv_st[j], 16 * NT + 32)
                with act.Fori(0, NT // 2) as i:
                    for j in range(2):
                        t = 2 * i + j
                        act.wait_ge(e_tr, t + 1)
                        for m in range(2):
                            last = nc.scalar.activation(et[:, j, m, :], kT[:, m, ds(t * P, P)], ACT.Exp, bias=kmax[:, m:m + 1])
                        last.then_inc(et_ok, 1)
                    for j in range(2):
                        t = 2 * i + j
                        act.wait_ge(e_tr, t + 3)
                        act.wait_ge(ctx_mm, t + 1)
                        nc.scalar.copy(etok[:, j, :, :], s.bank[j][:, 0:H].rearrange("p (c n) -> p c n", c=2)).then_inc(etok_ok, 1)
                act.wait_ge(cx_tr, 1)
                nc.scalar.copy(cxT[:, :, :], s.bank[4][:, 0:H].rearrange("p (c n) -> p c n", c=2)).then_inc(cxT_ok, 1)
                act.wait_ge(m_mm, 1)
                nc.scalar.copy(mix[:, :, :], s.bank[5][:, :].rearrange("p (c n) -> p c n", c=2)).then_inc(m_ok, 1)
                act.sem_inc(qsT_ok, 2)
                with act.Fori(0, NT // 2) as i:
                    for j in range(2):
                        t = 2 * i + j
                        act.wait_ge(qs_tr, t + 3)
                        act.wait_ge(o_mm, t + 1)
                        nc.scalar.copy(qsT[:, j, :, :], s.bank[j][:, 0:H].rearrange("p (c n) -> p c n", c=2)).then_inc(qsT_ok, 1)
                    for j in range(2):
                        t = 2 * i + j
                        act.wait_ge(o_var, t + 1)
                        nc.scalar.activation(rs[:, :], rs[:, :], ACT.Sqrt).then_inc(o_root, 1)
                        act.wait_ge(ot_ok, t + 3)
                        act.dma_start(s.xm_d[ds(t, 1)].rearrange("t p f -> p (t f)"), ot[:, j, :]).then_inc(ot_st[j], 16)
                for j in range(2):
                    act.wait_ge(ot_st[j], 8 * NT + 16)

            @block.vector
            def _(v):
                ch = Chain(v, s.v_step, s.v_steps)
                v.sem_inc(xn_ok, 2)
                for k in (fr_pq, fr_ga, fr_gb):
                    v.sem_inc(k, 1)
                v.sem_inc(gh_ok, 2)
                v.sem_inc(qs_ok, 2)
                v.tensor_copy(rem[0:EREM, ED:ED + 1].bitcast(I32), s.dst_i[0:EREM, EC:EC + 1])
                v.tensor_copy(rem[0:EREM, ED + 1:EW], s.rowl[0:EREM, EC:EC + 1])
                v.tensor_copy(rem_i[0:EREM, :], s.pos[0:EREM, EC:EC + 1]).then_inc(rem_meta, 1)
                base = ch.n
                with v.Fori(0, NT // 2) as i:
                    make_meta(v, i)
                    for j in range(2):
                        t = 2 * i + j
                        v.wait_ge(xt_in[j], 16 * i + 16)
                        v.wait_ge(x_tr, t + 1)
                        v.wait_ge(xn_st[j], 16 * i + 16)
                        v.tensor_scalar(xn[:, j, :], xt[:, j, :], s.mean[:, ds(t, 1)], s.rstd[:, ds(t, 1)],
                                        ALU.subtract, ALU.mult).then_inc(xn_ok, 1)
                    for j in range(2):
                        t = 2 * i + j
                        ch.n = base + t * 8
                        o = t * H3
                        v.wait_ge(mm_pq, t + 1)
                        ch.then(v.tensor_tensor(pf[:, :], s.bank[2][:, 0:H], s.b1b[:, :], ALU.add))
                        q_ps = s.bank[2][:, H:2 * H].rearrange("p (h e) -> p h e", e=DH)
                        ch.then(v.tensor_reduce(qred[:, 0, :], q_ps, AX.X, ALU.max))
                        v.wait_ge(qs_ok, t + 2)
                        v.tensor_tensor(qe[:, :].rearrange("p (h e) -> p h e", e=DH), q_ps,
                                        qred[:, 0, :].unsqueeze(2).to_broadcast([P, HEADS, DH]), ALU.subtract).then_inc(qsub, 1)
                        v.wait_ge(qsub, t + 1)
                        v.sem_inc(fr_pq, 1)
                        ch.then(v.tensor_copy(s.big_p[:, ds(o, H)], pf[:, :]))
                        ch.then(v.tensor_tensor(rest[:, :], pf[:, :], s.big_p[:, ds(o, H)], ALU.subtract))
                        ch.then(v.tensor_copy(s.big_p[:, ds(o + H, H)], rest[:, :]))
                        v.tensor_tensor(s.big_p[:, ds(o + 2 * H, H)], rest[:, :], s.big_p[:, ds(o + H, H)], ALU.subtract)
                        v.wait_ge(gh_st[j], 16 * i + 16)
                        v.wait_ge(mm_ga, t + 1)
                        v.tensor_tensor(gh[:, j, 0:512], s.bank[4][:, :], s.bhhb[:, 0:512], ALU.add).then_inc(fr_ga, 1)
                        v.wait_ge(mm_gb, t + 1)
                        v.tensor_tensor(gh[:, j, 512:H3], s.bank[5][:, 0:H], s.bhhb[:, 512:H3], ALU.add).then_inc(fr_gb, 1)
                        v.wait_ge(fr_gb, t + 2)
                        v.sem_inc(gh_ok, 1)
                        v.wait_ge(qexp, t + 2)
                        qe_v = qe[:, :].rearrange("p (h e) -> p h e", e=DH)
                        ch.then(v.tensor_reduce(qred[:, 1, :], qe_v, AX.X, ALU.add))
                        ch.then(v.reciprocal(qred[:, 1, :], qred[:, 1, :]))
                        ch.then(v.tensor_scalar(qred[:, 1, :], qred[:, 1, :], DH ** -0.5, None, ALU.mult))
                        v.wait_ge(qs_st[j], 16 * i + 16)
                        v.tensor_tensor(qs[:, j, :].rearrange("p (h e) -> p h e", e=DH), qe_v,
                                        qred[:, 1, :].unsqueeze(2).to_broadcast([P, HEADS, DH]), ALU.mult).then_inc(qs_ok, 1)
                ch.n = base + NT * 8
                v.wait_ge(k_ok, NT + 1)
                for m in range(2):
                    ch.then(v.tensor_reduce(kmax[:, m:m + 1], kT[:, m, 0:N], AX.X, ALU.max))
                v.memset(kT[:, :, N:NT * P], -1e30)
                v.tensor_scalar(kmax[:, :], kmax[:, :], -1.0, None, ALU.mult).then_inc(kmax_ok, 1)
                with v.Fori(0, NT // 2) as i:
                    make_meta(v, i + NT // 2)
                v.wait_ge(ctx_mm, NT + 2)
                v.wait_ge(const_ok, 1)
                for m in range(2):
                    ch.then(v.reciprocal(den[:, m:m + 1], s.bank[2 + m][:, P:P + 1]))
                    ch.then(v.tensor_scalar(cx[:, m, :], s.bank[2 + m][:, 0:P], den[:, m:m + 1], None, ALU.mult))
                    last = v.tensor_tensor(cx[:, m, :], cx[:, m, :], blockmask[:, :], ALU.mult)
                last.then_inc(cx_ok, 1)
                for j in range(2):
                    v.wait_ge(qs_st[j], 8 * NT + 16)
                v.sem_inc(o_fr, 2)
                v.sem_inc(ot_ok, 2)
                base = ch.n
                with v.Fori(0, NT // 2) as i:
                    make_meta(v, i + NT)
                    for j in range(2):
                        t = 2 * i + j
                        ch.n = base + t * 6
                        v.wait_ge(o_mm, t + 3)
                        ch.then(v.bn_stats(st[:, :], s.bank[6 + j][:, 0:H]))
                        apart(s, v)
                        ch.then(v.bn_aggr(mvt[:, :], st[:, :]))
                        v.tensor_scalar(rs[:, :], mvt[:, 1:2], EPS, None, ALU.add).then_inc(o_var, 1)
                        v.wait_ge(o_root, t + 1)
                        ch.then(v.reciprocal(rs[:, :], rs[:, :]))
                        v.wait_ge(ot_st[j], 16 * i + 16)
                        ch.then(v.tensor_scalar(ot[:, j, :], s.bank[6 + j][:, 0:H], mvt[:, 0:1], rs[:, 0:1],
                                                ALU.subtract, ALU.mult))
                        v.sem_inc(o_fr, 1)
                        ch.then(v.tensor_tensor(ot[:, j, :], ot[:, j, :], s.gammab[:, :], ALU.mult))
                        v.wait_ge(x2_in[j], 16 * i + 16)
                        ch.then(v.tensor_tensor(ot[:, j, :], ot[:, j, :], xt[:, j, :], ALU.add))
                        v.sem_inc(ot_ok, 1)
                ch.n = base + NT * 6
                s.v_steps = ch.n
                with v.Fori(0, NS - 3 * NT // 2) as i:
                    make_meta(v, i + 3 * NT // 2)


def edges(nc, s, a):
    with ExitStack() as ctx:
        def sb(name, shape, dt=F32):
            return ctx.enter_context(nc.sbuf_tensor(name, shape, dt))

        sem = s.sem

        LOAD = RING // 2
        eb = sb("eb", [P, 2, LOAD, 2, EW])
        qg = sb("qg", [P, 4, 2, H])
        oh = sb("oh", [P, 4, 2, P])
        eaT = sb("eaT", [P, 2, P])
        ohT = sb("ohT", [P, 2, 2, P], BF16)
        hq = sb("hq", [P, 2, 2, H])
        r = sb("r", [P, 2, 2, SW])

        eb_in, gathered = sem("eb_in", 2), sem("gathered", 4)
        oh_ok, t_tr, t_ok, h_mm, h_ok, r_ok, s_mm, s_ok, r_one = (
            sem("onehot_made"), sem("transposed"), sem("transposes_evacuated"), sem("h_mm"), sem("h_summed"),
            sem("relu_made"), sem("s_mm"), sem("s_added"), sem("ones_made"))
        got = sem("gather_steps")

        src_v = s.sorted_d.rearrange("(k g p j) w -> k p g (j w)", g=LOAD, p=P, j=2)

        with nc.Block() as block:
            @block.sync
            def _(sp):
                with sp.Fori(0, NG // RING) as i:
                    for c in range(2):
                        g = RING * i + LOAD * c
                        sp.wait_ge(got, 2 * i + c + 1)
                        apart(s, sp)
                        sp.wait_ge(t_tr, g + LOAD)
                        sp.wait_ge(oh_ok, g + LOAD)
                        sp.dma_start(eb[:, c, :, :, :].rearrange("p g j w -> p g (j w)"),
                                     src_v[ds(2 * i + c, 1)].rearrange("k p g w -> p (k g) w")).then_inc(eb_in[c], 16)

            @block.gpsimd
            def _(g):
                g.sem_inc(got, 2)
                with g.Fori(0, NG // RING) as i:
                    for n in range(RING):
                        c, q = n // LOAD, n % 4
                        pair = RING * i + n
                        if n % LOAD == 0:
                            g.wait_ge(eb_in[c], 16 * i + 16)
                        g.wait_ge(h_ok, pair + 1)
                        apart(s, g)
                        for j in range(2):
                            g.indirect_dma_start(out=qg[:, q, j, :], out_offset=None, in_=s.q_tab,
                                                 in_offset=OFF(ap=eb[:, c, n % LOAD, j, ED:ED + 1].bitcast(I32), axis=0)
                                                 ).then_inc(gathered[q], 16)
                        if n % LOAD == LOAD - 1:
                            for k in range(4):
                                g.wait_ge(gathered[k], 64 * i + 32 * (n // 4) + 32)
                            g.sem_inc(got, 1)

            @block.tensor
            def _(pe):
                pe.sem_inc(t_tr, 8)
                pe.sem_inc(h_mm, 2)
                pe.sem_inc(s_mm, 4)

                def transposes(pair, n):
                    c, q, b = n // LOAD % 2, n % 4, n % 2
                    pe.wait_ge(oh_ok, pair + 9)
                    pe.wait_ge(t_ok, pair + 1)
                    for j in range(2):
                        nc.tensor.transpose(s.bank[b][:, (2 + j) * P:(3 + j) * P], oh[:, q, j, :], s.ident[:, :])
                        last = nc.tensor.transpose(s.bank[b][0:ED, j * P:(j + 1) * P], eb[:, c, n % LOAD, j, 0:ED], s.ident[:, :])
                    last.then_inc(t_tr, 1)

                def hidden(pair, n, block_of):
                    b = n % 2
                    pe.wait_ge(t_ok, pair + 3)
                    pe.wait_ge(h_ok, pair + 3)
                    for j in range(2):
                        nc.tensor.matmul(s.bank[2 + 2 * b + j][:, 0:H], eaT[j * ED:(j + 1) * ED, b, :],
                                         s.w1c[j * ED:(j + 1) * ED, :], start=True, stop=False)
                    for j in range(2):
                        for part in range(3):
                            last = nc.tensor.matmul(s.bank[2 + 2 * b + j][:, 0:H], ohT[:, b, j, :],
                                                    s.big_p[:, ds(block_of * H3 + part * H, H)],
                                                    start=False, stop=part == 2)
                    last.then_inc(h_mm, 1)

                def summed(pair, n):
                    b = n % 2
                    pe.wait_ge(r_ok, pair + 3)
                    pe.wait_ge(s_ok, pair + 1)
                    for j in range(2):
                        last = nc.tensor.matmul(s.bank[6 + b][:, 0:SW], oh[:, n % 4, j, :], r[:, b, j, :],
                                                start=j == 0, stop=j == 1)
                    last.then_inc(s_mm, 1)

                def turn(i, first, last):
                    _, blk = nc.values_load_multi_w_load_instructions(
                        s.blk_i[0:1, ds(RING * i, RING)], engines=(mybir.EngineType.PE,), min_val=0, max_val=NB - 1,
                        skip_runtime_bounds_check_because="the table is capped at the last block")
                    for n in range(RING):
                        pair = RING * i + n
                        if not (last and n == RING - 1):
                            transposes(pair + 1, (n + 1) % RING)
                        hidden(pair, n, blk[n])
                        if not (first and n == 0):
                            summed(pair - 1, (n - 1) % RING)

                transposes(0, 0)
                turn(0, True, False)
                with pe.Fori(1, NG // RING - 1) as i:
                    turn(i, False, False)
                turn(NG // RING - 1, False, True)
                summed(NG - 1, RING - 1)

            @block.scalar
            def _(act):
                act.sem_inc(t_ok, 2)
                act.sem_inc(r_ok, 2)

                def evacuate(pair, n):
                    b = n % 2
                    act.wait_ge(t_tr, pair + 9)
                    act.wait_ge(h_mm, pair + 1)
                    for j in range(2):
                        nc.scalar.copy(eaT[j * ED:(j + 1) * ED, b, :], s.bank[b][0:ED, j * P:(j + 1) * P])
                    nc.scalar.copy(ohT[:, b, :, :], s.bank[b][:, 2 * P:4 * P].rearrange("p (j n) -> p j n", j=2)).then_inc(t_ok, 1)

                def relu(pair, n):
                    b = n % 2
                    act.wait_ge(h_ok, pair + 5)
                    act.wait_ge(s_mm, pair + 3)
                    nc.scalar.activation(r[:, b, :, 0:H], hq[:, b, :, :], ACT.Relu).then_inc(r_ok, 1)

                act.wait_ge(r_one, 1)
                evacuate(0, 0)
                with act.Fori(0, NG // RING - 1) as i:
                    for n in range(RING):
                        evacuate(RING * i + n + 1, (n + 1) % RING)
                        relu(RING * i + n, n)
                for n in range(RING):
                    pair = NG - RING + n
                    if n < RING - 1:
                        evacuate(pair + 1, n + 1)
                    relu(pair, n)

            @block.vector
            def _(v):
                v.sem_inc(h_ok, 4)
                v.sem_inc(s_ok, 2)
                v.sem_inc(oh_ok, 8)
                v.memset(s.big_s[:, :], 0.0)
                v.memset(r[:, :, :, H:SW], 1.0).then_inc(r_one, 1)
                v.wait_ge(r_one, 1)

                def onehot(pair, n, load):
                    c, q = n // LOAD, n % 4
                    v.wait_ge(eb_in[c], load)
                    v.wait_ge(s_mm, pair + 1)
                    for j in range(2):
                        last = v.tensor_scalar(oh[:, q, j, :], s.iota_f[:, :], eb[:, c, n % LOAD, j, ED + 1:EW], None,
                                               ALU.is_equal)
                    last.then_inc(oh_ok, 1)

                def add_q(pair, n, uses):
                    b, q = n % 2, n % 4
                    v.wait_ge(h_mm, pair + 3)
                    v.wait_ge(gathered[q], uses)
                    v.wait_ge(r_ok, pair + 1)
                    for j in range(2):
                        last = v.tensor_tensor(hq[:, b, j, :], s.bank[2 + 2 * b + j][:, 0:H], qg[:, q, j, :], ALU.add)
                    last.then_inc(h_ok, 1)

                def add_s(pair, n, block_of):
                    b = n % 2
                    v.wait_ge(s_mm, pair + 5)
                    v.wait_ge(s_ok, pair + 2)
                    rows = s.big_s[:, ds(block_of * SW, SW)]
                    v.tensor_tensor(rows, rows, s.bank[6 + b][:, 0:SW], ALU.add).then_inc(s_ok, 1)

                def load_blocks(at, count):
                    _, blk = nc.values_load_multi_w_load_instructions(
                        s.blk_i[0:1, ds(at, count)], engines=(mybir.EngineType.DVE,), min_val=0, max_val=NB - 1,
                        skip_runtime_bounds_check_because="the table is capped at the last block")
                    return blk

                def turn(i, first, last):
                    blk = load_blocks(RING * i, RING) if first else load_blocks(RING * i - 1, RING)
                    for n in range(RING):
                        pair = RING * i + n
                        if not (last and n >= RING - 2):
                            m = (n + 2) % RING
                            onehot(pair + 2, m, 16 * (i + (n + 2) // RING) + 16)
                        add_q(pair, n, 64 * i + 32 * (n // 4) + 32)
                        if not (first and n == 0):
                            add_s(pair - 1, (n - 1) % RING, blk[n - 1] if first else blk[n])

                onehot(0, 0, 16)
                onehot(1, 1, 16)
                turn(0, True, False)
                with v.Fori(1, NG // RING - 1) as i:
                    turn(i, False, False)
                turn(NG // RING - 1, False, True)
                add_s(NG - 1, RING - 1, load_blocks(NG - 1, 1)[0])


def gru(nc, s, a):
    with ExitStack() as ctx:
        def sb(name, shape, dt=F32):
            return ctx.enter_context(nc.sbuf_tensor(name, shape, dt))

        sem = s.sem

        sums = sb("sums", [P, 2, SW])
        sT = sb("sT", [P, 2, 2, P])
        degT = sb("degT", [2, 2, P])
        ght = sb("ght", [P, 2, H3])
        xnt = sb("xnt", [P, 2, H])
        xmt = sb("xmt", [P, 2, H])
        rz = sb("rz", [P, 2, 2 * H])
        cand = sb("cand", [P, 2, H])

        gh_in, xn_in, xm_in = sem("gh_in", 2), sem("xnt_in", 2), sem("xm_in", 2)
        s_cp, s_tr, s_ok, rz_mm, n_mm = sem("sums_copied"), sem("sums_transposed"), sem("sT_made"), sem("rz_mm"), sem("n_mm")
        rz_in, rz_ok, c_in, c_ok, done, deg_one = (sem("rz_summed"), sem("rz_made"), sem("cand_summed"), sem("cand_made"),
                                                   sem("tile_done"), sem("deg_ones"))

        with nc.Block() as block:
            @block.sync
            def _(sp):
                with sp.Fori(0, NT // 2) as i:
                    for j in range(2):
                        one = ds(2 * i + j, 1)
                        sp.wait_ge(done, 2 * i + j + 1)
                        sp.dma_start(ght[:, j, :], s.gh_d[one].rearrange("t p f -> p (t f)")).then_inc(gh_in[j], 16)
                        sp.dma_start(xnt[:, j, :], s.xn_d[one].rearrange("t p f -> p (t f)")).then_inc(xn_in[j], 16)
                        sp.dma_start(xmt[:, j, :], s.xm_d[one].rearrange("t p f -> p (t f)")).then_inc(xm_in[j], 16)

            @block.tensor
            def _(pe):
                pe.sem_inc(s_tr, 2)
                pe.sem_inc(n_mm, 2)
                with pe.Fori(0, NT // 2) as i:
                    for j in range(2):
                        t = 2 * i + j
                        pe.wait_ge(s_cp, t + 3)
                        pe.wait_ge(s_ok, t + 1)
                        for c in range(2):
                            nc.tensor.transpose(s.bank[j][:, c * P:(c + 1) * P], sums[:, j, c * P:(c + 1) * P], s.ident[:, :])
                        nc.tensor.transpose(s.bank[j][0:1, 2 * P:3 * P], sums[:, j, H:SW], s.ident[:, :]).then_inc(s_tr, 1)
                    for j in range(2):
                        t = 2 * i + j
                        pe.wait_ge(s_ok, t + 3)
                        pe.wait_ge(c_in, t + 1)
                        for bank, lo, hi, signal in ((2 + j, 0, 512, rz_mm), (4 + j, 512, H3, n_mm)):
                            for c in range(2):
                                nc.tensor.matmul(s.bank[bank][:, 0:hi - lo], sT[:, j, c, :], s.wg[:, c, lo:hi],
                                                 start=c == 0, stop=False)
                            nc.tensor.matmul(s.bank[bank][:, 0:hi - lo], degT[:, j, :], s.bg[:, lo:hi],
                                             start=False, stop=True).then_inc(signal, 1)

            @block.scalar
            def _(act):
                act.sem_inc(s_ok, 2)
                act.wait_ge(deg_one, 1)
                with act.Fori(0, NT // 2) as i:
                    for j in range(2):
                        t = 2 * i + j
                        act.wait_ge(s_tr, t + 3)
                        act.wait_ge(n_mm, t + 1)
                        nc.scalar.copy(degT[0:1, j, :], s.bank[j][0:1, 2 * P:3 * P])
                        nc.scalar.copy(sT[:, j, :, :], s.bank[j][:, 0:H].rearrange("p (c n) -> p c n", c=2)).then_inc(s_ok, 1)
                    for j in range(2):
                        t = 2 * i + j
                        act.wait_ge(rz_in, t + 1)
                        nc.scalar.activation(rz[:, j, :], rz[:, j, :], ACT.Sigmoid).then_inc(rz_ok, 1)
                        act.wait_ge(c_in, t + 3)
                        nc.scalar.activation(cand[:, j, :], cand[:, j, :], ACT.Tanh).then_inc(c_ok, 1)

            @block.vector
            def _(v):
                ch = Chain(v, s.v_step, s.v_steps)
                v.sem_inc(done, 2)
                v.sem_inc(s_cp, 2)
                v.sem_inc(c_in, 2)
                v.memset(degT[:, :, :], 1.0).then_inc(deg_one, 1)
                base = ch.n
                with v.Fori(0, NT // 2) as i:
                    for j in range(2):
                        t = 2 * i + j
                        v.wait_ge(s_tr, t + 1)
                        v.tensor_copy(sums[:, j, :], s.big_s[:, ds(t * SW, SW)]).then_inc(s_cp, 1)
                    for j in range(2):
                        t = 2 * i + j
                        v.wait_ge(rz_mm, t + 1)
                        v.wait_ge(gh_in[j], 16 * i + 16)
                        v.tensor_tensor(rz[:, j, :], s.bank[2 + j][:, :], ght[:, j, 0:512], ALU.add).then_inc(rz_in, 1)
                    for j in range(2):
                        t = 2 * i + j
                        ch.n = base + t * 6
                        v.wait_ge(rz_ok, t + 1)
                        v.wait_ge(n_mm, t + 3)
                        ch.then(v.tensor_tensor(cand[:, j, :], rz[:, j, 0:H], ght[:, j, 512:H3], ALU.mult))
                        v.tensor_tensor(cand[:, j, :], cand[:, j, :], s.bank[4 + j][:, 0:H], ALU.add).then_inc(c_in, 1)
                        v.wait_ge(c_ok, t + 1)
                        v.wait_ge(xn_in[j], 16 * i + 16)
                        v.wait_ge(xm_in[j], 16 * i + 16)
                        x1 = s.x1_all[:, ds(t * H, H)]
                        ch.then(v.tensor_tensor(xnt[:, j, :], xnt[:, j, :], cand[:, j, :], ALU.subtract))
                        ch.then(v.tensor_tensor(xnt[:, j, :], xnt[:, j, :], rz[:, j, H:2 * H], ALU.mult))
                        ch.then(v.tensor_tensor(xmt[:, j, :], xmt[:, j, :], cand[:, j, :], ALU.add))
                        ch.then(v.tensor_tensor(x1, xmt[:, j, :], xnt[:, j, :], ALU.add))
                        ch.then(v.bn_stats(s.st2[:, ds(t, 1), :].rearrange("p a b -> p (a b)"), x1))
                        v.sem_inc(done, 1)
                s.v_steps = base + NT * 6


def routing(nc, s, a):
    with ExitStack() as ctx:
        def sb(name, shape, dt=F32):
            return ctx.enter_context(nc.sbuf_tensor(name, shape, dt))

        sem = s.sem

        W = NT * NX
        var, tmp = sb("var2", [P, NT]), sb("tmp2", [P, NT])
        mean, rstd = sb("mean2", [P, NT]), sb("rstd2", [P, NT])
        xl = sb("xl", [P, 2, H])
        xlT = sb("xlT", [P, 2, 2, P])
        lg, pr, t1, t2, t3 = (sb(n, [P, NT, NX]) for n in ("lg", "pr", "t1", "t2", "t3"))
        keyv = sb("keyv", [P, NX])
        basev = sb("basev", [P, NX])
        m1, m2, valid, gate = (sb(n, [P, NT]) for n in ("m1", "m2", "valid", "gate"))
        xr = sb("xr", [P, 4, XW])
        xi = sb("xi", [P, 4], I32)
        zrow = sb("zrow2", [P, 8, XW])

        var_ok, root_ok = sem("var2_made"), sem("root2_made")
        xl_ok, xl_tr, xlT_ok, lg_mm, lg_ok = sem("xl_made"), sem("xl_transposed"), sem("xlT_made"), sem("lg_mm"), sem("lg_made")
        sh_ok, ex_ok, oh_ok, rank_mm = sem("shifted"), sem("exp_made"), sem("onehot2_made"), sem("rank_mm")
        z_ok, z_out, xr_ok, xr_out = sem("zeros_made"), sem("zeros_out"), sem("xr_made"), sem("xr_out", 2)

        def flat(x):
            return x[:, :, :].rearrange("p t e -> p (t e)")

        def over(x, t=NT):
            return x.unsqueeze(2).to_broadcast([P, t, NX])

        with nc.Block() as block:
            @block.sync
            def _(sp):
                sp.wait_ge(z_ok, 1)
                rows, step = NX * CAP, P * 8
                n = 0
                for at in range(0, rows - step + 1, step):
                    sp.dma_start(s.routed_d[at:at + step, :].rearrange("(p r) w -> p r w", r=8), zrow[:, :, :]).then_inc(z_out, 16)
                    n += 1
                rest = rows - n * step
                if rest >= P:
                    k = rest // P
                    sp.dma_start(s.routed_d[rows - rest:rows - rest + k * P, :].rearrange("(p r) w -> p r w", r=k),
                                 zrow[:, 0:k, :]).then_inc(z_out, 16)
                    n += 1
                    rest -= k * P
                if rest:
                    sp.dma_start(s.routed_d[rows - rest:rows, :], zrow[0:rest, 0, :]).then_inc(z_out, 16)
                    n += 1
                assert n == ZERO_DMAS
                sp.wait_ge(z_out, 16 * n)

            @block.gpsimd
            def _(g):
                g.memset(zrow[:, :, :], 0.0).then_inc(z_ok, 1)
                for q in range(2):
                    credit(s, g, xr_out[q], 16)
                g.wait_ge(z_out, 16 * ZERO_DMAS)
                with g.Fori(0, NT // 2) as i:
                    for j in range(2):
                        g.wait_ge(xr_ok, 2 * i + j + 1)
                        apart(s, g)
                        g.indirect_dma_start(out=s.routed_d, out_offset=OFF(ap=xi[:, j:j + 1], axis=0),
                                             in_=xr[:, j, :], in_offset=None, bounds_check=NX * CAP - 1,
                                             oob_is_err=False).then_inc(xr_out[j], 16)
                for j in range(2):
                    g.wait_ge(xr_out[j], 8 * NT + 16)

            @block.tensor
            def _(pe):
                pe.sem_inc(xl_tr, 2)
                pe.sem_inc(lg_mm, 2)
                with pe.Fori(0, NT // 2) as i:
                    for j in range(2):
                        t = 2 * i + j
                        pe.wait_ge(xl_ok, t + 1)
                        pe.wait_ge(xlT_ok, t + 1)
                        for c in range(2):
                            last = nc.tensor.transpose(s.bank[j][:, c * P:(c + 1) * P], xl[:, j, c * P:(c + 1) * P], s.ident[:, :])
                        last.then_inc(xl_tr, 1)
                    for j in range(2):
                        t = 2 * i + j
                        pe.wait_ge(xlT_ok, t + 3)
                        pe.wait_ge(lg_ok, t + 1)
                        for c in range(2):
                            last = nc.tensor.matmul(s.bank[2 + j][:, 0:NX], xlT[:, j, c, :], s.gatew[:, c, :],
                                                    start=c == 0, stop=c == 1)
                        last.then_inc(lg_mm, 1)
                pe.wait_ge(oh_ok, 1)
                nc.tensor.matmul(s.bank[4][:, 0:W], s.upper[:, :], flat(t1), start=True, stop=True)
                nc.tensor.matmul(s.bank[5][:, 0:W], s.ones[:, :], flat(t1), start=True, stop=True).then_inc(rank_mm, 1)

            @block.scalar
            def _(act):
                act.wait_ge(var_ok, 1)
                nc.scalar.activation(rstd[:, :], var[:, :], ACT.Sqrt).then_inc(root_ok, 1)
                act.sem_inc(xlT_ok, 2)
                with act.Fori(0, NT // 2) as i:
                    for j in range(2):
                        t = 2 * i + j
                        act.wait_ge(xl_tr, t + 3)
                        act.wait_ge(lg_mm, t + 1)
                        nc.scalar.copy(xlT[:, j, :, :], s.bank[j][:, 0:H].rearrange("p (c n) -> p c n", c=2)).then_inc(xlT_ok, 1)
                act.wait_ge(sh_ok, 1)
                nc.scalar.activation(flat(lg), flat(lg), ACT.Exp).then_inc(ex_ok, 1)

            @block.vector
            def _(v):
                ch = Chain(v, s.v_step, s.v_steps)
                batch_norm_factors(v, ch, s.st2, mean[:, :], var[:, :], tmp[:, :])
                v.tensor_copy(tmp[:, :], var[:, :]).then_inc(var_ok, 1)
                v.wait_ge(root_ok, 1)
                ch.then(v.reciprocal(rstd[:, :], rstd[:, :]))
                v.sem_inc(lg_ok, 2)
                with v.Fori(0, NT // 2) as i:
                    for j in range(2):
                        t = 2 * i + j
                        v.wait_ge(xl_tr, t + 1)
                        v.tensor_scalar(xl[:, j, :], s.x1_all[:, ds(t * H, H)], mean[:, ds(t, 1)], rstd[:, ds(t, 1)],
                                        ALU.subtract, ALU.mult).then_inc(xl_ok, 1)
                    for j in range(2):
                        t = 2 * i + j
                        v.wait_ge(lg_mm, t + 3)
                        v.tensor_tensor(lg[:, ds(t, 1), :].rearrange("p a e -> p (a e)"), s.bank[2 + j][:, 0:NX],
                                        s.gateb[:, :], ALU.add).then_inc(lg_ok, 1)
                v.wait_ge(lg_ok, NT + 2)
                ch.then(v.tensor_reduce(m1[:, :], lg[:, :, :], AX.X, ALU.max))
                v.tensor_tensor(lg[:, :, :], lg[:, :, :], over(m1[:, :]), ALU.subtract).then_inc(sh_ok, 1)
                v.wait_ge(ex_ok, 1)
                ch.then(v.tensor_reduce(m1[:, :], lg[:, :, :], AX.X, ALU.add))
                ch.then(v.reciprocal(m1[:, :], m1[:, :]))
                ch.then(v.tensor_tensor(pr[:, :, :], lg[:, :, :], over(m1[:, :]), ALU.mult))
                ch.then(v.tensor_reduce(gate[:, :], pr[:, :, :], AX.X, ALU.max))
                ch.then(v.tensor_scalar(keyv[:, :], s.iota_f[:, 0:NX], -1.0, float(NX), ALU.mult, ALU.add))
                ch.then(v.tensor_tensor(t1[:, :, :], pr[:, :, :], over(gate[:, :]), ALU.is_equal))
                ch.then(v.tensor_tensor(t1[:, :, :], t1[:, :, :], keyv[:, :].unsqueeze(1).to_broadcast([P, NT, NX]), ALU.mult))
                ch.then(v.tensor_reduce(m1[:, :], t1[:, :, :], AX.X, ALU.max))
                ch.then(v.tensor_tensor(t1[:, :, :], t1[:, :, :], over(m1[:, :]), ALU.is_equal))
                ch.then(v.tensor_scalar(valid[:, :], s.node_f[:, :], float(N), None, ALU.is_lt))
                v.tensor_tensor(t1[:, :, :], t1[:, :, :], over(valid[:, :]), ALU.mult).then_inc(oh_ok, 1)
                v.wait_ge(rank_mm, 1)
                ch.then(v.tensor_copy(flat(t2), s.bank[5][:, 0:W]))
                for e in range(NX):
                    last = v.tensor_tensor_scan(t3[:, :, e], s.ones[:, 0:NT], t2[:, :, e], 0.0, ALU.mult, ALU.add)
                ch.then(last)
                ch.then(v.tensor_tensor(flat(t3), flat(t3), flat(t2), ALU.subtract))
                ch.then(v.tensor_tensor(flat(t3), flat(t3), s.bank[4][:, 0:W], ALU.add))
                ch.then(v.tensor_tensor(flat(t2), flat(t3), flat(t1), ALU.mult))
                ch.then(v.tensor_reduce(m1[:, :], t2[:, :, :], AX.X, ALU.add))
                ch.then(v.tensor_scalar(s.kept[:, :], m1[:, :], float(CAP), None, ALU.is_lt))
                ch.then(v.tensor_tensor(s.kept[:, :], s.kept[:, :], valid[:, :], ALU.mult))
                ch.then(v.tensor_scalar(basev[:, :], s.iota_f[:, 0:NX], float(CAP), None, ALU.mult))
                ch.then(v.tensor_tensor(t2[:, :, :], t1[:, :, :], basev[:, :].unsqueeze(1).to_broadcast([P, NT, NX]), ALU.mult))
                ch.then(v.tensor_reduce(m2[:, :], t2[:, :, :], AX.X, ALU.add))
                ch.then(v.tensor_tensor(m1[:, :], m1[:, :], m2[:, :], ALU.add))
                ch.then(v.tensor_tensor(m1[:, :], m1[:, :], s.kept[:, :], ALU.mult))
                ch.then(v.tensor_copy(s.place[:, :], m1[:, :]))
                ch.then(v.tensor_scalar(m2[:, :], s.kept[:, :], -float(2 * NX * CAP), float(2 * NX * CAP), ALU.mult, ALU.add))
                ch.then(v.tensor_tensor(m1[:, :], m1[:, :], m2[:, :], ALU.add))
                s.v_steps = ch.n
                with v.Fori(0, NT // 2) as i:
                    for j in range(2):
                        t = 2 * i + j
                        v.wait_ge(xr_out[j], 16 * i + 16)
                        v.tensor_scalar(xr[:, j, 0:H], s.x1_all[:, ds(t * H, H)], mean[:, ds(t, 1)], rstd[:, ds(t, 1)],
                                        ALU.subtract, ALU.mult)
                        v.tensor_copy(xr[:, j, H:XW], gate[:, ds(t, 1)])
                        v.tensor_copy(xi[:, j:j + 1], m1[:, ds(t, 1)]).then_inc(xr_ok, 1)


def experts(nc, s, a):
    with ExitStack() as ctx:
        def sb(name, shape, dt=F32):
            return ctx.enter_context(nc.sbuf_tensor(name, shape, dt))

        sem = s.sem

        FT = FF // P
        HALVES = ((0, -(-CAP // 2)), (-(-CAP // 2), CAP))
        w1 = sb("w1", [P, 2, 2, FF])
        w2 = sb("w2", [P, 2, FT, H])
        b1raw = sb("b1raw", [NX * FT, P])
        b1T = sb("b1T", [P, NX * FT])
        b1e = sb("b1e", [P, 2, FT])
        b2b = sb("b2b", [P, 2, H])
        xg = sb("xg", [P, 2, CT, XW])
        xT = s.big_s[:, 0:2 * CT * P].rearrange("p (c n) -> p c n", c=2)
        hT = s.big_s[:, 2 * CT * P:(2 + FT) * CT * P].rearrange("p (f n) -> p f n", f=FT)
        y = sb("y", [P, 2, H])
        fix = sb("fix", [P, 2])
        mask = sb("mask", [P, 3, H], I32)

        b1_in, b1_tr, b1_ok = sem("b1_in"), sem("b1_tr"), sem("b1_made")
        w_in, x_in = sem("w_in6", 2), sem("x_in6", 2)
        x_tr, x_ok, h_mm, h_ok, y_mm, y_ok, y_st, y_fr = (sem("x_tr6"), sem("xT_made"), sem("h_mm6"), sem("hT_made"), sem("y_mm"),
                                                          sem("y_made"), sem("y_stored", 2), sem("y_used"))
        w1_v = a.fw1.rearrange("e (c p) f -> e p c f", p=P)
        w2_v = a.fw2.rearrange("e (k p) d -> e p k d", p=P)
        rows_v = s.routed_d.rearrange("(e c) w -> e c w", e=NX)
        y_v = s.y_d.rearrange("(e c) w -> e c w", e=NX)
        FULL = (CT - 1) * P

        with nc.Block() as block:
            @block.sync
            def _(sp):
                sp.dma_start(b1raw[:, :], a.fb1.rearrange("e (k p) -> (e k) p", p=P)).then_inc(b1_in, 16)
                with sp.Fori(0, NX // 2) as i:
                    for j in range(2):
                        e = 2 * i + j
                        one = ds(e, 1)
                        sp.wait_ge(y_fr, (e + 1) * CT - (CT - 1))
                        sp.dma_start(xg[:, j, 0:CT - 1, :], rows_v[one, 0:FULL, :].rearrange("e (t p) w -> p (e t) w", p=P)).then_inc(x_in[j], 16)
                        sp.dma_start(xg[0:CLAST, j, CT - 1, :], rows_v[one, FULL:CAP, :].rearrange("e p w -> p (e w)")).then_inc(x_in[j], 16)
                        sp.dma_start(w1[:, j, :, :], w1_v[one].rearrange("e p c f -> p (e c) f")).then_inc(w_in[j], 16)
                        sp.dma_start(w2[:, j, :, :], w2_v[one].rearrange("e p k d -> p (e k) d")).then_inc(w_in[j], 16)
                        sp.dma_start(b2b[:, j, :], a.fb2[one].rearrange("e d -> (e d)").partition_broadcast(P)).then_inc(w_in[j], 16)

            @block.tensor
            def _(pe):
                pe.wait_ge(b1_in, 16)
                nc.tensor.transpose(s.bank[0][:, 0:NX * FT], b1raw[:, :], s.ident[0:NX * FT, 0:NX * FT]).then_inc(b1_tr, 1)
                pe.wait_ge(b1_ok, 1)
                pe.sem_inc(y_mm, 2)
                with pe.Fori(0, NX // 2) as i:
                    for j in range(2):
                        e = 2 * i + j
                        pe.wait_ge(x_in[j], 32 * i + 32)
                        for t in range(CT):
                            rows = P if t < CT - 1 else CLAST
                            b = t % 2
                            pe.wait_ge(x_ok, e * CT + t + 1)
                            for c in range(2):
                                last = nc.tensor.transpose(s.bank[b][:, c * P:c * P + rows], xg[0:rows, j, t, c * P:(c + 1) * P],
                                                           s.ident[0:rows, 0:rows])
                            last.then_inc(x_tr, 1)
                        pe.wait_ge(x_ok, e * CT + CT + 2)
                        pe.wait_ge(w_in[j], 48 * i + 48)
                        for f in range(FT):
                            for k, (lo, hi) in enumerate(HALVES):
                                q = 2 * f + k
                                pe.wait_ge(h_ok, e * 2 * FT + q + 1)
                                for c in range(2):
                                    last = nc.tensor.matmul(s.bank[2 + q % 4][:, 0:hi - lo], w1[:, j, c, f * P:(f + 1) * P],
                                                            xT[:, c, lo:hi], start=c == 0, stop=c == 1)
                                last.then_inc(h_mm, 1)
                        pe.wait_ge(h_ok, (e + 1) * 2 * FT + 4)
                        for t in range(CT):
                            rows = P if t < CT - 1 else CLAST
                            pe.wait_ge(y_fr, e * CT + t + 1)
                            for f in range(FT):
                                last = nc.tensor.matmul(s.bank[6 + t % 2][0:rows, 0:H], hT[:, f, t * P:t * P + rows],
                                                        w2[:, j, f, :], start=f == 0, stop=f == FT - 1)
                            last.then_inc(y_mm, 1)

            @block.scalar
            def _(act):
                act.sem_inc(h_ok, 4)
                act.sem_inc(x_ok, 2)
                act.wait_ge(b1_tr, 1)
                nc.scalar.copy(b1T[:, :], s.bank[0][:, 0:NX * FT]).then_inc(b1_ok, 1)
                act.wait_ge(b1_ok, 1)
                with act.Fori(0, NX // 2) as i:
                    for j in range(2):
                        e = 2 * i + j
                        for t in range(CT):
                            rows = P if t < CT - 1 else CLAST
                            act.wait_ge(x_tr, e * CT + t + 1)
                            nc.scalar.copy(xT[:, :, t * P:t * P + rows],
                                           s.bank[t % 2][:, 0:H].rearrange("p (c n) -> p c n", c=2)[:, :, 0:rows]).then_inc(x_ok, 1)
                        nc.scalar.copy(b1e[:, j, :], b1T[:, ds(e * FT, FT)]).then_inc(b1_ok, 1)
                        act.wait_ge(b1_ok, e + 2)
                        act.wait_ge(y_mm, e * CT + 2)
                        for f in range(FT):
                            for k, (lo, hi) in enumerate(HALVES):
                                q = 2 * f + k
                                act.wait_ge(h_mm, e * 2 * FT + q + 1)
                                nc.scalar.activation(hT[:, f, lo:hi], s.bank[2 + q % 4][:, 0:hi - lo], ACT.Relu,
                                                     bias=b1e[:, j, f:f + 1]).then_inc(h_ok, 1)

            @block.vector
            def _(v):
                ch = Chain(v, s.v_step, s.v_steps)
                v.sem_inc(y_fr, 2)
                ch.then(v.memset(fix[:, 0:1], 1e4))
                ch.then(v.memset(fix[:, 1:2], -1e4))
                base = ch.n
                with v.Fori(0, NX // 2) as i:
                    for j in range(2):
                        e = 2 * i + j
                        v.wait_ge(w_in[j], 48 * i + 48)
                        v.wait_ge(x_in[j], 32 * i + 32)
                        for t in range(CT):
                            rows = P if t < CT - 1 else CLAST
                            b = t % 2
                            ch.n = base + (e * CT + t) * 5
                            v.wait_ge(y_mm, e * CT + t + 3)
                            v.wait_ge(y_st[b], 16 * (e * (CT // 2) + t // 2) + 16)
                            yt = y[0:rows, b, :]
                            ch.then(v.tensor_tensor(yt, s.bank[6 + b][0:rows, 0:H], b2b[0:rows, j, :], ALU.add))
                            ch.then(v.tensor_scalar(yt, yt, xg[0:rows, j, t, H:XW], None, ALU.mult))
                            v.tensor_tensor(mask[0:rows, 0, :], yt, yt, ALU.not_equal)
                            v.tensor_scalar(mask[0:rows, 1, :], yt, FMAX, None, ALU.is_gt)
                            ch.then(v.tensor_scalar(mask[0:rows, 2, :], yt, -FMAX, None, ALU.is_lt))
                            apart(s, v)
                            ch.then(v.copy_predicated(yt, mask[0:rows, 0, :], s.zerob[0:rows, 0:1].to_broadcast([rows, H])))
                            apart(s, v)
                            ch.then(v.copy_predicated(yt, mask[0:rows, 1, :], fix[0:rows, 0:1].to_broadcast([rows, H])))
                            apart(s, v)
                            v.copy_predicated(yt, mask[0:rows, 2, :], fix[0:rows, 1:2].to_broadcast([rows, H])).then_inc(y_fr, 1)

            @block.gpsimd
            def _(g):
                for j in range(2):
                    credit(s, g, y_st[j], 16)
                with g.Fori(0, NX // 2) as i:
                    for j in range(2):
                        e = 2 * i + j
                        for t in range(CT):
                            rows = P if t < CT - 1 else CLAST
                            g.wait_ge(y_fr, e * CT + t + 3)
                            g.dma_start(y_v[ds(e, 1), t * P:t * P + rows, :].rearrange("e p w -> p (e w)"),
                                        y[0:rows, t % 2, :]).then_inc(y_st[t % 2], 16)
                for j in range(2):
                    g.wait_ge(y_st[j], 16 * NX * CT // 2 + 16)


def combine(nc, s, a):
    with ExitStack() as ctx:
        def sb(name, shape, dt=F32):
            return ctx.enter_context(nc.sbuf_tensor(name, shape, dt))

        sem = s.sem

        RC = 2
        yg = sb("yg", [P, RC, H])
        gi = sb("gi", [P, RC], I32)
        ot = sb("ot7", [P, RC, H])
        gi_ok = sem("place_copied")
        o_ok = sem("o_made")
        y_in, o_st = sem("y_in", RC), sem("o_stored", RC)
        full = REAL - 1
        assert full % RC == 0
        out_v = a.out[0:full * P, :].rearrange("(t p) f -> t p f", p=P)

        with nc.Block() as block:
            @block.gpsimd
            def _(g):
                def gather(q, n):
                    g.wait_ge(gi_ok, n + 1)
                    apart(s, g)
                    g.indirect_dma_start(out=yg[:, q, :], out_offset=None, in_=s.y_d,
                                         in_offset=OFF(ap=gi[:, q:q + 1], axis=0)).then_inc(y_in[q], 16)

                with g.Fori(0, full // RC) as i:
                    for q in range(RC):
                        gather(q, RC * i + q)
                gather(0, full)

            @block.vector
            def _(v):
                v.sem_inc(o_ok, RC)

                def place(q, t):
                    v.tensor_copy(gi[:, q:q + 1], s.place[:, ds(t, 1)]).then_inc(gi_ok, 1)

                def add(q, t, turns):
                    v.wait_ge(y_in[q], 16 * turns + 16)
                    v.wait_ge(o_st[q], 16 * turns + 16)
                    v.scalar_tensor_tensor(out=ot[:, q, :], in0=yg[:, q, :], scalar=s.kept[:, ds(t, 1)],
                                           in1=s.x1_all[:, ds(t * H, H)], op0=ALU.mult, op1=ALU.add).then_inc(o_ok, 1)
                    v.wait_ge(o_ok, t + RC + 1)

                for q in range(RC):
                    place(q, q)
                with v.Fori(0, full // RC - 1) as i:
                    for q in range(RC):
                        add(q, RC * i + q, i)
                        place(q, RC * i + q + RC)
                for q in range(RC):
                    add(q, full - RC + q, full // RC - 1)
                    if q == 0:
                        place(0, full)
                add(0, full, full // RC)

            @block.sync
            def _(sp):
                for q in range(RC):
                    credit(s, sp, o_st[q], 16)
                with sp.Fori(0, full // RC) as i:
                    for q in range(RC):
                        sp.wait_ge(o_ok, RC * i + q + RC + 1)
                        sp.dma_start(out_v[ds(RC * i + q, 1)].rearrange("t p f -> p (t f)"), ot[:, q, :]).then_inc(o_st[q], 16)
                sp.wait_ge(o_ok, full + RC + 1)
                sp.dma_start(a.out[full * P:N, :], ot[0:TAIL, 0, :]).then_inc(o_st[0], 16)
                sp.wait_ge(o_st[0], 16 * (full // RC + 2))
                sp.wait_ge(o_st[1], 16 * (full // RC + 1))


def build(nc, a):
    with ExitStack() as ctx:
        def sb(name, shape, dt=F32):
            return ctx.enter_context(nc.sbuf_tensor(name, shape, dt))

        def dram(name, shape):
            return nc.dram_tensor(name, shape, F32).ap()

        def sem(name, n=None):
            if n is None:
                return ctx.enter_context(nc.semaphore(name))
            return [ctx.enter_context(nc.semaphore(f"{name}{k}")) for k in range(n)]

        s = Shared()
        s.sem = sem
        s.carried = sem("waits_carried")
        s.v_step, s.v_steps = sem("v_step"), 0
        s.bank = [ctx.enter_context(nc.psum_tensor(f"bank{k}", [P, 512], F32)) for k in range(8)]
        s.x_pad = dram("x_pad", [NTX, P, H])
        s.xn_d = dram("xn_d", [NT, P, H])
        s.q_tab = dram("q_tab", [NT * P, H])
        s.q_tiles = s.q_tab.rearrange("(t p) f -> t p f", p=P)
        s.v_d = dram("v_d", [NT, P, H])
        s.qs_d = dram("qs_d", [NT, P, H])
        s.gh_d = dram("gh_d", [NT, P, H3])
        s.xm_d = dram("xm_d", [NT, P, H])
        s.sorted_d = dram("sorted_d", [SLOTS, EW])
        s.routed_d = dram("routed_d", [NX * CAP, XW])
        s.y_d = dram("y_d", [NX * CAP, H])
        s.credit_d, s.credits = dram("credit_d", [32, 2]), 0
        s.big_s = sb("big_s", [P, NT * SW])
        s.big_p = sb("big_p", [P, NT * H3], BF16)
        s.x1_all = s.big_p[:, 0:2 * NT * H].bitcast(F32)
        s.ident = sb("ident", [P, P])
        s.iota_f = sb("iota_f", [P, P])
        s.node_f = sb("node_f", [P, NT])
        s.ones = sb("ones", [P, P])
        s.upper = sb("upper", [P, P])
        s.zerob = sb("zerob", [P, 2])
        s.w1c = sb("w1c", [P, H])
        s.wg = sb("wg", [P, 2, H3])
        s.bg = sb("bg", [2, H3])
        s.gatew = sb("gatew", [P, 2, NX])
        s.gateb = sb("gateb", [P, NX])
        s.blk_i = sb("blk_i", [1, NG], I32)
        s.st2 = sb("st2_all", [P, NT, 6])
        s.kept = sb("kept", [P, NT])
        s.place = sb("place", [P, NT], I32)
        with ExitStack() as early:
            def eb(name, shape, dt=F32):
                return early.enter_context(nc.sbuf_tensor(name, shape, dt))

            s.fused_w = eb("fused_w", [P, 2, 4 * H])
            s.whhT = eb("whhT", [P, 2, H3])
            s.wk = eb("wk", [P, 2, H])
            s.wout = eb("wout", [P, 2, H])
            s.b1b = eb("b1b", [P, H])
            s.bhhb = eb("bhhb", [P, H3])
            s.gammab = eb("gammab", [P, H])
            s.dst_i = eb("dst_i", [P, EC + 1], I32)
            s.pos = eb("pos", [P, EC + 1])
            s.rowl = eb("rowl", [P, EC + 1])
            s.mean = eb("mean", [P, NT])
            s.rstd = eb("rstd", [P, NT])
            prepare(nc, s, a)
            nodes(nc, s, a)
        edges(nc, s, a)
        gru(nc, s, a)
        routing(nc, s, a)
        experts(nc, s, a)
        combine(nc, s, a)


_NAMES = {"x": "x", "src": "src", "dst": "dst", "edge_attr_64": "edge_attr", "L0_gnn_W1": "W1", "L0_gnn_b1": "b1",
          "L0_gnn_W2": "W2", "L0_gnn_b2": "b2", "L0_gnn_W_ih": "W_ih", "L0_gnn_b_ih": "b_ih",
          "L0_gnn_W_hh": "W_hh", "L0_gnn_b_hh": "b_hh", "L0_mix_Wqkv": "Wqkv", "L0_mix_Wout": "Wout",
          "L0_mix_gamma": "gamma", "L0_ffn_gate_w": "gate_w", "L0_ffn_gate_b": "gate_b", "L0_ffn_w1": "fw1",
          "L0_ffn_b1": "fb1", "L0_ffn_w2": "fw2", "L0_ffn_b2": "fb2"}


def kernel(**inputs):
    import numpy as _np
    import concourse.bacc as _bacc
    from concourse import mybir as _mybir
    from concourse.bass_utils import run_bass_kernel_spmd as _run

    nc = _bacc.Bacc("TRN2", target_bir_lowering=False, num_devices=1)
    arrays, args = {}, {}
    for name, short in _NAMES.items():
        arr = _np.ascontiguousarray(inputs[name])
        arrays[f"in_{name}"] = arr
        args[short] = nc.dram_tensor(f"in_{name}", arr.shape, _mybir.dt.from_np(arr.dtype), kind="ExternalInput").ap()
    args["out"] = nc.dram_tensor("out_dram", (N, H), F32, kind="ExternalOutput").ap()
    build(nc, Arrays(**args))
    r = _run(nc, [arrays], core_ids=[0])
    return r.results[0]["out_dram"]
```

```python
from contextlib import ExitStack

import concourse.bass as bass
import concourse.mybir as mybir
from concourse.alu_op_type import AluOpType as ALU

F32, F32R, BF16, I32, U16 = (mybir.dt.float32, mybir.dt.float32r, mybir.dt.bfloat16, mybir.dt.int32,
                              mybir.dt.uint16)
ACT = mybir.ActivationFunctionType
AX = mybir.AxisListType
OFF = bass.IndirectOffsetOnAxis
ds = bass.ds

P = 128
N, H, E, ED = 6250, 256, 106250, 64
H3 = 3 * H
HEADS, DH = 8, 32
NX, FF = 8, 1024
EPS = 1e-5
REAL = -(-N // P)
NT = REAL + REAL % 2
NTX = NT + 2
TAIL = N - (REAL - 1) * P
NB = REAL
EC = E // P
EREM = E - EC * P
UNROLL = 8
STEP = 10
NS = EC // STEP
PAIR = 2 * P
RING = 8
SPREAD = 3
MID = NT // 2 // SPREAD
LATE = NS // 2 - 1 - NT // 2 - MID
NG = -(-((E + NB * (PAIR - 1)) // PAIR) // RING) * RING
SLOTS = NG * PAIR
PR = 8
EW = ED + 2
SW = H + 1
CAP = -(-(5 * N) // (4 * NX))
CT = -(-CAP // P)
CLAST = CAP - (CT - 1) * P
XW = H + 1
ZERO_DMAS = NX * CAP // (8 * P) + (NX * CAP % (8 * P) >= P) + (NX * CAP % P > 0)
FMAX = 3.4028235e38
assert NS * STEP == EC and SLOTS % (P * PR) == 0
assert NS % 2 == 1 and 0 < LATE * SPREAD < NT // 2


class Shared:
    pass


class Arrays:

    def __init__(self, x, src, dst, edge_attr, W1, b1, W2, b2, W_ih, b_ih, W_hh, b_hh, Wqkv, Wout, gamma,
                 gate_w, gate_b, fw1, fb1, fw2, fb2, out):
        self.x, self.src, self.dst, self.edge_attr = x, src, dst, edge_attr
        self.W1, self.b1, self.W2, self.b2 = W1, b1, W2, b2
        self.W_ih, self.b_ih, self.W_hh, self.b_hh = W_ih, b_ih, W_hh, b_hh
        self.Wqkv, self.Wout, self.gamma = Wqkv, Wout, gamma
        self.gate_w, self.gate_b, self.fw1, self.fb1, self.fw2, self.fb2 = gate_w, gate_b, fw1, fb1, fw2, fb2
        self.out = out


class Chain:

    def __init__(self, eng, sem, n=0):
        self.eng, self.sem, self.n = eng, sem, n

    def then(self, ins):
        ins.then_inc(self.sem, 1)
        self.n = self.n + 1
        self.eng.wait_ge(self.sem, self.n)

    def mark(self, ins):
        ins.then_inc(self.sem, 1)
        self.n = self.n + 1

    def all_but(self, last):
        self.eng.wait_ge(self.sem, self.n - last)


def apart(s, eng):
    eng.sem_inc(s.carried, 1)


def credit(s, eng, sem, n):
    k = s.credits
    s.credits += 1
    eng.dma_start(s.credit_d[k:k + 1, :], s.zerob[0:1, :]).then_inc(sem, n)


def batch_norm_factors(v, ch, st, mean, var, tmp):
    me, qe, mo, qo = st[:, :, 1], st[:, :, 2], st[:, :, 4], st[:, :, 5]
    ch.then(v.tensor_tensor(mean, me, mo, ALU.add))
    ch.then(v.tensor_tensor(tmp, me, mo, ALU.subtract))
    ch.then(v.tensor_scalar(mean, mean, 0.5, None, ALU.mult))
    ch.then(v.tensor_tensor(tmp, tmp, tmp, ALU.mult))
    ch.then(v.tensor_tensor(var, qe, qo, ALU.add))
    ch.then(v.tensor_scalar(tmp, tmp, 0.25, EPS, ALU.mult, ALU.add))
    ch.then(v.tensor_scalar(var, var, 1.0 / H, None, ALU.mult))
    ch.then(v.tensor_tensor(var, var, tmp, ALU.add))


def prepare(nc, s, a):
    with ExitStack() as ctx:
        def sb(name, shape, dt=F32):
            return ctx.enter_context(nc.sbuf_tensor(name, shape, dt))

        sem = s.sem
        raw1 = s.big_s[:, 0:1152].rearrange("p (c f) -> p c f", c=2)
        raw_hh = s.big_s[:, 1152:2688].rearrange("p (c f) -> p c f", c=6)
        raw_ih = s.big_s[:, 2688:4224].rearrange("p (c f) -> p c f", c=6)
        raw2 = s.big_s[:, 4224:4736].rearrange("p (c f) -> p c f", c=2)
        raw1c = s.big_s[:, 4736:4992].rearrange("p (c f) -> p c f", c=2)
        prefill = s.big_s[:, 4992:4992 + PR * EW].rearrange("p (r w) -> p r w", w=EW)
        zrow = s.big_s[:, 5600:5856]
        wihT = sb("wihT", [P, 2, H3])
        b2col = sb("b2col", [P, 2])
        src_i = sb("src_i", [P, EC + 1], I32)
        tmp_i = sb("tmp_i", [P, EC + 1], I32)
        bkt = sb("bkt", [P, EC + 1], BF16)
        eqm = sb("eqm", [P, 2, EC + 1], BF16)
        ranks = sb("ranks", [P, 2, EC + 1])
        onesb = sb("onesb", [P, EC + 1], BF16)
        cnt = sb("cnt", [P, NB])
        pairs_i = sb("pairs_i", [P, NB], I32)
        pairs = sb("pairs", [P, NB])
        incl = sb("incl", [P, NB])
        carry = sb("carry", [P, NB])
        inclT = sb("inclT", [NB, 1])
        iota_g = sb("iota_g", [P, NG])

        p_step = sem("p_step")
        masks, edges_in, filler = sem("masks_made"), sem("edges_in"), sem("filler_made")
        w_in, pad_out = sem("weights_in"), sem("padding_out")
        tr, ev = sem("weights_transposed"), sem("weights_evacuated")
        fold, folded = sem("fold_products"), sem("fold_evacuated")
        counted, sums, incl_ok, inclT_mm = sem("counted"), sem("sums"), sem("incl_made"), sem("inclT_mm")
        inclT_ok, ind_ok, blk_mm = sem("inclT_made"), sem("ind_made"), sem("blk_mm")

        jobs = []
        for c in range(2):
            k = slice(c * P, (c + 1) * P)
            jobs.append((s.fused_w[:, c, 0:H], [raw1[:, m, k] for m in range(2)]))
            jobs.append((s.fused_w[:, c, 2 * H:3 * H], [raw1[:, m, H + c * P:H + (c + 1) * P] for m in range(2)]))
            for raw, wt in ((raw_hh, s.whhT), (raw_ih, wihT)):
                jobs.append((wt[:, c, 0:512], [raw[:, m, k] for m in range(4)]))
                jobs.append((wt[:, c, 512:H3], [raw[:, m, k] for m in range(4, 6)]))
        jobs.append((s.w1c[:, :], [raw1c[:, m, :] for m in range(2)]))
        folds = [(s.wg[:, jc, lo:hi], [(raw2[:, oc, jc * P:(jc + 1) * P], wihT[:, oc, lo:hi]) for oc in range(2)])
                 for jc in range(2) for lo, hi in ((0, 512), (512, H3))]
        folds += [(s.bg[0:1, lo:hi], [(b2col[:, oc:oc + 1], wihT[:, oc, lo:hi]) for oc in range(2)])
                  for lo, hi in ((0, 512), (512, H3))]

        with nc.Block() as block:
            @block.gpsimd
            def _(g):
                ch = Chain(g, p_step)
                g.memset(src_i[:, EC:EC + 1], NB * P)
                g.memset(s.dst_i[:, EC:EC + 1], 0).then_inc(masks, 1)
                g.memset(s.zerob[:, :], 0.0)
                ch.then(g.memset(prefill, 0.0))
                ch.then(g.memset(prefill[:, :, EW - 1:EW], -1.0))
                g.memset(zrow, 0.0).then_inc(filler, 1)
                ch.then(g.memset(s.ident[:, :], 0.0))
                ch.then(g.affine_select(out=s.ident[:, :], in_=s.ident[:, :], compare_op=ALU.not_equal, fill=1.0,
                                        base=0, pattern=[[-1, P]], channel_multiplier=1))
                ch.then(g.memset(s.ones[:, :], 1.0))
                g.affine_select(out=s.upper[:, :], in_=s.ones[:, :], compare_op=ALU.is_gt, fill=0.0,
                                base=0, pattern=[[1, P]], channel_multiplier=-1)
                g.memset(onesb[:, :], 1.0)
                g.iota(s.iota_f[:, :], pattern=[[1, P]], base=0, channel_multiplier=0,
                       allow_small_or_imprecise_dtypes=True)
                g.iota(s.node_f[:, :], pattern=[[P, NT]], base=0, channel_multiplier=1,
                       allow_small_or_imprecise_dtypes=True)
                g.iota(iota_g[:, :], pattern=[[1, NG]], base=0, channel_multiplier=0,
                       allow_small_or_imprecise_dtypes=True).then_inc(masks, 1)

            @block.sync
            def _(sp):
                sp.dma_start(src_i[:, 0:EC], a.src[0:EC * P].rearrange("(p c) -> p c", p=P)).then_inc(edges_in, 16)
                sp.dma_start(s.dst_i[:, 0:EC], a.dst[0:EC * P].rearrange("(p c) -> p c", p=P)).then_inc(edges_in, 16)
                sp.wait_ge(masks, 1)
                for to, of in ((src_i, a.src), (s.dst_i, a.dst)):
                    sp.dma_start(to[0:EREM, EC:EC + 1],
                                 of[EC * P:E].rearrange("(p c) -> p c", c=1)).then_inc(edges_in, 16)
                sp.dma_start(raw1, a.W1.rearrange("(c p) f -> p c f", p=P)).then_inc(w_in, 16)
                for k in range(2):
                    sp.dma_start(raw1c[:, :, k * ED:(k + 1) * ED],
                                 a.W1[:, 2 * H:2 * H + ED].rearrange("(c p) f -> p c f", p=P)).then_inc(w_in, 16)
                sp.dma_start(raw_hh, a.W_hh.rearrange("(c p) f -> p c f", p=P)).then_inc(w_in, 16)
                sp.dma_start(raw_ih, a.W_ih.rearrange("(c p) f -> p c f", p=P)).then_inc(w_in, 16)
                sp.dma_start(raw2, a.W2.rearrange("(c p) f -> p c f", p=P)).then_inc(w_in, 16)
                sp.dma_start(b2col[:, :], a.b2.rearrange("(c p) -> p c", p=P), allow_slow_non_contiguous=True).then_inc(w_in, 16)
                sp.dma_start(s.bg[1:2, :], a.b_ih.rearrange("(a f) -> a f", a=1)).then_inc(w_in, 16)
                qkv = a.Wqkv.rearrange("(c p) f -> p c f", p=P)
                sp.dma_start(s.fused_w[:, :, H:2 * H], qkv[:, :, 0:H]).then_inc(w_in, 16)
                sp.dma_start(s.wk[:, :, :], qkv[:, :, H:2 * H]).then_inc(w_in, 16)
                sp.dma_start(s.fused_w[:, :, 3 * H:4 * H], qkv[:, :, 2 * H:3 * H]).then_inc(w_in, 16)
                sp.dma_start(s.wout[:, :, :], a.Wout.rearrange("(c p) f -> p c f", p=P)).then_inc(w_in, 16)
                for to, of in ((s.b1b, a.b1), (s.bhhb, a.b_hh), (s.gammab, a.gamma), (s.gateb, a.gate_b)):
                    sp.dma_start(to[:, :], of.partition_broadcast(P)).then_inc(w_in, 16)
                sp.dma_start(s.gatew[:, :, :], a.gate_w.rearrange("(c p) e -> p c e", p=P)).then_inc(w_in, 16)
                x_rows = s.x_pad.rearrange("t p f -> (t p) f")
                sp.dma_start(x_rows[0:N, :], a.x).then_inc(pad_out, 16)
                sp.wait_ge(filler, 1)
                sp.dma_start(x_rows[N:REAL * P, :], zrow[0:REAL * P - N, :]).then_inc(pad_out, 16)
                for t in range(REAL, NTX):
                    sp.dma_start(s.x_pad[t], zrow).then_inc(pad_out, 16)
                sorted_v = s.sorted_d.rearrange("(k p r) w -> k p r w", p=P, r=PR)
                fills = SLOTS // (P * PR)
                with sp.Fori(0, fills) as k:
                    sp.dma_start(sorted_v[ds(k, 1)].rearrange("k p r w -> p (k r) w"), prefill).then_inc(pad_out, 16)
                sp.wait_ge(pad_out, 16 * (2 + NTX - REAL + fills))
                sp.dma_start(s.x1_all.rearrange("p (t f) -> p t f", f=H),
                             s.x_pad[0:NT].rearrange("t p f -> p t f")).then_inc(s.x_in, 16)

            @block.tensor
            def _(pe):
                pe.wait_ge(w_in, 16 * 17)
                pe.wait_ge(masks, 2)
                for q, (to, ins) in enumerate(jobs):
                    if q >= 4:
                        pe.wait_ge(ev, q - 3)
                    for m, i in enumerate(ins):
                        last = nc.tensor.transpose(s.bank[q % 4][:, m * P:(m + 1) * P], i, s.ident[:, :])
                    last.then_inc(tr, 1)
                pe.wait_ge(ev, len(jobs))
                for q, (to, terms) in enumerate(folds):
                    if q >= 4:
                        pe.wait_ge(folded, q - 3)
                    rows, cols = to.shape
                    for n, (left, right) in enumerate(terms):
                        last = nc.tensor.matmul(s.bank[q % 4][0:rows, 0:cols], left, right,
                                                start=n == 0, stop=n == len(terms) - 1)
                    last.then_inc(fold, 1)
                pe.wait_ge(counted, 1)
                nc.tensor.matmul(s.bank[4][:, 0:NB], s.ones[:, :], cnt[:, :], start=True, stop=True)
                nc.tensor.matmul(s.bank[5][:, 0:NB], s.upper[:, :], cnt[:, :], start=True,
                                 stop=True).then_inc(sums, 1)
                pe.wait_ge(incl_ok, 1)
                nc.tensor.matmul(s.bank[4][0:NB, 0:1], incl[0:1, :], s.ones[0:1, 0:1], start=True,
                                 stop=True).then_inc(inclT_mm, 1)
                pe.wait_ge(ind_ok, 1)
                nc.tensor.matmul(s.bank[4][0:1, 0:NG], s.ones[0:NB, 0:1], iota_g[0:NB, :], start=True,
                                 stop=True).then_inc(blk_mm, 1)

            @block.scalar
            def _(act):
                for q, (to, ins) in enumerate(jobs):
                    act.wait_ge(tr, q + 1)
                    nc.scalar.copy(to, s.bank[q % 4][:, 0:P * len(ins)]).then_inc(ev, 1)
                for q, (to, terms) in enumerate(folds):
                    act.wait_ge(fold, q + 1)
                    rows, cols = to.shape
                    nc.scalar.copy(to, s.bank[q % 4][0:rows, 0:cols]).then_inc(folded, 1)

            @block.vector
            def _(v):
                ch = Chain(v, s.v_step, s.v_steps)
                v.wait_ge(edges_in, 64)
                v.wait_ge(masks, 2)
                ch.then(v.tensor_scalar(tmp_i[:, :], src_i[:, :], 7, None, ALU.arith_shift_right))
                ch.then(v.tensor_copy(bkt[:, :], tmp_i[:, :]))
                ch.then(v.tensor_scalar(tmp_i[:, :], src_i[:, :], P - 1, None, ALU.bitwise_and))
                ch.then(v.tensor_copy(s.rowl[:, :], tmp_i[:, :]))

                def count(b, k):
                    ch.all_but(1)
                    ch.mark(v.tensor_scalar(eqm[:, k, :], bkt[:, :], s.iota_f[:, ds(b, 1)], 0.0, ALU.is_equal, ALU.add,
                                            accum_out=cnt[:, ds(b, 1)]))

                base = ch.n
                with v.Fori(0, NB // UNROLL) as i:
                    for k in range(UNROLL):
                        ch.n = base + i * UNROLL + k
                        count(i * UNROLL + k, k % 2)
                ch.n = base + NB // UNROLL * UNROLL
                for b in range(NB // UNROLL * UNROLL, NB):
                    count(b, b % 2)
                ch.all_but(0)
                v.tensor_copy(pairs[:, :], cnt[:, :]).then_inc(counted, 1)
                v.wait_ge(sums, 1)
                ch.then(v.tensor_scalar(pairs_i[:, :], s.bank[4][:, 0:NB], float(PAIR - 1), None, ALU.add))
                ch.then(v.tensor_scalar(pairs_i[:, :], pairs_i[:, :], PAIR.bit_length() - 1, None, ALU.arith_shift_right))
                ch.then(v.tensor_copy(pairs[:, :], pairs_i[:, :]))
                ch.then(v.tensor_tensor_scan(incl[:, :], s.ones[:, 0:NB], pairs[:, :], 0.0, ALU.mult, ALU.add))
                v.tensor_tensor(carry[:, :], incl[:, :], pairs[:, :], ALU.subtract).then_inc(incl_ok, 1)
                v.wait_ge(incl_ok, 1)
                ch.then(v.tensor_scalar(carry[:, :], carry[:, :], float(PAIR), -1.0, ALU.mult, ALU.add))
                ch.then(v.tensor_tensor(carry[:, :], carry[:, :], s.bank[5][:, 0:NB], ALU.add))
                v.wait_ge(inclT_mm, 1)
                ch.then(v.tensor_copy(inclT[:, :], s.bank[4][0:NB, 0:1]))
                v.tensor_scalar(iota_g[0:NB, :], iota_g[0:NB, :], inclT[:, 0:1], None, ALU.is_ge).then_inc(ind_ok, 1)
                v.wait_ge(blk_mm, 1)
                ch.then(v.tensor_scalar(s.blk_i[0:1, :], s.bank[4][0:1, 0:NG], float(NB - 1), None, ALU.min))

                def mask(b, k):
                    ch.mark(v.tensor_scalar(eqm[:, k, :], bkt[:, :], s.iota_f[:, ds(b, 1)], None, ALU.is_equal))

                def place(b, k):
                    ch.all_but(1)
                    ch.mark(v.tensor_tensor_scan(ranks[:, k, :], onesb[:, :], eqm[:, k, :], carry[:, ds(b, 1)],
                                                 ALU.mult, ALU.add))
                    ch.all_but(1)
                    mask(b + 1, 1 - k)
                    ch.all_but(1)
                    apart(s, v)
                    ch.mark(v.copy_predicated(s.pos[:, :], eqm[:, k, :].bitcast(U16), ranks[:, k, :]))

                ch.mark(v.memset(s.pos[:, :], 0.0))
                mask(0, 0)
                ch.all_but(0)
                base = ch.n
                with v.Fori(0, NB // UNROLL) as i:
                    for k in range(UNROLL):
                        ch.n = base + (i * UNROLL + k) * 3
                        place(i * UNROLL + k, k % 2)
                ch.n = base + NB // UNROLL * UNROLL * 3
                for b in range(NB // UNROLL * UNROLL, NB):
                    place(b, b % 2)
                ch.all_but(0)
                s.v_steps = ch.n


def nodes(nc, s, a):
    with ExitStack() as ctx:
        def sb(name, shape, dt=F32):
            return ctx.enter_context(nc.sbuf_tensor(name, shape, dt))

        sem = s.sem

        ea = sb("ea", [P, 2, STEP, EW])
        slot_i = sb("slot_i", [P, 2, STEP], I32)
        rem = sb("rem", [16, EW])
        rem_i = sb("rem_i", [16, 1], I32)
        xt = sb("xt", [P, 2, H])
        xn = sb("xn", [P, 2, H])
        xnT = sb("xnT", [P, 2, 2, P])
        qt = sb("qt", [P, 2, H])
        vt = sb("vt", [P, 2, H])
        gh = sb("gh", [P, 2, H3])
        pf = sb("pf", [P, H])
        rest = sb("rest", [P, H])
        qe = sb("qe", [P, H])
        qs = sb("qs", [P, 2, H])
        qred = sb("qred", [P, 2, HEADS])
        kmax = sb("kmax", [P, 2])
        et, etok = (x[:, :, :].rearrange("p j (c n) -> p j c n", c=2) for x in (qt, vt))
        v1 = sb("v1", [P, 2, 2, P + 1])
        zero = sb("zero", [P, P + 1])
        blockmask = sb("blockmask", [P, P])
        den = sb("den", [P, 2])
        cx = sb("cx", [P, 2, P])
        cxT = sb("cxT", [P, 2, P])
        mix = sb("mix", [P, 2, H])
        qsT, ot, qsl = xnT, qs, qt
        st = sb("st2", [P, 2, 6])
        mvt = sb("mvt", [P, 2, 2])
        rs = sb("rs", [P, 2])
        kT = s.big_s[:, 0:2 * NT * P].rearrange("p (c n) -> p c n", c=2)

        p_step, varred, rooted = sem("p2_step"), sem("var_made"), sem("roots_made")
        ea_in, meta, scattered = sem("ea_in", 2), sem("meta_made"), sem("scattered", 2)
        rem_in, rem_meta, rem_out = sem("rem_in"), sem("rem_meta"), sem("rem_out")
        xt_in, xn_st = sem("xt_in", 2), sem("xn_stored", 2)
        xn_ok, x_tr, xnT_ok = sem("xn_made"), sem("xn_transposed"), sem("xnT_made")
        mm_pq, mm_qv, mm_ga, mm_gb, mm_k = (sem("mm_pq"), sem("mm_qv"), sem("mm_ga"), sem("mm_gb"), sem("mm_k"))
        fr_pq, fr_ga, fr_gb = sem("pq_used"), sem("ga_used"), sem("gb_used")
        q_ok, v_ok, k_ok = sem("q_evacuated"), sem("v_evacuated"), sem("k_evacuated")
        qv_st, gh_st, qs_st = sem("qv_stored", 2), sem("gh_stored", 2), sem("qs_stored", 2)
        gh_ok, qsub, qexp, qs_ok = sem("gh_made"), sem("q_shifted"), sem("q_exp"), sem("qs_made")
        const_ok, kmax_ok = sem("const_made"), sem("kmax_made")
        v_in, et_ok, e_tr, etok_ok, ctx_mm = sem("v_in", 2), sem("e_made"), sem("e_transposed"), sem("etok_made"), sem("context_mm")
        cx_ok, cx_tr, cxT_ok, m_mm, m_ok = sem("cx_made"), sem("cx_transposed"), sem("cxT_made"), sem("m_mm"), sem("m_made")
        qs_in, x2_in, qs_tr, qsT_ok, o_mm = sem("qs_in", 2), sem("x2_in", 2), sem("qs_transposed"), sem("qsT_made"), sem("o_mm")
        o_fr, o_var, o_root, ot_ok, ot_st = sem("o_used"), sem("o_var"), sem("o_root"), sem("ot_made"), sem("ot_stored", 2)

        ea_head = a.edge_attr[0:EC * P, :].rearrange("(p c) f -> p c f", p=P)

        def load_edges(sp, h, turn):
            sp.wait_ge(scattered[h], 16 * STEP * (turn + 1))
            sp.dma_start(ea[:, h, :, 0:ED], ea_head[:, ds((2 * turn + h) * STEP, STEP), :]).then_inc(ea_in[h], 16)

        def make_meta(v, h, turn):
            v.wait_ge(scattered[h], 16 * STEP * (turn + 1))
            cols = ds((2 * turn + h) * STEP, STEP)
            v.tensor_copy(ea[:, h, :, ED:ED + 1].bitcast(I32).rearrange("p a b -> p (a b)"), s.dst_i[:, cols])
            v.tensor_copy(ea[:, h, :, ED + 1:EW].rearrange("p a b -> p (a b)"), s.rowl[:, cols])
            v.tensor_copy(slot_i[:, h, :], s.pos[:, cols]).then_inc(meta, 1)

        def scatter(g, h, turn):
            g.wait_ge(ea_in[h], 16 * turn + 16)
            g.wait_ge(meta, 2 * turn + h + 1)
            apart(s, g)
            for j in range(STEP):
                g.indirect_dma_start(out=s.sorted_d, out_offset=OFF(ap=slot_i[:, h, j:j + 1], axis=0),
                                     in_=ea[:, h, j, :], in_offset=None).then_inc(scattered[h], 16)

        with nc.Block() as block:
            @block.gpsimd
            def _(g):
                for h in range(2):
                    credit(s, g, scattered[h], 16 * STEP)
                ch = Chain(g, p_step)
                g.memset(zero[:, :], 0.0)
                g.memset(v1[:, :, :, P:P + 1], 1.0)
                ch.then(g.memset(blockmask[:, :], 1.0))
                view = blockmask[:, :].rearrange("p (h e) -> p h e", e=DH)
                ch.then(g.affine_select(out=view, in_=view, compare_op=ALU.is_ge, fill=0.0, base=0,
                                        pattern=[[-DH, P // DH], [0, DH]], channel_multiplier=1))
                g.affine_select(out=view, in_=view, compare_op=ALU.is_ge, fill=0.0, base=DH - 1,
                                pattern=[[DH, P // DH], [0, DH]], channel_multiplier=-1).then_inc(const_ok, 1)
                with g.Fori(0, NS // 2) as k:
                    for h in range(2):
                        scatter(g, h, k)
                scatter(g, 0, NS // 2)
                g.wait_ge(rem_in, 16)
                g.wait_ge(rem_meta, 1)
                g.indirect_dma_start(out=s.sorted_d, out_offset=OFF(ap=rem_i[0:EREM, :], axis=0),
                                     in_=rem[0:EREM, :], in_offset=None).then_inc(rem_out, 16)
                g.wait_ge(rem_out, 16)
                for h in range(2):
                    g.wait_ge(scattered[h], 16 * STEP * (NS // 2 + 2 - h))

            @block.sync
            def _(sp):
                for j in range(2):
                    sp.dma_start(xt[:, j, :], s.x_pad[j]).then_inc(xt_in[j], 16)
                    credit(s, sp, xn_st[j], 16)
                    credit(s, sp, qv_st[j], 32)
                    credit(s, sp, gh_st[j], 16)
                    credit(s, sp, qs_st[j], 16)
                    credit(s, sp, ot_st[j], 16)
                sp.dma_start(rem[0:EREM, 0:ED], a.edge_attr[EC * P:E, :]).then_inc(rem_in, 16)
                for h in range(2):
                    load_edges(sp, h, 0)
                with sp.Fori(0, NT // 2) as i:
                    for j in range(2):
                        t = 2 * i + j
                        load_edges(sp, j, i + 1)
                        one = ds(t, 1)
                        sp.wait_ge(xn_ok, t + 3)
                        sp.dma_start(s.xn_d[one].rearrange("t p f -> p (t f)"), xn[:, j, :]).then_inc(xn_st[j], 16)
                        sp.dma_start(xt[:, j, :], s.x_pad[ds(t + 2, 1)].rearrange("t p f -> p (t f)")).then_inc(xt_in[j], 16)
                        sp.wait_ge(v_ok, t + 3)
                        sp.dma_start(s.q_tiles[one].rearrange("t p f -> p (t f)"), qt[:, j, :]).then_inc(qv_st[j], 16)
                        sp.dma_start(s.v_d[one].rearrange("t p f -> p (t f)"), vt[:, j, :]).then_inc(qv_st[j], 16)
                        sp.wait_ge(qs_ok, t + 3)
                        sp.dma_start(s.qs_d[one].rearrange("t p f -> p (t f)"), qs[:, j, :]).then_inc(qs_st[j], 16)
                        sp.wait_ge(gh_ok, t + 3)
                        sp.dma_start(s.gh_d[one].rearrange("t p f -> p (t f)"), gh[:, j, :]).then_inc(gh_st[j], 16)
                for j in range(2):
                    sp.wait_ge(qv_st[j], 16 * NT + 32)

                def load_v(i):
                    for j in range(2):
                        t = 2 * i + j
                        sp.wait_ge(ctx_mm, t + 1)
                        sp.dma_start(v1[:, j, :, 0:P],
                                     s.v_d[ds(t, 1)].rearrange("t p (c f) -> p (t c) f", c=2)).then_inc(v_in[j], 16)

                with sp.Fori(0, MID) as k:
                    for m in range(SPREAD):
                        if m < 2:
                            load_edges(sp, m, k + 1 + NT // 2)
                        load_v(SPREAD * k + m)
                for i in range(MID * SPREAD, NT // 2):
                    load_v(i)
                for j in range(2):
                    sp.wait_ge(qs_st[j], 8 * NT + 16)
                    sp.wait_ge(ctx_mm, NT + 2)

                def load_output(i):
                    for j in range(2):
                        one = ds(2 * i + j, 1)
                        sp.wait_ge(qsT_ok, 2 * i + j + 1)
                        sp.dma_start(qsl[:, j, :], s.qs_d[one].rearrange("t p f -> p (t f)")).then_inc(qs_in[j], 16)
                    for j in range(2):
                        one = ds(2 * i + j, 1)
                        sp.wait_ge(ot_ok, 2 * i + j + 1)
                        sp.dma_start(xt[:, j, :], s.x_pad[one].rearrange("t p f -> p (t f)")).then_inc(x2_in[j], 16)

                with sp.Fori(0, LATE) as k:
                    for m in range(SPREAD):
                        if m < 2:
                            load_edges(sp, m, k + 1 + NT // 2 + MID)
                        load_output(SPREAD * k + m)
                load_edges(sp, 0, NS // 2)
                with sp.Fori(LATE * SPREAD, NT // 2) as i:
                    load_output(i)
                for j in range(2):
                    sp.wait_ge(xn_st[j], 8 * NT + 16)
                    sp.wait_ge(gh_st[j], 8 * NT + 16)

            @block.tensor
            def _(pe):
                pe.sem_inc(x_tr, 2)
                pe.sem_inc(mm_k, 2)
                with pe.Fori(0, NT // 2) as i:
                    for j in range(2):
                        t = 2 * i + j
                        pe.wait_ge(xn_ok, t + 3)
                        pe.wait_ge(xnT_ok, t + 1)
                        for c in range(2):
                            last = nc.tensor.transpose(s.bank[j][:, c * P:(c + 1) * P],
                                                       xn[:, j, c * P:(c + 1) * P], s.ident[:, :])
                        last.then_inc(x_tr, 1)
                    for j in range(2):
                        t = 2 * i + j
                        pe.wait_ge(xnT_ok, t + 3)

                        def product(bank, right, free, value, signal):
                            pe.wait_ge(free, value)
                            for c in range(2):
                                last = nc.tensor.matmul(s.bank[bank][:, 0:right.shape[2]], xnT[:, j, c, :],
                                                        right[:, c, :], start=c == 0, stop=c == 1)
                            last.then_inc(signal, 1)

                        product(2, s.fused_w[:, :, 0:512], fr_pq, t + 1, mm_pq)
                        product(3, s.fused_w[:, :, 512:1024], v_ok, t + 2, mm_qv)
                        product(4, s.whhT[:, :, 0:512], fr_ga, t + 1, mm_ga)
                        product(5, s.whhT[:, :, 512:H3], fr_gb, t + 1, mm_gb)
                        pe.wait_ge(k_ok, t + 1)
                        for m in range(2):
                            for c in range(2):
                                last = nc.tensor.matmul(s.bank[6][:, m * P:(m + 1) * P], s.wk[:, c, m * P:(m + 1) * P],
                                                        xnT[:, j, c, :], start=c == 0, stop=c == 1)
                        last.then_inc(mm_k, 1)
                pe.sem_inc(ctx_mm, 2)
                pe.sem_inc(e_tr, 2)
                pe.wait_ge(const_ok, 1)
                pe.wait_ge(fr_pq, NT + 1)
                pe.wait_ge(v_ok, NT + 2)
                for m in range(2):
                    nc.tensor.matmul(s.bank[2 + m][:, 0:P + 1], zero[:, 0:P], zero[:, :], start=True, stop=True)
                with pe.Fori(0, NT // 2) as i:
                    for j in range(2):
                        t = 2 * i + j
                        pe.wait_ge(et_ok, t + 3)
                        pe.wait_ge(etok_ok, t + 1)
                        for m in range(2):
                            last = nc.tensor.transpose(s.bank[j][:, m * P:(m + 1) * P], et[:, j, m, :], s.ident[:, :])
                        last.then_inc(e_tr, 1)
                    for j in range(2):
                        t = 2 * i + j
                        pe.wait_ge(etok_ok, t + 3)
                        pe.wait_ge(v_in[j], 16 * i + 16)
                        for m in range(2):
                            last = nc.tensor.matmul(s.bank[2 + m][:, 0:P + 1], etok[:, j, m, :], v1[:, j, m, :],
                                                    start=False, stop=True, skip_group_check=True)
                        last.then_inc(ctx_mm, 1)
                pe.wait_ge(cx_ok, 1)
                for m in range(2):
                    last = nc.tensor.transpose(s.bank[4][:, m * P:(m + 1) * P], cx[:, m, :], s.ident[:, :])
                last.then_inc(cx_tr, 1)
                pe.wait_ge(cxT_ok, 1)
                for m in range(2):
                    last = nc.tensor.matmul(s.bank[5][:, m * H:(m + 1) * H], cxT[:, m, :], s.wout[:, m, :],
                                            start=True, stop=True)
                last.then_inc(m_mm, 1)
                pe.wait_ge(m_ok, 1)
                pe.sem_inc(qs_tr, 2)
                pe.sem_inc(o_mm, 2)
                with pe.Fori(0, NT // 2) as i:
                    for j in range(2):
                        t = 2 * i + j
                        pe.wait_ge(qs_in[j], 16 * i + 16)
                        pe.wait_ge(qsT_ok, t + 1)
                        for m in range(2):
                            last = nc.tensor.transpose(s.bank[j][:, m * P:(m + 1) * P], qsl[:, j, m * P:(m + 1) * P],
                                                       s.ident[:, :])
                        last.then_inc(qs_tr, 1)
                    for j in range(2):
                        t = 2 * i + j
                        pe.wait_ge(qsT_ok, t + 3)
                        pe.wait_ge(o_fr, t + 1)
                        for m in range(2):
                            last = nc.tensor.matmul(s.bank[6 + j][:, 0:H], qsT[:, j, m, :], mix[:, m, :],
                                                    start=m == 0, stop=m == 1)
                        last.then_inc(o_mm, 1)

            @block.scalar
            def _(act):
                act.wait_ge(varred, 1)
                nc.scalar.activation(s.rstd[:, :], pf[:, 0:NT], ACT.Sqrt).then_inc(rooted, 1)
                act.sem_inc(xnT_ok, 2)
                act.sem_inc(q_ok, 2)
                act.sem_inc(v_ok, 2)
                act.sem_inc(k_ok, 1)
                act.sem_inc(qexp, 1)
                with act.Fori(0, NT // 2) as i:
                    for j in range(2):
                        t = 2 * i + j
                        act.wait_ge(x_tr, t + 3)
                        act.wait_ge(mm_k, t + 1)
                        nc.scalar.copy(xnT[:, j, :, :], s.bank[j][:, 0:H].rearrange("p (c n) -> p c n", c=2)).then_inc(xnT_ok, 1)
                    for j in range(2):
                        t = 2 * i + j
                        act.wait_ge(mm_qv, t + 1)
                        act.wait_ge(qv_st[j], 32 * i + 32)
                        nc.scalar.copy(qt[:, j, :], s.bank[3][:, 0:H]).then_inc(q_ok, 1)
                        act.wait_ge(q_ok, t + 3)
                        nc.scalar.copy(vt[:, j, :], s.bank[3][:, H:2 * H]).then_inc(v_ok, 1)
                        act.wait_ge(qsub, t + 1)
                        nc.scalar.activation(qe[:, :], qe[:, :], ACT.Exp).then_inc(qexp, 1)
                        act.wait_ge(mm_k, t + 3)
                        nc.scalar.copy(kT[:, :, ds(t * P, P)], s.bank[6][:, 0:H].rearrange("p (c n) -> p c n", c=2)).then_inc(k_ok, 1)
                act.sem_inc(et_ok, 2)
                act.sem_inc(etok_ok, 2)
                act.wait_ge(kmax_ok, 1)
                for j in range(2):
                    act.wait_ge(qv_st[j], 16 * NT + 32)
                with act.Fori(0, NT // 2) as i:
                    for j in range(2):
                        t = 2 * i + j
                        act.wait_ge(e_tr, t + 1)
                        for m in range(2):
                            last = nc.scalar.activation(et[:, j, m, :], kT[:, m, ds(t * P, P)], ACT.Exp, bias=kmax[:, m:m + 1])
                        last.then_inc(et_ok, 1)
                    for j in range(2):
                        t = 2 * i + j
                        act.wait_ge(e_tr, t + 3)
                        act.wait_ge(ctx_mm, t + 1)
                        nc.scalar.copy(etok[:, j, :, :], s.bank[j][:, 0:H].rearrange("p (c n) -> p c n", c=2)).then_inc(etok_ok, 1)
                act.wait_ge(cx_tr, 1)
                nc.scalar.copy(cxT[:, :, :], s.bank[4][:, 0:H].rearrange("p (c n) -> p c n", c=2)).then_inc(cxT_ok, 1)
                act.wait_ge(m_mm, 1)
                nc.scalar.copy(mix[:, :, :], s.bank[5][:, :].rearrange("p (c n) -> p c n", c=2)).then_inc(m_ok, 1)
                act.sem_inc(qsT_ok, 2)
                with act.Fori(0, NT // 2) as i:
                    for j in range(2):
                        t = 2 * i + j
                        act.wait_ge(qs_tr, t + 3)
                        act.wait_ge(o_mm, t + 1)
                        nc.scalar.copy(qsT[:, j, :, :], s.bank[j][:, 0:H].rearrange("p (c n) -> p c n", c=2)).then_inc(qsT_ok, 1)
                    act.wait_ge(o_var, i + 1)
                    nc.scalar.activation(rs[:, :], rs[:, :], ACT.Sqrt).then_inc(o_root, 1)
                    for j in range(2):
                        t = 2 * i + j
                        act.wait_ge(ot_ok, t + 3)
                        act.dma_start(s.xm_d[ds(t, 1)].rearrange("t p f -> p (t f)"), ot[:, j, :]).then_inc(ot_st[j], 16)
                for j in range(2):
                    act.wait_ge(ot_st[j], 8 * NT + 16)

            @block.vector
            def _(v):
                ch = Chain(v, s.v_step, s.v_steps)
                v.tensor_copy(rem[0:EREM, ED:ED + 1].bitcast(I32), s.dst_i[0:EREM, EC:EC + 1])
                v.tensor_copy(rem[0:EREM, ED + 1:EW], s.rowl[0:EREM, EC:EC + 1])
                v.tensor_copy(rem_i[0:EREM, :], s.pos[0:EREM, EC:EC + 1]).then_inc(rem_meta, 1)
                for h in range(2):
                    make_meta(v, h, 0)
                v.wait_ge(s.x_in, 16)
                base = ch.n
                with v.Fori(0, NT // 10) as i:
                    for k in range(10):
                        t = 10 * i + k
                        ch.mark(v.bn_stats(s.st2[:, ds(t, 1), :].rearrange("p a b -> p (a b)"), s.x1_all[:, ds(t * H, H)]))
                ch.n = base + NT
                ch.all_but(0)
                var, tmp = pf[:, 0:NT], rest[:, 0:NT]
                batch_norm_factors(v, ch, s.st2, s.mean[:, :], var, tmp)
                v.tensor_copy(tmp, var).then_inc(varred, 1)
                v.wait_ge(rooted, 1)
                ch.then(v.reciprocal(s.rstd[:, :], s.rstd[:, :]))
                v.sem_inc(xn_ok, 2)
                for k in (fr_pq, fr_ga, fr_gb):
                    v.sem_inc(k, 1)
                v.sem_inc(gh_ok, 2)
                v.sem_inc(qs_ok, 2)
                base = ch.n
                with v.Fori(0, NT // 2) as i:
                    for j in range(2):
                        t = 2 * i + j
                        v.wait_ge(xt_in[j], 16 * i + 16)
                        v.wait_ge(x_tr, t + 1)
                        v.wait_ge(xn_st[j], 16 * i + 16)
                        v.tensor_scalar(xn[:, j, :], xt[:, j, :], s.mean[:, ds(t, 1)], s.rstd[:, ds(t, 1)],
                                        ALU.subtract, ALU.mult).then_inc(xn_ok, 1)
                    for j in range(2):
                        t = 2 * i + j
                        ch.n = base + t * 8
                        o = t * H3
                        v.wait_ge(mm_pq, t + 1)
                        ch.then(v.tensor_tensor(pf[:, :], s.bank[2][:, 0:H], s.b1b[:, :], ALU.add))
                        q_ps = s.bank[2][:, H:2 * H].rearrange("p (h e) -> p h e", e=DH)
                        ch.then(v.tensor_reduce(qred[:, 0, :], q_ps, AX.X, ALU.max))
                        v.wait_ge(qs_ok, t + 2)
                        v.tensor_tensor(qe[:, :].rearrange("p (h e) -> p h e", e=DH), q_ps,
                                        qred[:, 0, :].unsqueeze(2).to_broadcast([P, HEADS, DH]), ALU.subtract).then_inc(qsub, 1)
                        v.wait_ge(qsub, t + 1)
                        v.sem_inc(fr_pq, 1)
                        ch.then(v.tensor_copy(s.big_p[:, ds(o, H)], pf[:, :]))
                        ch.then(v.tensor_tensor(rest[:, :], pf[:, :], s.big_p[:, ds(o, H)], ALU.subtract))
                        ch.then(v.tensor_copy(s.big_p[:, ds(o + H, H)], rest[:, :]))
                        v.tensor_tensor(s.big_p[:, ds(o + 2 * H, H)], rest[:, :], s.big_p[:, ds(o + H, H)], ALU.subtract)
                        v.wait_ge(gh_st[j], 16 * i + 16)
                        v.wait_ge(mm_ga, t + 1)
                        v.tensor_tensor(gh[:, j, 0:512], s.bank[4][:, :], s.bhhb[:, 0:512], ALU.add).then_inc(fr_ga, 1)
                        v.wait_ge(mm_gb, t + 1)
                        v.tensor_tensor(gh[:, j, 512:H3], s.bank[5][:, 0:H], s.bhhb[:, 512:H3], ALU.add).then_inc(fr_gb, 1)
                        v.wait_ge(fr_gb, t + 2)
                        v.sem_inc(gh_ok, 1)
                        v.wait_ge(qexp, t + 2)
                        qe_v = qe[:, :].rearrange("p (h e) -> p h e", e=DH)
                        ch.then(v.tensor_reduce(qred[:, 1, :], qe_v, AX.X, ALU.add))
                        ch.then(v.reciprocal(qred[:, 1, :], qred[:, 1, :]))
                        ch.then(v.tensor_scalar(qred[:, 1, :], qred[:, 1, :], DH ** -0.5, None, ALU.mult))
                        v.wait_ge(qs_st[j], 16 * i + 16)
                        v.tensor_tensor(qs[:, j, :].rearrange("p (h e) -> p h e", e=DH), qe_v,
                                        qred[:, 1, :].unsqueeze(2).to_broadcast([P, HEADS, DH]), ALU.mult).then_inc(qs_ok, 1)
                        make_meta(v, j, i + 1)
                ch.n = base + NT * 8
                v.wait_ge(k_ok, NT + 1)
                for m in range(2):
                    ch.then(v.tensor_reduce(kmax[:, m:m + 1], kT[:, m, 0:N], AX.X, ALU.max))
                v.memset(kT[:, :, N:NT * P], -1e30)
                v.tensor_scalar(kmax[:, :], kmax[:, :], -1.0, None, ALU.mult).then_inc(kmax_ok, 1)
                with v.Fori(0, MID) as i:
                    for h in range(2):
                        make_meta(v, h, i + 1 + NT // 2)
                v.wait_ge(ctx_mm, NT + 2)
                v.wait_ge(const_ok, 1)
                for m in range(2):
                    ch.then(v.reciprocal(den[:, m:m + 1], s.bank[2 + m][:, P:P + 1]))
                    ch.then(v.tensor_scalar(cx[:, m, :], s.bank[2 + m][:, 0:P], den[:, m:m + 1], None, ALU.mult))
                    last = v.tensor_tensor(cx[:, m, :], cx[:, m, :], blockmask[:, :], ALU.mult)
                last.then_inc(cx_ok, 1)
                for j in range(2):
                    v.wait_ge(qs_st[j], 8 * NT + 16)
                v.sem_inc(o_fr, 2)
                v.sem_inc(ot_ok, 2)
                base = ch.n

                def output(i):
                    ch.n = base + i * 10
                    for j in range(2):
                        v.wait_ge(o_mm, 2 * i + j + 3)
                        ch.mark(v.bn_stats(st[:, j, :], s.bank[6 + j][:, 0:H]))
                    for j in range(2):
                        ch.all_but(1)
                        apart(s, v)
                        ch.mark(v.bn_aggr(mvt[:, j, :], st[:, j, :]))
                    ch.all_but(0)
                    ch.mark(v.tensor_scalar(rs[:, :], mvt[:, :, 1:2].rearrange("p a b -> p (a b)"), EPS, None, ALU.add))
                    ch.all_but(0)
                    v.sem_inc(o_var, 1)
                    for j in range(2):
                        v.wait_ge(ot_st[j], 16 * i + 16)
                        ch.mark(v.scalar_tensor_tensor(out=ot[:, j, :], in0=s.bank[6 + j][:, 0:H], scalar=mvt[:, j, 0:1],
                                                       in1=s.gammab[:, :], op0=ALU.subtract, op1=ALU.mult))
                    ch.all_but(0)
                    v.sem_inc(o_fr, 2)
                    v.wait_ge(o_root, i + 1)
                    ch.mark(v.reciprocal(rs[:, :], rs[:, :]))
                    ch.all_but(0)
                    for j in range(2):
                        v.wait_ge(x2_in[j], 16 * i + 16)
                        ch.mark(v.scalar_tensor_tensor(out=ot[:, j, :], in0=ot[:, j, :], scalar=rs[:, j:j + 1],
                                                       in1=xt[:, j, :], op0=ALU.mult, op1=ALU.add))
                    ch.all_but(0)
                    v.sem_inc(ot_ok, 2)

                with v.Fori(0, LATE) as k:
                    for m in range(SPREAD):
                        output(SPREAD * k + m)
                        if m < 2:
                            make_meta(v, m, k + 1 + NT // 2 + MID)
                make_meta(v, 0, NS // 2)
                with v.Fori(LATE * SPREAD, NT // 2) as i:
                    output(i)
                ch.n = base + (NT // 2) * 10
                s.v_steps = ch.n


def edges(nc, s, a):
    with ExitStack() as ctx:
        def sb(name, shape, dt=F32):
            return ctx.enter_context(nc.sbuf_tensor(name, shape, dt))

        sem = s.sem

        LOAD = RING // 2
        eb = sb("eb", [P, 2, LOAD, 2, EW])
        qg = sb("qg", [P, 4, 2, H])
        oh = sb("oh", [P, RING, 2, P])
        eaT = sb("eaT", [P, 4, 2 * P], F32R)
        w1c_high = sb("w1c_high", [P, H], F32R)
        w1c_low = sb("w1c_low", [P, H], F32R)
        ohT = sb("ohT", [P, 4, 2, P], BF16)
        hq = sb("hq", [P, 2, 2, H])
        r = sb("r", [P, 2, 2, SW])

        eb_in, gathered = sem("eb_in", 2), sem("gathered", 4)
        oh_ok, t_tr, t_ok, h_mm, h_ok, r_ok, s_mm, s_ok, r_one = (
            sem("onehot_made"), sem("transposed"), sem("transposes_evacuated"), sem("h_mm"), sem("h_summed"),
            sem("relu_made"), sem("s_mm"), sem("s_added"), sem("ones_made"))
        low_ok = sem("low_parts_made")

        TR_BANKS = (0, 1, 4, 5)
        src_v = s.sorted_d.rearrange("(k g p j) w -> k p g (j w)", g=LOAD, p=P, j=2)

        with nc.Block() as block:
            @block.sync
            def _(sp):
                def load(i, c, first):
                    g = RING * i + LOAD * c
                    if not first:
                        for q in range(4):
                            sp.wait_ge(gathered[q], 64 * i + 32 * (c - 1))
                        apart(s, sp)
                        sp.wait_ge(t_tr, g + LOAD)
                        sp.wait_ge(oh_ok, g + LOAD)
                    sp.dma_start(eb[:, c, :, :, :].rearrange("p g j w -> p g (j w)"),
                                 src_v[ds(2 * i + c, 1)].rearrange("k p g w -> p (k g) w")).then_inc(eb_in[c], 16)

                for c in range(2):
                    load(0, c, True)
                with sp.Fori(1, NG // RING) as i:
                    for c in range(2):
                        load(i, c, False)

            @block.gpsimd
            def _(g):
                with g.Fori(0, NG // RING) as i:
                    for n in range(RING):
                        c, q = n // LOAD, n % 4
                        pair = RING * i + n
                        if n % LOAD == 0:
                            g.wait_ge(eb_in[c], 16 * i + 16)
                        g.wait_ge(h_ok, pair + 1)
                        apart(s, g)
                        for j in range(2):
                            g.indirect_dma_start(out=qg[:, q, j, :], out_offset=None, in_=s.q_tab,
                                                 in_offset=OFF(ap=eb[:, c, n % LOAD, j, ED:ED + 1].bitcast(I32), axis=0)
                                                 ).then_inc(gathered[q], 16)

            @block.tensor
            def _(pe):
                pe.sem_inc(t_tr, 8)
                pe.sem_inc(h_mm, 4)
                pe.sem_inc(s_mm, 8)

                def transposes(pair, n):
                    c, bank = n // LOAD % 2, s.bank[TR_BANKS[n % 4]]
                    pe.wait_ge(oh_ok, pair + 9)
                    pe.wait_ge(low_ok, pair + 1)
                    for j in range(2):
                        nc.tensor.transpose(bank[:, (2 + j) * P:(3 + j) * P], oh[:, n, j, :], s.ident[:, :])
                        last = nc.tensor.transpose(bank[0:ED, j * P:(j + 1) * P], eb[:, c, n % LOAD, j, 0:ED], s.ident[:, :])
                    last.then_inc(t_tr, 1)

                def hidden(pair, n, block_of):
                    q, b = n % 4, n % 2
                    pe.wait_ge(low_ok, pair + 5)
                    pe.wait_ge(h_ok, pair + 3)
                    for j in range(2):
                        into = s.bank[2 + b][:, j * H:(j + 1) * H]
                        both = eaT[:, q, j * P:(j + 1) * P]
                        nc.tensor.matmul(into, both, w1c_high[:, :], start=True, stop=False)
                        nc.tensor.matmul(into, both, w1c_low[:, :], start=False, stop=False)
                        for part in range(3):
                            last = nc.tensor.matmul(into, ohT[:, q, j, :],
                                                    s.big_p[:, ds(block_of * H3 + part * H, H)],
                                                    start=False, stop=part == 2)
                    last.then_inc(h_mm, 1)

                def summed(pair, n):
                    b = n % 2
                    pe.wait_ge(r_ok, pair + 3)
                    pe.wait_ge(s_ok, pair + 1)
                    for j in range(2):
                        last = nc.tensor.matmul(s.bank[6 + b][:, 0:SW], oh[:, n, j, :], r[:, b, j, :],
                                                start=j == 0, stop=j == 1)
                    last.then_inc(s_mm, 1)

                def turn(i, first, last):
                    _, blk = nc.values_load_multi_w_load_instructions(
                        s.blk_i[0:1, ds(RING * i, RING)], engines=(mybir.EngineType.PE,), min_val=0, max_val=NB - 1,
                        skip_runtime_bounds_check_because="the table is capped at the last block")
                    for n in range(RING):
                        pair = RING * i + n
                        if not (last and n >= RING - 2):
                            transposes(pair + 2, (n + 2) % RING)
                        hidden(pair, n, blk[n])
                        if not (first and n == 0):
                            summed(pair - 1, (n - 1) % RING)

                transposes(0, 0)
                transposes(1, 1)
                turn(0, True, False)
                with pe.Fori(1, NG // RING - 1) as i:
                    turn(i, False, False)
                turn(NG // RING - 1, False, True)
                summed(NG - 1, RING - 1)

            @block.scalar
            def _(act):
                act.sem_inc(t_ok, 2)
                act.sem_inc(r_ok, 2)

                def evacuate(pair, n):
                    q, bank = n % 4, s.bank[TR_BANKS[n % 4]]
                    act.wait_ge(t_tr, pair + 9)
                    act.wait_ge(h_mm, pair + 1)
                    nc.scalar.copy(ohT[:, q, :, :], bank[:, 2 * P:4 * P].rearrange("p (j n) -> p j n", j=2))
                    nc.scalar.copy(eaT[0:ED, q, :], bank[0:ED, 0:2 * P]).then_inc(t_ok, 1)

                def relu(pair, n):
                    b = n % 2
                    act.wait_ge(h_ok, pair + 5)
                    act.wait_ge(s_mm, pair + 7)
                    nc.scalar.activation(r[:, b, :, 0:H], hq[:, b, :, :], ACT.Relu).then_inc(r_ok, 1)

                act.wait_ge(r_one, 1)
                evacuate(0, 0)
                evacuate(1, 1)
                with act.Fori(0, NG // RING - 1) as i:
                    for n in range(RING):
                        evacuate(RING * i + n + 2, (n + 2) % RING)
                        relu(RING * i + n, n)
                for n in range(RING):
                    pair = NG - RING + n
                    if n < RING - 2:
                        evacuate(pair + 2, n + 2)
                    relu(pair, n)

            @block.vector
            def _(v):
                v.sem_inc(h_ok, 4)
                v.sem_inc(s_ok, 2)
                v.sem_inc(oh_ok, 8)
                v.sem_inc(low_ok, 4)
                v.memset(s.big_s[:, :], 0.0)
                v.tensor_copy(w1c_high[:, :], s.w1c[:, :])
                v.memset(r[:, :, :, H:SW], 1.0).then_inc(r_one, 1)
                v.wait_ge(r_one, 1)
                v.tensor_tensor(w1c_low[:, :], s.w1c[:, :], w1c_high[:, :].bitcast(F32), ALU.subtract)

                def onehot(pair, n, load):
                    c = n // LOAD
                    v.wait_ge(eb_in[c], load)
                    v.wait_ge(s_mm, pair + 1)
                    for j in range(2):
                        last = v.tensor_scalar(oh[:, n, j, :], s.iota_f[:, :], eb[:, c, n % LOAD, j, ED + 1:EW], None,
                                               ALU.is_equal)
                    last.then_inc(oh_ok, 1)

                def low_parts(pair, n):
                    q = n % 4
                    v.wait_ge(t_ok, pair + 3)
                    v.tensor_tensor(eaT[ED:P, q, :], s.bank[TR_BANKS[q]][0:ED, 0:2 * P], eaT[0:ED, q, :].bitcast(F32),
                                    ALU.subtract).then_inc(low_ok, 1)

                def add_q(pair, n, uses):
                    b, q = n % 2, n % 4
                    v.wait_ge(h_mm, pair + 5)
                    v.wait_ge(gathered[q], uses)
                    v.wait_ge(r_ok, pair + 1)
                    v.tensor_tensor(hq[:, b, :, :].rearrange("p j f -> p (j f)"), s.bank[2 + b][:, :],
                                    qg[:, q, :, :].rearrange("p j f -> p (j f)"), ALU.add).then_inc(h_ok, 1)

                def add_s(pair, n, block_of):
                    b = n % 2
                    v.wait_ge(s_mm, pair + 9)
                    v.wait_ge(s_ok, pair + 2)
                    rows = s.big_s[:, ds(block_of * SW, SW)]
                    v.tensor_tensor(rows, rows, s.bank[6 + b][:, 0:SW], ALU.add).then_inc(s_ok, 1)

                def load_blocks(at, count):
                    _, blk = nc.values_load_multi_w_load_instructions(
                        s.blk_i[0:1, ds(at, count)], engines=(mybir.EngineType.DVE,), min_val=0, max_val=NB - 1,
                        skip_runtime_bounds_check_because="the table is capped at the last block")
                    return blk

                def turn(i, first, last):
                    blk = load_blocks(RING * i, RING) if first else load_blocks(RING * i - 1, RING)
                    for n in range(RING):
                        pair = RING * i + n
                        add_q(pair, n, 64 * i + 32 * (n // 4) + 32)
                        if not (last and n >= RING - 2):
                            low_parts(pair + 2, (n + 2) % RING)
                        if not (last and n >= RING - 4):
                            onehot(pair + 4, (n + 4) % RING, 16 * (i + (n + 4) // RING) + 16)
                        if not (first and n == 0):
                            add_s(pair - 1, (n - 1) % RING, blk[n - 1] if first else blk[n])

                for n in range(4):
                    onehot(n, n, 16)
                low_parts(0, 0)
                low_parts(1, 1)
                turn(0, True, False)
                with v.Fori(1, NG // RING - 1) as i:
                    turn(i, False, False)
                turn(NG // RING - 1, False, True)
                add_s(NG - 1, RING - 1, load_blocks(NG - 1, 1)[0])


def gru(nc, s, a):
    with ExitStack() as ctx:
        def sb(name, shape, dt=F32):
            return ctx.enter_context(nc.sbuf_tensor(name, shape, dt))

        sem = s.sem

        sums = sb("sums", [P, 2, SW])
        sT = sb("sT", [P, 2, 2, P])
        degT = sb("degT", [2, 2, P])
        ght = sb("ght", [P, 2, H3])
        xnt = sb("xnt", [P, 2, H])
        xmt = sb("xmt", [P, 2, H])
        rz = sb("rz", [P, 2, 2 * H])
        cand = sb("cand", [P, 2, H])

        gh_in, xn_in, xm_in = sem("gh_in", 2), sem("xnt_in", 2), sem("xm_in", 2)
        s_cp, s_tr, s_ok, rz_mm, n_mm = sem("sums_copied"), sem("sums_transposed"), sem("sT_made"), sem("rz_mm"), sem("n_mm")
        rz_in, rz_ok, c_in, c_ok, done, deg_one = (sem("rz_summed"), sem("rz_made"), sem("cand_summed"), sem("cand_made"),
                                                   sem("tile_done"), sem("deg_ones"))

        with nc.Block() as block:
            @block.sync
            def _(sp):
                with sp.Fori(0, NT // 2) as i:
                    for j in range(2):
                        one = ds(2 * i + j, 1)
                        sp.wait_ge(c_in, 2 * i + j + 1)
                        sp.dma_start(ght[:, j, :], s.gh_d[one].rearrange("t p f -> p (t f)")).then_inc(gh_in[j], 16)
                        sp.wait_ge(done, 2 * i + j + 1)
                        sp.dma_start(xnt[:, j, :], s.xn_d[one].rearrange("t p f -> p (t f)")).then_inc(xn_in[j], 16)
                        sp.dma_start(xmt[:, j, :], s.xm_d[one].rearrange("t p f -> p (t f)")).then_inc(xm_in[j], 16)

            @block.tensor
            def _(pe):
                pe.sem_inc(s_tr, 2)
                pe.sem_inc(n_mm, 2)

                def transposes(t, j):
                    pe.wait_ge(s_cp, t + 1)
                    pe.wait_ge(s_ok, t + 1)
                    for c in range(2):
                        nc.tensor.transpose(s.bank[j][:, c * P:(c + 1) * P], sums[:, j, c * P:(c + 1) * P], s.ident[:, :])
                    nc.tensor.transpose(s.bank[j][0:1, 2 * P:3 * P], sums[:, j, H:SW], s.ident[:, :]).then_inc(s_tr, 1)

                def products(t, j):
                    pe.wait_ge(s_ok, t + 3)
                    pe.wait_ge(c_in, t + 1)
                    for bank, lo, hi, signal in ((2 + j, 0, 512, rz_mm), (4 + j, 512, H3, n_mm)):
                        for c in range(2):
                            nc.tensor.matmul(s.bank[bank][:, 0:hi - lo], sT[:, j, c, :], s.wg[:, c, lo:hi],
                                             start=c == 0, stop=False)
                        nc.tensor.matmul(s.bank[bank][:, 0:hi - lo], degT[:, j, :], s.bg[:, lo:hi],
                                         start=False, stop=True).then_inc(signal, 1)

                transposes(0, 0)
                with pe.Fori(0, NT // 2 - 1) as i:
                    for j in range(2):
                        transposes(2 * i + j + 1, 1 - j)
                        products(2 * i + j, j)
                transposes(NT - 1, 1)
                products(NT - 2, 0)
                products(NT - 1, 1)

            @block.scalar
            def _(act):
                act.sem_inc(s_ok, 2)
                act.wait_ge(deg_one, 1)

                def copy_sums(t, j):
                    act.wait_ge(s_tr, t + 1)
                    nc.scalar.copy(sums[:, j, :], s.big_s[:, ds(t * SW, SW)]).then_inc(s_cp, 1)

                def evacuate(t, j):
                    act.wait_ge(s_tr, t + 3)
                    act.wait_ge(n_mm, t + 1)
                    nc.scalar.copy(degT[0:1, j, :], s.bank[j][0:1, 2 * P:3 * P])
                    nc.scalar.copy(sT[:, j, :, :], s.bank[j][:, 0:H].rearrange("p (c n) -> p c n", c=2)).then_inc(s_ok, 1)

                def gates(t, j):
                    act.wait_ge(rz_in, t + 1)
                    nc.scalar.activation(rz[:, j, :], rz[:, j, :], ACT.Sigmoid).then_inc(rz_ok, 1)
                    act.wait_ge(c_in, t + 3)
                    nc.scalar.activation(cand[:, j, :], cand[:, j, :], ACT.Tanh).then_inc(c_ok, 1)

                copy_sums(0, 0)
                copy_sums(1, 1)
                evacuate(0, 0)
                with act.Fori(0, NT // 2 - 1) as i:
                    for j in range(2):
                        evacuate(2 * i + j + 1, 1 - j)
                        copy_sums(2 * i + j + 2, j)
                        gates(2 * i + j, j)
                evacuate(NT - 1, 1)
                gates(NT - 2, 0)
                gates(NT - 1, 1)

            @block.vector
            def _(v):
                ch = Chain(v, s.v_step, s.v_steps)
                v.sem_inc(done, 2)
                v.sem_inc(c_in, 2)
                v.memset(degT[:, :, :], 1.0).then_inc(deg_one, 1)
                base = ch.n

                def gate_sums(t, j, turn):
                    v.wait_ge(rz_mm, t + 1)
                    v.wait_ge(gh_in[j], 16 * turn + 16)
                    v.tensor_tensor(rz[:, j, :], s.bank[2 + j][:, :], ght[:, j, 0:512], ALU.add).then_inc(rz_in, 1)

                def candidate(t, j):
                    ch.n = base + 6 * t
                    v.wait_ge(rz_ok, t + 1)
                    v.wait_ge(n_mm, t + 3)
                    ch.then(v.tensor_tensor(cand[:, j, :], rz[:, j, 0:H], ght[:, j, 512:H3], ALU.mult))
                    v.tensor_tensor(cand[:, j, :], cand[:, j, :], s.bank[4 + j][:, 0:H], ALU.add).then_inc(c_in, 1)

                def update(t, j, turn):
                    ch.n = base + 6 * t + 1
                    v.wait_ge(c_ok, t + 1)
                    v.wait_ge(xn_in[j], 16 * turn + 16)
                    v.wait_ge(xm_in[j], 16 * turn + 16)
                    x1 = s.x1_all[:, ds(t * H, H)]
                    ch.mark(v.tensor_tensor(xnt[:, j, :], xnt[:, j, :], cand[:, j, :], ALU.subtract))
                    ch.mark(v.tensor_tensor(xmt[:, j, :], xmt[:, j, :], cand[:, j, :], ALU.add))
                    ch.all_but(1)
                    ch.mark(v.tensor_tensor(xnt[:, j, :], xnt[:, j, :], rz[:, j, H:2 * H], ALU.mult))
                    ch.all_but(0)
                    ch.mark(v.tensor_tensor(x1, xmt[:, j, :], xnt[:, j, :], ALU.add))
                    ch.all_but(0)
                    v.sem_inc(done, 1)
                    ch.mark(v.bn_stats(s.st2[:, ds(t, 1), :].rearrange("p a b -> p (a b)"), x1))

                gate_sums(0, 0, 0)
                candidate(0, 0)
                gate_sums(1, 1, 0)
                update(0, 0, 0)
                candidate(1, 1)
                with v.Fori(1, NT // 2) as i:
                    gate_sums(2 * i, 0, i)
                    update(2 * i - 1, 1, i - 1)
                    candidate(2 * i, 0)
                    gate_sums(2 * i + 1, 1, i)
                    update(2 * i, 0, i)
                    candidate(2 * i + 1, 1)
                update(NT - 1, 1, NT // 2 - 1)
                s.v_steps = base + NT * 6


def routing(nc, s, a):
    with ExitStack() as ctx:
        def sb(name, shape, dt=F32):
            return ctx.enter_context(nc.sbuf_tensor(name, shape, dt))

        sem = s.sem

        W = NT * NX
        var, tmp = sb("var2", [P, NT]), sb("tmp2", [P, NT])
        mean, rstd = sb("mean2", [P, NT]), sb("rstd2", [P, NT])
        xl = sb("xl", [P, 2, H])
        xlT = sb("xlT", [P, 2, 2, P])
        lg, pr, t1, t2, t3 = (sb(n, [P, NT, NX]) for n in ("lg", "pr", "t1", "t2", "t3"))
        keyv = sb("keyv", [P, NX])
        basev = sb("basev", [P, NX])
        m1, m2, valid, gate = (sb(n, [P, NT]) for n in ("m1", "m2", "valid", "gate"))
        xr = sb("xr", [P, 4, XW])
        xi = sb("xi", [P, 4], I32)
        zrow = sb("zrow2", [P, 8, XW])

        var_ok, root_ok = sem("var2_made"), sem("root2_made")
        xl_ok, xl_tr, xlT_ok, lg_mm, lg_ok = sem("xl_made"), sem("xl_transposed"), sem("xlT_made"), sem("lg_mm"), sem("lg_made")
        sh_ok, ex_ok, oh_ok, rank_mm = sem("shifted"), sem("exp_made"), sem("onehot2_made"), sem("rank_mm")
        z_ok, z_out, xr_ok, xr_out = sem("zeros_made"), sem("zeros_out"), sem("xr_made"), sem("xr_out", 2)

        def flat(x):
            return x[:, :, :].rearrange("p t e -> p (t e)")

        def over(x, t=NT):
            return x.unsqueeze(2).to_broadcast([P, t, NX])

        with nc.Block() as block:
            @block.sync
            def _(sp):
                sp.wait_ge(z_ok, 1)
                rows, step = NX * CAP, P * 8
                n = 0
                for at in range(0, rows - step + 1, step):
                    sp.dma_start(s.routed_d[at:at + step, :].rearrange("(p r) w -> p r w", r=8), zrow[:, :, :]).then_inc(z_out, 16)
                    n += 1
                rest = rows - n * step
                if rest >= P:
                    k = rest // P
                    sp.dma_start(s.routed_d[rows - rest:rows - rest + k * P, :].rearrange("(p r) w -> p r w", r=k),
                                 zrow[:, 0:k, :]).then_inc(z_out, 16)
                    n += 1
                    rest -= k * P
                if rest:
                    sp.dma_start(s.routed_d[rows - rest:rows, :], zrow[0:rest, 0, :]).then_inc(z_out, 16)
                    n += 1
                assert n == ZERO_DMAS
                sp.wait_ge(z_out, 16 * n)

            @block.gpsimd
            def _(g):
                g.memset(zrow[:, :, :], 0.0).then_inc(z_ok, 1)
                for q in range(2):
                    credit(s, g, xr_out[q], 16)
                g.wait_ge(z_out, 16 * ZERO_DMAS)
                with g.Fori(0, NT // 2) as i:
                    for j in range(2):
                        g.wait_ge(xr_ok, 2 * i + j + 1)
                        apart(s, g)
                        g.indirect_dma_start(out=s.routed_d, out_offset=OFF(ap=xi[:, j:j + 1], axis=0),
                                             in_=xr[:, j, :], in_offset=None, bounds_check=NX * CAP - 1,
                                             oob_is_err=False).then_inc(xr_out[j], 16)
                for j in range(2):
                    g.wait_ge(xr_out[j], 8 * NT + 16)

            @block.tensor
            def _(pe):
                pe.sem_inc(xl_tr, 2)
                pe.sem_inc(lg_mm, 2)
                with pe.Fori(0, NT // 2) as i:
                    for j in range(2):
                        t = 2 * i + j
                        pe.wait_ge(xl_ok, t + 1)
                        pe.wait_ge(xlT_ok, t + 1)
                        for c in range(2):
                            last = nc.tensor.transpose(s.bank[j][:, c * P:(c + 1) * P], xl[:, j, c * P:(c + 1) * P], s.ident[:, :])
                        last.then_inc(xl_tr, 1)
                    for j in range(2):
                        t = 2 * i + j
                        pe.wait_ge(xlT_ok, t + 3)
                        pe.wait_ge(lg_ok, t + 1)
                        for c in range(2):
                            last = nc.tensor.matmul(s.bank[2 + j][:, 0:NX], xlT[:, j, c, :], s.gatew[:, c, :],
                                                    start=c == 0, stop=c == 1)
                        last.then_inc(lg_mm, 1)
                pe.wait_ge(oh_ok, 1)
                nc.tensor.matmul(s.bank[4][:, 0:W], s.upper[:, :], flat(t1), start=True, stop=True)
                nc.tensor.matmul(s.bank[5][:, 0:W], s.ones[:, :], flat(t1), start=True, stop=True).then_inc(rank_mm, 1)

            @block.scalar
            def _(act):
                act.wait_ge(var_ok, 1)
                nc.scalar.activation(rstd[:, :], var[:, :], ACT.Sqrt).then_inc(root_ok, 1)
                act.sem_inc(xlT_ok, 2)
                with act.Fori(0, NT // 2) as i:
                    for j in range(2):
                        t = 2 * i + j
                        act.wait_ge(xl_tr, t + 3)
                        act.wait_ge(lg_mm, t + 1)
                        nc.scalar.copy(xlT[:, j, :, :], s.bank[j][:, 0:H].rearrange("p (c n) -> p c n", c=2)).then_inc(xlT_ok, 1)
                act.wait_ge(sh_ok, 1)
                nc.scalar.activation(flat(lg), flat(lg), ACT.Exp).then_inc(ex_ok, 1)

            @block.vector
            def _(v):
                ch = Chain(v, s.v_step, s.v_steps)
                batch_norm_factors(v, ch, s.st2, mean[:, :], var[:, :], tmp[:, :])
                v.tensor_copy(tmp[:, :], var[:, :]).then_inc(var_ok, 1)
                v.wait_ge(root_ok, 1)
                ch.then(v.reciprocal(rstd[:, :], rstd[:, :]))
                v.sem_inc(lg_ok, 2)
                with v.Fori(0, NT // 2) as i:
                    for j in range(2):
                        t = 2 * i + j
                        v.wait_ge(xl_tr, t + 1)
                        v.tensor_scalar(xl[:, j, :], s.x1_all[:, ds(t * H, H)], mean[:, ds(t, 1)], rstd[:, ds(t, 1)],
                                        ALU.subtract, ALU.mult).then_inc(xl_ok, 1)
                    for j in range(2):
                        t = 2 * i + j
                        v.wait_ge(lg_mm, t + 3)
                        v.tensor_tensor(lg[:, ds(t, 1), :].rearrange("p a e -> p (a e)"), s.bank[2 + j][:, 0:NX],
                                        s.gateb[:, :], ALU.add).then_inc(lg_ok, 1)
                v.wait_ge(lg_ok, NT + 2)
                ch.then(v.tensor_reduce(m1[:, :], lg[:, :, :], AX.X, ALU.max))
                v.tensor_tensor(lg[:, :, :], lg[:, :, :], over(m1[:, :]), ALU.subtract).then_inc(sh_ok, 1)
                v.wait_ge(ex_ok, 1)
                ch.then(v.tensor_reduce(m1[:, :], lg[:, :, :], AX.X, ALU.add))
                ch.then(v.reciprocal(m1[:, :], m1[:, :]))
                ch.then(v.tensor_tensor(pr[:, :, :], lg[:, :, :], over(m1[:, :]), ALU.mult))
                ch.then(v.tensor_reduce(gate[:, :], pr[:, :, :], AX.X, ALU.max))
                ch.then(v.tensor_scalar(keyv[:, :], s.iota_f[:, 0:NX], -1.0, float(NX), ALU.mult, ALU.add))
                ch.then(v.tensor_tensor(t1[:, :, :], pr[:, :, :], over(gate[:, :]), ALU.is_equal))
                ch.then(v.tensor_tensor(t1[:, :, :], t1[:, :, :], keyv[:, :].unsqueeze(1).to_broadcast([P, NT, NX]), ALU.mult))
                ch.then(v.tensor_reduce(m1[:, :], t1[:, :, :], AX.X, ALU.max))
                ch.then(v.tensor_tensor(t1[:, :, :], t1[:, :, :], over(m1[:, :]), ALU.is_equal))
                ch.then(v.tensor_scalar(valid[:, :], s.node_f[:, :], float(N), None, ALU.is_lt))
                v.tensor_tensor(t1[:, :, :], t1[:, :, :], over(valid[:, :]), ALU.mult).then_inc(oh_ok, 1)
                v.wait_ge(rank_mm, 1)
                ch.then(v.tensor_copy(flat(t2), s.bank[5][:, 0:W]))
                for e in range(NX):
                    last = v.tensor_tensor_scan(t3[:, :, e], s.ones[:, 0:NT], t2[:, :, e], 0.0, ALU.mult, ALU.add)
                ch.then(last)
                ch.then(v.tensor_tensor(flat(t3), flat(t3), flat(t2), ALU.subtract))
                ch.then(v.tensor_tensor(flat(t3), flat(t3), s.bank[4][:, 0:W], ALU.add))
                ch.then(v.tensor_tensor(flat(t2), flat(t3), flat(t1), ALU.mult))
                ch.then(v.tensor_reduce(m1[:, :], t2[:, :, :], AX.X, ALU.add))
                ch.then(v.tensor_scalar(s.kept[:, :], m1[:, :], float(CAP), None, ALU.is_lt))
                ch.then(v.tensor_tensor(s.kept[:, :], s.kept[:, :], valid[:, :], ALU.mult))
                ch.then(v.tensor_scalar(basev[:, :], s.iota_f[:, 0:NX], float(CAP), None, ALU.mult))
                ch.then(v.tensor_tensor(t2[:, :, :], t1[:, :, :], basev[:, :].unsqueeze(1).to_broadcast([P, NT, NX]), ALU.mult))
                ch.then(v.tensor_reduce(m2[:, :], t2[:, :, :], AX.X, ALU.add))
                ch.then(v.tensor_tensor(m1[:, :], m1[:, :], m2[:, :], ALU.add))
                ch.then(v.tensor_tensor(m1[:, :], m1[:, :], s.kept[:, :], ALU.mult))
                ch.then(v.tensor_copy(s.place[:, :], m1[:, :]))
                ch.then(v.tensor_scalar(m2[:, :], s.kept[:, :], -float(2 * NX * CAP), float(2 * NX * CAP), ALU.mult, ALU.add))
                ch.then(v.tensor_tensor(m1[:, :], m1[:, :], m2[:, :], ALU.add))
                s.v_steps = ch.n
                with v.Fori(0, NT // 2) as i:
                    for j in range(2):
                        t = 2 * i + j
                        v.wait_ge(xr_out[j], 16 * i + 16)
                        v.tensor_scalar(xr[:, j, 0:H], s.x1_all[:, ds(t * H, H)], mean[:, ds(t, 1)], rstd[:, ds(t, 1)],
                                        ALU.subtract, ALU.mult)
                        v.tensor_copy(xr[:, j, H:XW], gate[:, ds(t, 1)])
                        v.tensor_copy(xi[:, j:j + 1], m1[:, ds(t, 1)]).then_inc(xr_ok, 1)


def experts(nc, s, a):
    with ExitStack() as ctx:
        def sb(name, shape, dt=F32):
            return ctx.enter_context(nc.sbuf_tensor(name, shape, dt))

        sem = s.sem

        FT = FF // P
        HALVES = ((0, -(-CAP // 2)), (-(-CAP // 2), CAP))
        w1 = sb("w1", [P, 2, 2, FF])
        w2 = sb("w2", [P, 2, FT, H])
        b1raw = sb("b1raw", [NX * FT, P])
        b1T = sb("b1T", [P, NX * FT])
        b1e = sb("b1e", [P, 2, FT])
        b2b = sb("b2b", [P, 2, H])
        xg = sb("xg", [P, 2, CT, XW])
        xT = s.big_s[:, 0:2 * CT * P].rearrange("p (c n) -> p c n", c=2)
        hT = s.big_s[:, 2 * CT * P:(2 + FT) * CT * P].rearrange("p (f n) -> p f n", f=FT)
        y = sb("y", [P, 2, H])
        fix = sb("fix", [P, 2])
        mask = sb("mask", [P, 3, H], I32)

        b1_in, b1_tr, b1_ok = sem("b1_in"), sem("b1_tr"), sem("b1_made")
        w_in, x_in = sem("w_in6", 2), sem("x_in6", 2)
        x_tr, x_ok, h_mm, h_ok, y_mm, y_ok, y_st, y_fr = (sem("x_tr6"), sem("xT_made"), sem("h_mm6"), sem("hT_made"), sem("y_mm"),
                                                          sem("y_made"), sem("y_stored", 2), sem("y_used"))
        w1_v = a.fw1.rearrange("e (c p) f -> e p c f", p=P)
        w2_v = a.fw2.rearrange("e (k p) d -> e p k d", p=P)
        rows_v = s.routed_d.rearrange("(e c) w -> e c w", e=NX)
        y_v = s.y_d.rearrange("(e c) w -> e c w", e=NX)
        FULL = (CT - 1) * P

        with nc.Block() as block:
            @block.sync
            def _(sp):
                sp.dma_start(b1raw[:, :], a.fb1.rearrange("e (k p) -> (e k) p", p=P)).then_inc(b1_in, 16)
                with sp.Fori(0, NX // 2) as i:
                    for j in range(2):
                        e = 2 * i + j
                        one = ds(e, 1)
                        sp.wait_ge(y_fr, (e + 1) * CT - (CT - 1))
                        sp.dma_start(xg[:, j, 0:CT - 1, :], rows_v[one, 0:FULL, :].rearrange("e (t p) w -> p (e t) w", p=P)).then_inc(x_in[j], 16)
                        sp.dma_start(xg[0:CLAST, j, CT - 1, :], rows_v[one, FULL:CAP, :].rearrange("e p w -> p (e w)")).then_inc(x_in[j], 16)
                        sp.dma_start(w1[:, j, :, :], w1_v[one].rearrange("e p c f -> p (e c) f")).then_inc(w_in[j], 16)
                        sp.dma_start(w2[:, j, :, :], w2_v[one].rearrange("e p k d -> p (e k) d")).then_inc(w_in[j], 16)
                        sp.dma_start(b2b[:, j, :], a.fb2[one].rearrange("e d -> (e d)").partition_broadcast(P)).then_inc(w_in[j], 16)

            @block.tensor
            def _(pe):
                pe.wait_ge(b1_in, 16)
                nc.tensor.transpose(s.bank[0][:, 0:NX * FT], b1raw[:, :], s.ident[0:NX * FT, 0:NX * FT]).then_inc(b1_tr, 1)
                pe.wait_ge(b1_ok, 1)
                pe.sem_inc(y_mm, 2)
                with pe.Fori(0, NX // 2) as i:
                    for j in range(2):
                        e = 2 * i + j
                        pe.wait_ge(x_in[j], 32 * i + 32)
                        for t in range(CT):
                            rows = P if t < CT - 1 else CLAST
                            b = t % 2
                            pe.wait_ge(x_ok, e * CT + t + 1)
                            for c in range(2):
                                last = nc.tensor.transpose(s.bank[b][:, c * P:c * P + rows], xg[0:rows, j, t, c * P:(c + 1) * P],
                                                           s.ident[0:rows, 0:rows])
                            last.then_inc(x_tr, 1)
                        pe.wait_ge(x_ok, e * CT + CT + 2)
                        pe.wait_ge(w_in[j], 48 * i + 48)
                        for f in range(FT):
                            for k, (lo, hi) in enumerate(HALVES):
                                q = 2 * f + k
                                pe.wait_ge(h_ok, e * 2 * FT + q + 1)
                                for c in range(2):
                                    last = nc.tensor.matmul(s.bank[2 + q % 4][:, 0:hi - lo], w1[:, j, c, f * P:(f + 1) * P],
                                                            xT[:, c, lo:hi], start=c == 0, stop=c == 1)
                                last.then_inc(h_mm, 1)
                        pe.wait_ge(h_ok, (e + 1) * 2 * FT + 4)
                        for t in range(CT):
                            rows = P if t < CT - 1 else CLAST
                            pe.wait_ge(y_fr, e * CT + t + 1)
                            for f in range(FT):
                                last = nc.tensor.matmul(s.bank[6 + t % 2][0:rows, 0:H], hT[:, f, t * P:t * P + rows],
                                                        w2[:, j, f, :], start=f == 0, stop=f == FT - 1)
                            last.then_inc(y_mm, 1)

            @block.scalar
            def _(act):
                act.sem_inc(h_ok, 4)
                act.sem_inc(x_ok, 2)
                act.wait_ge(b1_tr, 1)
                nc.scalar.copy(b1T[:, :], s.bank[0][:, 0:NX * FT]).then_inc(b1_ok, 1)
                act.wait_ge(b1_ok, 1)
                with act.Fori(0, NX // 2) as i:
                    for j in range(2):
                        e = 2 * i + j
                        for t in range(CT):
                            rows = P if t < CT - 1 else CLAST
                            act.wait_ge(x_tr, e * CT + t + 1)
                            nc.scalar.copy(xT[:, :, t * P:t * P + rows],
                                           s.bank[t % 2][:, 0:H].rearrange("p (c n) -> p c n", c=2)[:, :, 0:rows]).then_inc(x_ok, 1)
                        nc.scalar.copy(b1e[:, j, :], b1T[:, ds(e * FT, FT)]).then_inc(b1_ok, 1)
                        act.wait_ge(b1_ok, e + 2)
                        act.wait_ge(y_mm, e * CT + 2)
                        for f in range(FT):
                            for k, (lo, hi) in enumerate(HALVES):
                                q = 2 * f + k
                                act.wait_ge(h_mm, e * 2 * FT + q + 1)
                                nc.scalar.activation(hT[:, f, lo:hi], s.bank[2 + q % 4][:, 0:hi - lo], ACT.Relu,
                                                     bias=b1e[:, j, f:f + 1]).then_inc(h_ok, 1)

            @block.vector
            def _(v):
                ch = Chain(v, s.v_step, s.v_steps)
                v.sem_inc(y_fr, 2)
                ch.then(v.memset(fix[:, 0:1], 1e4))
                ch.then(v.memset(fix[:, 1:2], -1e4))
                base = ch.n
                with v.Fori(0, NX // 2) as i:
                    for j in range(2):
                        e = 2 * i + j
                        v.wait_ge(w_in[j], 48 * i + 48)
                        v.wait_ge(x_in[j], 32 * i + 32)
                        for t in range(CT):
                            rows = P if t < CT - 1 else CLAST
                            b = t % 2
                            ch.n = base + (e * CT + t) * 5
                            v.wait_ge(y_mm, e * CT + t + 3)
                            v.wait_ge(y_st[b], 16 * (e * (CT // 2) + t // 2) + 16)
                            yt = y[0:rows, b, :]
                            ch.then(v.tensor_tensor(yt, s.bank[6 + b][0:rows, 0:H], b2b[0:rows, j, :], ALU.add))
                            ch.then(v.tensor_scalar(yt, yt, xg[0:rows, j, t, H:XW], None, ALU.mult))
                            v.tensor_tensor(mask[0:rows, 0, :], yt, yt, ALU.not_equal)
                            v.tensor_scalar(mask[0:rows, 1, :], yt, FMAX, None, ALU.is_gt)
                            ch.then(v.tensor_scalar(mask[0:rows, 2, :], yt, -FMAX, None, ALU.is_lt))
                            apart(s, v)
                            ch.then(v.copy_predicated(yt, mask[0:rows, 0, :], s.zerob[0:rows, 0:1].to_broadcast([rows, H])))
                            apart(s, v)
                            ch.then(v.copy_predicated(yt, mask[0:rows, 1, :], fix[0:rows, 0:1].to_broadcast([rows, H])))
                            apart(s, v)
                            v.copy_predicated(yt, mask[0:rows, 2, :], fix[0:rows, 1:2].to_broadcast([rows, H])).then_inc(y_fr, 1)

            @block.gpsimd
            def _(g):
                for j in range(2):
                    credit(s, g, y_st[j], 16)
                with g.Fori(0, NX // 2) as i:
                    for j in range(2):
                        e = 2 * i + j
                        for t in range(CT):
                            rows = P if t < CT - 1 else CLAST
                            g.wait_ge(y_fr, e * CT + t + 3)
                            g.dma_start(y_v[ds(e, 1), t * P:t * P + rows, :].rearrange("e p w -> p (e w)"),
                                        y[0:rows, t % 2, :]).then_inc(y_st[t % 2], 16)
                for j in range(2):
                    g.wait_ge(y_st[j], 16 * NX * CT // 2 + 16)


def combine(nc, s, a):
    with ExitStack() as ctx:
        def sb(name, shape, dt=F32):
            return ctx.enter_context(nc.sbuf_tensor(name, shape, dt))

        sem = s.sem

        RC = 2
        yg = sb("yg", [P, RC, H])
        gi = sb("gi", [P, RC], I32)
        ot = sb("ot7", [P, RC, H])
        gi_ok = sem("place_copied")
        o_ok = sem("o_made")
        y_in, o_st = sem("y_in", RC), sem("o_stored", RC)
        full = REAL - 1
        assert full % RC == 0
        out_v = a.out[0:full * P, :].rearrange("(t p) f -> t p f", p=P)

        with nc.Block() as block:
            @block.gpsimd
            def _(g):
                def gather(q, n):
                    g.wait_ge(gi_ok, n + 1)
                    apart(s, g)
                    g.indirect_dma_start(out=yg[:, q, :], out_offset=None, in_=s.y_d,
                                         in_offset=OFF(ap=gi[:, q:q + 1], axis=0)).then_inc(y_in[q], 16)

                with g.Fori(0, full // RC) as i:
                    for q in range(RC):
                        gather(q, RC * i + q)
                gather(0, full)

            @block.vector
            def _(v):
                v.sem_inc(o_ok, RC)

                def place(q, t):
                    v.tensor_copy(gi[:, q:q + 1], s.place[:, ds(t, 1)]).then_inc(gi_ok, 1)

                def add(q, t, turns):
                    v.wait_ge(y_in[q], 16 * turns + 16)
                    v.wait_ge(o_st[q], 16 * turns + 16)
                    v.scalar_tensor_tensor(out=ot[:, q, :], in0=yg[:, q, :], scalar=s.kept[:, ds(t, 1)],
                                           in1=s.x1_all[:, ds(t * H, H)], op0=ALU.mult, op1=ALU.add).then_inc(o_ok, 1)
                    v.wait_ge(o_ok, t + RC + 1)

                for q in range(RC):
                    place(q, q)
                with v.Fori(0, full // RC - 1) as i:
                    for q in range(RC):
                        add(q, RC * i + q, i)
                        place(q, RC * i + q + RC)
                for q in range(RC):
                    add(q, full - RC + q, full // RC - 1)
                    if q == 0:
                        place(0, full)
                add(0, full, full // RC)

            @block.sync
            def _(sp):
                for q in range(RC):
                    credit(s, sp, o_st[q], 16)
                with sp.Fori(0, full // RC) as i:
                    for q in range(RC):
                        sp.wait_ge(o_ok, RC * i + q + RC + 1)
                        sp.dma_start(out_v[ds(RC * i + q, 1)].rearrange("t p f -> p (t f)"), ot[:, q, :]).then_inc(o_st[q], 16)
                sp.wait_ge(o_ok, full + RC + 1)
                sp.dma_start(a.out[full * P:N, :], ot[0:TAIL, 0, :]).then_inc(o_st[0], 16)
                sp.wait_ge(o_st[0], 16 * (full // RC + 2))
                sp.wait_ge(o_st[1], 16 * (full // RC + 1))


def build(nc, a):
    with ExitStack() as ctx:
        def sb(name, shape, dt=F32):
            return ctx.enter_context(nc.sbuf_tensor(name, shape, dt))

        def dram(name, shape):
            return nc.dram_tensor(name, shape, F32).ap()

        def sem(name, n=None):
            if n is None:
                return ctx.enter_context(nc.semaphore(name))
            return [ctx.enter_context(nc.semaphore(f"{name}{k}")) for k in range(n)]

        s = Shared()
        s.sem = sem
        s.carried = sem("waits_carried")
        s.x_in = sem("x_in")
        s.v_step, s.v_steps = sem("v_step"), 0
        s.bank = [ctx.enter_context(nc.psum_tensor(f"bank{k}", [P, 512], F32)) for k in range(8)]
        s.x_pad = dram("x_pad", [NTX, P, H])
        s.xn_d = dram("xn_d", [NT, P, H])
        s.q_tab = dram("q_tab", [NT * P, H])
        s.q_tiles = s.q_tab.rearrange("(t p) f -> t p f", p=P)
        s.v_d = dram("v_d", [NT, P, H])
        s.qs_d = dram("qs_d", [NT, P, H])
        s.gh_d = dram("gh_d", [NT, P, H3])
        s.xm_d = dram("xm_d", [NT, P, H])
        s.sorted_d = dram("sorted_d", [SLOTS, EW])
        s.routed_d = dram("routed_d", [NX * CAP, XW])
        s.y_d = dram("y_d", [NX * CAP, H])
        s.credit_d, s.credits = dram("credit_d", [32, 2]), 0
        s.big_s = sb("big_s", [P, NT * SW])
        s.big_p = sb("big_p", [P, NT * H3], BF16)
        s.x1_all = s.big_p[:, 0:2 * NT * H].bitcast(F32)
        s.ident = sb("ident", [P, P])
        s.iota_f = sb("iota_f", [P, P])
        s.node_f = sb("node_f", [P, NT])
        s.ones = sb("ones", [P, P])
        s.upper = sb("upper", [P, P])
        s.zerob = sb("zerob", [P, 2])
        s.w1c = sb("w1c", [P, H])
        s.wg = sb("wg", [P, 2, H3])
        s.bg = sb("bg", [2, H3])
        s.gatew = sb("gatew", [P, 2, NX])
        s.gateb = sb("gateb", [P, NX])
        s.blk_i = sb("blk_i", [1, NG], I32)
        s.st2 = sb("st2_all", [P, NT, 6])
        s.kept = sb("kept", [P, NT])
        s.place = sb("place", [P, NT], I32)
        with ExitStack() as early:
            def eb(name, shape, dt=F32):
                return early.enter_context(nc.sbuf_tensor(name, shape, dt))

            s.fused_w = eb("fused_w", [P, 2, 4 * H])
            s.whhT = eb("whhT", [P, 2, H3])
            s.wk = eb("wk", [P, 2, H])
            s.wout = eb("wout", [P, 2, H])
            s.b1b = eb("b1b", [P, H])
            s.bhhb = eb("bhhb", [P, H3])
            s.gammab = eb("gammab", [P, H])
            s.dst_i = eb("dst_i", [P, EC + 1], I32)
            s.pos = eb("pos", [P, EC + 1])
            s.rowl = eb("rowl", [P, EC + 1], BF16)
            s.mean = eb("mean", [P, NT])
            s.rstd = eb("rstd", [P, NT])
            prepare(nc, s, a)
            nodes(nc, s, a)
        edges(nc, s, a)
        gru(nc, s, a)
        routing(nc, s, a)
        experts(nc, s, a)
        combine(nc, s, a)


_NAMES = {"x": "x", "src": "src", "dst": "dst", "edge_attr_64": "edge_attr", "L0_gnn_W1": "W1", "L0_gnn_b1": "b1",
          "L0_gnn_W2": "W2", "L0_gnn_b2": "b2", "L0_gnn_W_ih": "W_ih", "L0_gnn_b_ih": "b_ih",
          "L0_gnn_W_hh": "W_hh", "L0_gnn_b_hh": "b_hh", "L0_mix_Wqkv": "Wqkv", "L0_mix_Wout": "Wout",
          "L0_mix_gamma": "gamma", "L0_ffn_gate_w": "gate_w", "L0_ffn_gate_b": "gate_b", "L0_ffn_w1": "fw1",
          "L0_ffn_b1": "fb1", "L0_ffn_w2": "fw2", "L0_ffn_b2": "fb2"}


def kernel(**inputs):
    import numpy as _np
    import concourse.bacc as _bacc
    from concourse import mybir as _mybir
    from concourse.bass_utils import run_bass_kernel_spmd as _run

    nc = _bacc.Bacc("TRN2", target_bir_lowering=False, num_devices=1)
    arrays, args = {}, {}
    for name, short in _NAMES.items():
        arr = _np.ascontiguousarray(inputs[name])
        arrays[f"in_{name}"] = arr
        args[short] = nc.dram_tensor(f"in_{name}", arr.shape, _mybir.dt.from_np(arr.dtype), kind="ExternalInput").ap()
    args["out"] = nc.dram_tensor("out_dram", (N, H), F32, kind="ExternalOutput").ap()
    build(nc, Arrays(**args))
    r = _run(nc, [arrays], core_ids=[0])
    return r.results[0]["out_dram"]
```

```python
from contextlib import ExitStack

import concourse.bass as bass
import concourse.mybir as mybir
from concourse.alu_op_type import AluOpType as ALU

F32, F32R, BF16, I32, U16 = (mybir.dt.float32, mybir.dt.float32r, mybir.dt.bfloat16, mybir.dt.int32,
                              mybir.dt.uint16)
ACT = mybir.ActivationFunctionType
AX = mybir.AxisListType
OFF = bass.IndirectOffsetOnAxis
ds = bass.ds

P = 128
N, H, E, ED = 6250, 256, 106250, 64
H3 = 3 * H
HEADS, DH = 8, 32
NX, FF = 8, 1024
EPS = 1e-5
REAL = -(-N // P)
NT = REAL + REAL % 2
NTX = NT + 2
TAIL = N - (REAL - 1) * P
NB = REAL
EC = E // P
EREM = E - EC * P
UNROLL = 8
STEP = 10
NS = EC // STEP
PAIR = 2 * P
RING = 8
SPREAD = 3
LATE = NT // 2 // SPREAD
MID = NS // 2 - 1 - NT // 2 - LATE
NG = -(-((E + NB * (PAIR - 1)) // PAIR) // RING) * RING
SLOTS = NG * PAIR
PR = 8
EW = ED + 2
SW = H + 1
CAP = -(-(5 * N) // (4 * NX))
CT = -(-CAP // P)
CLAST = CAP - (CT - 1) * P
XW = H + 1
ZERO_DMAS = NX * CAP // (8 * P) + (NX * CAP % (8 * P) >= P) + (NX * CAP % P > 0)
FMAX = 3.4028235e38
assert NS * STEP == EC and SLOTS % (P * PR) == 0
assert NS % 2 == 1 and 0 < LATE * SPREAD < NT // 2 and 0 < MID * SPREAD <= NT // 2


class Shared:
    pass


class Arrays:

    def __init__(self, x, src, dst, edge_attr, W1, b1, W2, b2, W_ih, b_ih, W_hh, b_hh, Wqkv, Wout, gamma,
                 gate_w, gate_b, fw1, fb1, fw2, fb2, out):
        self.x, self.src, self.dst, self.edge_attr = x, src, dst, edge_attr
        self.W1, self.b1, self.W2, self.b2 = W1, b1, W2, b2
        self.W_ih, self.b_ih, self.W_hh, self.b_hh = W_ih, b_ih, W_hh, b_hh
        self.Wqkv, self.Wout, self.gamma = Wqkv, Wout, gamma
        self.gate_w, self.gate_b, self.fw1, self.fb1, self.fw2, self.fb2 = gate_w, gate_b, fw1, fb1, fw2, fb2
        self.out = out


class Chain:

    def __init__(self, eng, sem, n=0):
        self.eng, self.sem, self.n = eng, sem, n

    def then(self, ins):
        ins.then_inc(self.sem, 1)
        self.n = self.n + 1
        self.eng.wait_ge(self.sem, self.n)

    def mark(self, ins):
        ins.then_inc(self.sem, 1)
        self.n = self.n + 1

    def all_but(self, last):
        self.eng.wait_ge(self.sem, self.n - last)


def apart(s, eng):
    eng.sem_inc(s.carried, 1)


def credit(s, eng, sem, n):
    k = s.credits
    s.credits += 1
    eng.dma_start(s.credit_d[k:k + 1, :], s.zerob[0:1, :]).then_inc(sem, n)


def batch_norm_factors(v, ch, st, mean, var, tmp):
    me, qe, mo, qo = st[:, :, 1], st[:, :, 2], st[:, :, 4], st[:, :, 5]
    ch.then(v.tensor_tensor(mean, me, mo, ALU.add))
    ch.then(v.tensor_tensor(tmp, me, mo, ALU.subtract))
    ch.then(v.tensor_scalar(mean, mean, 0.5, None, ALU.mult))
    ch.then(v.tensor_tensor(tmp, tmp, tmp, ALU.mult))
    ch.then(v.tensor_tensor(var, qe, qo, ALU.add))
    ch.then(v.tensor_scalar(tmp, tmp, 0.25, EPS, ALU.mult, ALU.add))
    ch.then(v.tensor_scalar(var, var, 1.0 / H, None, ALU.mult))
    ch.then(v.tensor_tensor(var, var, tmp, ALU.add))


def prepare(nc, s, a):
    with ExitStack() as ctx:
        def sb(name, shape, dt=F32):
            return ctx.enter_context(nc.sbuf_tensor(name, shape, dt))

        sem = s.sem
        raw1 = s.big_s[:, 0:1152].rearrange("p (c f) -> p c f", c=2)
        raw_hh = s.big_s[:, 1152:2688].rearrange("p (c f) -> p c f", c=6)
        raw_ih = s.big_s[:, 2688:4224].rearrange("p (c f) -> p c f", c=6)
        raw2 = s.big_s[:, 4224:4736].rearrange("p (c f) -> p c f", c=2)
        raw1c = s.big_s[:, 4736:4992].rearrange("p (c f) -> p c f", c=2)
        prefill = s.big_s[:, 4992:4992 + PR * EW].rearrange("p (r w) -> p r w", w=EW)
        zrow = s.big_s[:, 5600:5856]
        wihT = sb("wihT", [P, 2, H3])
        b2col = sb("b2col", [P, 2])
        src_i = sb("src_i", [P, EC + 1], I32)
        tmp_i = sb("tmp_i", [P, EC + 1], I32)
        bkt = sb("bkt", [P, EC + 1], BF16)
        eqm = sb("eqm", [P, 2, EC + 1], BF16)
        ranks = sb("ranks", [P, 2, EC + 1])
        onesb = sb("onesb", [P, EC + 1], BF16)
        cnt = sb("cnt", [P, NB])
        pairs_i = sb("pairs_i", [P, NB], I32)
        pairs = sb("pairs", [P, NB])
        incl = sb("incl", [P, NB])
        carry = sb("carry", [P, NB])
        inclT = sb("inclT", [NB, 1])
        iota_g = sb("iota_g", [P, NG])

        masks, edges_in, filler = sem("masks_made"), sem("edges_in"), sem("filler_made")
        w_in, pad_out = sem("weights_in"), s.pad_out
        tr, ev = sem("weights_transposed"), sem("weights_evacuated")
        fold, folded = sem("fold_products"), sem("fold_evacuated")
        counted, sums, incl_ok, inclT_mm = sem("counted"), sem("sums"), sem("incl_made"), sem("inclT_mm")
        inclT_ok, ind_ok, blk_mm = sem("inclT_made"), sem("ind_made"), sem("blk_mm")

        jobs = []
        for c in range(2):
            k = slice(c * P, (c + 1) * P)
            jobs.append((s.fused_w[:, c, 0:H], [raw1[:, m, k] for m in range(2)]))
            jobs.append((s.fused_w[:, c, 2 * H:3 * H], [raw1[:, m, H + c * P:H + (c + 1) * P] for m in range(2)]))
            for raw, wt in ((raw_hh, s.whhT), (raw_ih, wihT)):
                jobs.append((wt[:, c, 0:512], [raw[:, m, k] for m in range(4)]))
                jobs.append((wt[:, c, 512:H3], [raw[:, m, k] for m in range(4, 6)]))
        jobs.append((s.w1c[:, :], [raw1c[:, m, :] for m in range(2)]))
        folds = [(s.wg[:, jc, lo:hi], [(raw2[:, oc, jc * P:(jc + 1) * P], wihT[:, oc, lo:hi]) for oc in range(2)])
                 for jc in range(2) for lo, hi in ((0, 512), (512, H3))]
        folds += [(s.bg[0:1, lo:hi], [(b2col[:, oc:oc + 1], wihT[:, oc, lo:hi]) for oc in range(2)])
                  for lo, hi in ((0, 512), (512, H3))]

        with nc.Block() as block:
            @block.gpsimd
            def _(g):
                ch = Chain(g, s.p_step)
                g.memset(src_i[:, EC:EC + 1], NB * P)
                g.memset(s.dst_i[:, EC:EC + 1], 0).then_inc(masks, 1)
                g.memset(s.zerob[:, :], 0.0)
                ch.then(g.memset(prefill, 0.0))
                ch.then(g.memset(prefill[:, :, EW - 1:EW], -1.0))
                g.memset(zrow, 0.0).then_inc(filler, 1)
                ch.then(g.memset(s.ident[:, :], 0.0))
                ch.then(g.affine_select(out=s.ident[:, :], in_=s.ident[:, :], compare_op=ALU.not_equal, fill=1.0,
                                        base=0, pattern=[[-1, P]], channel_multiplier=1))
                ch.then(g.memset(s.ones[:, :], 1.0))
                g.affine_select(out=s.upper[:, :], in_=s.ones[:, :], compare_op=ALU.is_gt, fill=0.0,
                                base=0, pattern=[[1, P]], channel_multiplier=-1)
                g.memset(onesb[:, :], 1.0)
                g.iota(s.iota_f[:, :], pattern=[[1, P]], base=0, channel_multiplier=0,
                       allow_small_or_imprecise_dtypes=True)
                g.iota(s.node_f[:, :], pattern=[[P, NT]], base=0, channel_multiplier=1,
                       allow_small_or_imprecise_dtypes=True)
                g.iota(iota_g[:, :], pattern=[[1, NG]], base=0, channel_multiplier=0,
                       allow_small_or_imprecise_dtypes=True).then_inc(masks, 1)
                s.p_steps = ch.n

            @block.sync
            def _(sp):
                sp.dma_start(src_i[:, 0:EC], a.src[0:EC * P].rearrange("(p c) -> p c", p=P)).then_inc(edges_in, 16)
                sp.dma_start(s.dst_i[:, 0:EC], a.dst[0:EC * P].rearrange("(p c) -> p c", p=P)).then_inc(edges_in, 16)
                sp.wait_ge(masks, 1)
                for to, of in ((src_i, a.src), (s.dst_i, a.dst)):
                    sp.dma_start(to[0:EREM, EC:EC + 1],
                                 of[EC * P:E].rearrange("(p c) -> p c", c=1)).then_inc(edges_in, 16)
                sp.dma_start(raw1, a.W1.rearrange("(c p) f -> p c f", p=P)).then_inc(w_in, 16)
                for k in range(2):
                    sp.dma_start(raw1c[:, :, k * ED:(k + 1) * ED],
                                 a.W1[:, 2 * H:2 * H + ED].rearrange("(c p) f -> p c f", p=P)).then_inc(w_in, 16)
                sp.dma_start(raw_hh, a.W_hh.rearrange("(c p) f -> p c f", p=P)).then_inc(w_in, 16)
                sp.dma_start(raw_ih, a.W_ih.rearrange("(c p) f -> p c f", p=P)).then_inc(w_in, 16)
                sp.dma_start(raw2, a.W2.rearrange("(c p) f -> p c f", p=P)).then_inc(w_in, 16)
                sp.dma_start(b2col[:, :], a.b2.rearrange("(c p) -> p c", p=P), allow_slow_non_contiguous=True).then_inc(w_in, 16)
                sp.dma_start(s.bg[1:2, :], a.b_ih.rearrange("(a f) -> a f", a=1)).then_inc(w_in, 16)
                qkv = a.Wqkv.rearrange("(c p) f -> p c f", p=P)
                sp.dma_start(s.fused_w[:, :, H:2 * H], qkv[:, :, 0:H]).then_inc(w_in, 16)
                sp.dma_start(s.wk[:, :, :], qkv[:, :, H:2 * H]).then_inc(w_in, 16)
                sp.dma_start(s.fused_w[:, :, 3 * H:4 * H], qkv[:, :, 2 * H:3 * H]).then_inc(w_in, 16)
                sp.dma_start(s.wout[:, :, :], a.Wout.rearrange("(c p) f -> p c f", p=P)).then_inc(w_in, 16)
                for to, of in ((s.b1b, a.b1), (s.bhhb, a.b_hh), (s.gammab, a.gamma), (s.gateb, a.gate_b)):
                    sp.dma_start(to[:, :], of.partition_broadcast(P)).then_inc(w_in, 16)
                sp.dma_start(s.gatew[:, :, :], a.gate_w.rearrange("(c p) e -> p c e", p=P)).then_inc(w_in, 16)
                x_rows = s.x_pad.rearrange("t p f -> (t p) f")
                sp.dma_start(x_rows[0:N, :], a.x).then_inc(pad_out, 16)
                sp.wait_ge(filler, 1)
                sp.dma_start(x_rows[N:REAL * P, :], zrow[0:REAL * P - N, :]).then_inc(pad_out, 16)
                for t in range(REAL, NTX):
                    sp.dma_start(s.x_pad[t], zrow).then_inc(pad_out, 16)
                sorted_v = s.sorted_d.rearrange("(k p r) w -> k p r w", p=P, r=PR)
                fills = SLOTS // (P * PR)
                with sp.Fori(0, fills) as k:
                    sp.dma_start(sorted_v[ds(k, 1)].rearrange("k p r w -> p (k r) w"), prefill).then_inc(pad_out, 16)
                s.pads = 2 + NTX - REAL + fills
                sp.wait_ge(pad_out, 16 * s.pads)
                sp.dma_start(s.x1_all.rearrange("p (t f) -> p t f", f=H),
                             s.x_pad[0:NT].rearrange("t p f -> p t f")).then_inc(s.x_in, 16)

            @block.tensor
            def _(pe):
                pe.wait_ge(w_in, 16 * 17)
                pe.wait_ge(masks, 2)
                for q, (to, ins) in enumerate(jobs):
                    if q >= 4:
                        pe.wait_ge(ev, q - 3)
                    for m, i in enumerate(ins):
                        last = nc.tensor.transpose(s.bank[q % 4][:, m * P:(m + 1) * P], i, s.ident[:, :])
                    last.then_inc(tr, 1)
                pe.wait_ge(ev, len(jobs))
                for q, (to, terms) in enumerate(folds):
                    if q >= 4:
                        pe.wait_ge(folded, q - 3)
                    rows, cols = to.shape
                    for n, (left, right) in enumerate(terms):
                        last = nc.tensor.matmul(s.bank[q % 4][0:rows, 0:cols], left, right,
                                                start=n == 0, stop=n == len(terms) - 1)
                    last.then_inc(fold, 1)
                pe.wait_ge(counted, 1)
                nc.tensor.matmul(s.bank[4][:, 0:NB], s.ones[:, :], cnt[:, :], start=True, stop=True)
                nc.tensor.matmul(s.bank[5][:, 0:NB], s.upper[:, :], cnt[:, :], start=True,
                                 stop=True).then_inc(sums, 1)
                pe.wait_ge(incl_ok, 1)
                nc.tensor.matmul(s.bank[4][0:NB, 0:1], incl[0:1, :], s.ones[0:1, 0:1], start=True,
                                 stop=True).then_inc(inclT_mm, 1)
                pe.wait_ge(ind_ok, 1)
                nc.tensor.matmul(s.bank[4][0:1, 0:NG], s.ones[0:NB, 0:1], iota_g[0:NB, :], start=True,
                                 stop=True).then_inc(blk_mm, 1)

            @block.scalar
            def _(act):
                for q, (to, ins) in enumerate(jobs):
                    act.wait_ge(tr, q + 1)
                    nc.scalar.copy(to, s.bank[q % 4][:, 0:P * len(ins)]).then_inc(ev, 1)
                for q, (to, terms) in enumerate(folds):
                    act.wait_ge(fold, q + 1)
                    rows, cols = to.shape
                    nc.scalar.copy(to, s.bank[q % 4][0:rows, 0:cols]).then_inc(folded, 1)

            @block.vector
            def _(v):
                ch = Chain(v, s.v_step, s.v_steps)
                v.wait_ge(edges_in, 64)
                v.wait_ge(masks, 2)
                ch.then(v.tensor_scalar(tmp_i[:, :], src_i[:, :], 7, None, ALU.arith_shift_right))
                ch.then(v.tensor_copy(bkt[:, :], tmp_i[:, :]))
                ch.then(v.tensor_scalar(tmp_i[:, :], src_i[:, :], P - 1, None, ALU.bitwise_and))
                ch.then(v.tensor_copy(s.rowl[:, :], tmp_i[:, :]))

                def count(b, k):
                    ch.all_but(1)
                    ch.mark(v.tensor_scalar(eqm[:, k, :], bkt[:, :], s.iota_f[:, ds(b, 1)], 0.0, ALU.is_equal, ALU.add,
                                            accum_out=cnt[:, ds(b, 1)]))

                base = ch.n
                with v.Fori(0, NB // UNROLL) as i:
                    for k in range(UNROLL):
                        ch.n = base + i * UNROLL + k
                        count(i * UNROLL + k, k % 2)
                ch.n = base + NB // UNROLL * UNROLL
                for b in range(NB // UNROLL * UNROLL, NB):
                    count(b, b % 2)
                ch.all_but(0)
                v.tensor_copy(pairs[:, :], cnt[:, :]).then_inc(counted, 1)
                v.wait_ge(sums, 1)
                ch.then(v.tensor_scalar(pairs_i[:, :], s.bank[4][:, 0:NB], float(PAIR - 1), None, ALU.add))
                ch.then(v.tensor_scalar(pairs_i[:, :], pairs_i[:, :], PAIR.bit_length() - 1, None, ALU.arith_shift_right))
                ch.then(v.tensor_copy(pairs[:, :], pairs_i[:, :]))
                ch.then(v.tensor_tensor_scan(incl[:, :], s.ones[:, 0:NB], pairs[:, :], 0.0, ALU.mult, ALU.add))
                v.tensor_tensor(carry[:, :], incl[:, :], pairs[:, :], ALU.subtract).then_inc(incl_ok, 1)
                v.wait_ge(incl_ok, 1)
                ch.then(v.tensor_scalar(carry[:, :], carry[:, :], float(PAIR), -1.0, ALU.mult, ALU.add))
                ch.then(v.tensor_tensor(carry[:, :], carry[:, :], s.bank[5][:, 0:NB], ALU.add))
                v.wait_ge(inclT_mm, 1)
                ch.then(v.tensor_copy(inclT[:, :], s.bank[4][0:NB, 0:1]))
                v.tensor_scalar(iota_g[0:NB, :], iota_g[0:NB, :], inclT[:, 0:1], None, ALU.is_ge).then_inc(ind_ok, 1)
                v.wait_ge(blk_mm, 1)
                ch.then(v.tensor_scalar(s.blk_i[0:1, :], s.bank[4][0:1, 0:NG], float(NB - 1), None, ALU.min))

                def mask(b, k):
                    ch.mark(v.tensor_scalar(eqm[:, k, :], bkt[:, :], s.iota_f[:, ds(b, 1)], None, ALU.is_equal))

                def place(b, k):
                    ch.all_but(1)
                    ch.mark(v.tensor_tensor_scan(ranks[:, k, :], onesb[:, :], eqm[:, k, :], carry[:, ds(b, 1)],
                                                 ALU.mult, ALU.add))
                    ch.all_but(1)
                    mask(b + 1, 1 - k)
                    ch.all_but(1)
                    apart(s, v)
                    ch.mark(v.copy_predicated(s.pos[:, :], eqm[:, k, :].bitcast(U16), ranks[:, k, :]))

                ch.mark(v.memset(s.pos[:, :], 0.0))
                mask(0, 0)
                ch.all_but(0)
                base = ch.n
                with v.Fori(0, NB // UNROLL) as i:
                    for k in range(UNROLL):
                        ch.n = base + (i * UNROLL + k) * 3
                        place(i * UNROLL + k, k % 2)
                ch.n = base + NB // UNROLL * UNROLL * 3
                for b in range(NB // UNROLL * UNROLL, NB):
                    place(b, b % 2)
                ch.all_but(0)
                s.v_steps = ch.n


def nodes(nc, s, a):
    with ExitStack() as ctx:
        def sb(name, shape, dt=F32):
            return ctx.enter_context(nc.sbuf_tensor(name, shape, dt))

        sem = s.sem

        ea = sb("ea", [P, 2, STEP, EW])
        slot_i = sb("slot_i", [P, 2, STEP], I32)
        rem = sb("rem", [16, EW])
        rem_i = sb("rem_i", [16, 1], I32)
        xt = sb("xt", [P, 2, H])
        xn = sb("xn", [P, 2, H])
        xnT = sb("xnT", [P, 2, 2, P])
        qt = sb("qt", [P, 2, H])
        vt = sb("vt", [P, 2, H])
        gh = sb("gh", [P, 2, H3])
        pf = sb("pf", [P, H])
        rest = sb("rest", [P, H])
        qe = sb("qe", [P, H])
        qs = sb("qs", [P, 2, H])
        qred = sb("qred", [P, 2, HEADS])
        kmax = sb("kmax", [P, 2])
        et, etok = (x[:, :, :].rearrange("p j (c n) -> p j c n", c=2) for x in (qt, vt))
        v1 = sb("v1", [P, 2, 2, P + 1])
        zero = sb("zero", [P, P + 1])
        blockmask = sb("blockmask", [P, P])
        den = sb("den", [P, 2])
        cx = sb("cx", [P, 2, P])
        cxT = sb("cxT", [P, 2, P])
        mix = sb("mix", [P, 2, H])
        qsT, ot, qsl = xnT, qs, qt
        st = sb("st2", [P, 2, 6])
        mvt = sb("mvt", [P, 2, 2])
        rs = sb("rs", [P, 2])
        kT = s.big_s[:, 0:2 * NT * P].rearrange("p (c n) -> p c n", c=2)

        varred, rooted = sem("var_made"), sem("roots_made")
        ea_in, meta, scattered = sem("ea_in", 2), sem("meta_made"), sem("scattered", 2)
        rem_in, rem_meta, rem_out = sem("rem_in"), sem("rem_meta"), sem("rem_out")
        xt_in, xn_st = sem("xt_in", 2), sem("xn_stored", 2)
        xn_ok, x_tr, xnT_ok = sem("xn_made"), sem("xn_transposed"), sem("xnT_made")
        mm_pq, mm_qv, mm_ga, mm_gb, mm_k = (sem("mm_pq"), sem("mm_qv"), sem("mm_ga"), sem("mm_gb"), sem("mm_k"))
        fr_pq, fr_ga, fr_gb = sem("pq_used"), sem("ga_used"), sem("gb_used")
        q_ok, v_ok, k_ok = sem("q_evacuated"), sem("v_evacuated"), sem("k_evacuated")
        qv_st, gh_st, qs_st = sem("qv_stored", 2), sem("gh_stored", 2), sem("qs_stored", 2)
        gh_ok, qsub, qexp, qs_ok = sem("gh_made"), sem("q_shifted"), sem("q_exp"), sem("qs_made")
        const_ok, kmax_ok = sem("const_made"), sem("kmax_made")
        v_in, et_ok, e_tr, etok_ok, ctx_mm = sem("v_in", 2), sem("e_made"), sem("e_transposed"), sem("etok_made"), sem("context_mm")
        cx_ok, cx_tr, cxT_ok, m_mm, m_ok = sem("cx_made"), sem("cx_transposed"), sem("cxT_made"), sem("m_mm"), sem("m_made")
        qs_in, qs_tr, qsT_ok, o_mm = sem("qs_in", 2), sem("qs_transposed"), sem("qsT_made"), sem("o_mm")
        o_fr, o_var, o_root, ot_ok, ot_st = sem("o_used"), sem("o_var"), sem("o_root"), sem("ot_made"), sem("ot_stored", 2)

        ea_head = a.edge_attr[0:EC * P, :].rearrange("(p c) f -> p c f", p=P)

        def load_edges(sp, h, turn, first=False):
            if not first:
                sp.wait_ge(scattered[h], 16 * STEP * (turn + 1))
            sp.dma_start(ea[:, h, :, 0:ED], ea_head[:, ds((2 * turn + h) * STEP, STEP), :]).then_inc(ea_in[h], 16)

        def make_meta(v, h, turn):
            v.wait_ge(scattered[h], 16 * STEP * (turn + 1))
            cols = ds((2 * turn + h) * STEP, STEP)
            v.tensor_copy(ea[:, h, :, ED:ED + 1].bitcast(I32).rearrange("p a b -> p (a b)"), s.dst_i[:, cols])
            v.tensor_copy(ea[:, h, :, ED + 1:EW].rearrange("p a b -> p (a b)"), s.rowl[:, cols])
            v.tensor_copy(slot_i[:, h, :], s.pos[:, cols]).then_inc(meta, 1)

        def scatter(g, h, turn):
            g.wait_ge(ea_in[h], 16 * turn + 16)
            g.wait_ge(meta, 2 * turn + h + 1)
            apart(s, g)
            for j in range(STEP):
                g.indirect_dma_start(out=s.sorted_d, out_offset=OFF(ap=slot_i[:, h, j:j + 1], axis=0),
                                     in_=ea[:, h, j, :], in_offset=None).then_inc(scattered[h], 16)

        with nc.Block() as block:
            @block.gpsimd
            def _(g):
                for h in range(2):
                    credit(s, g, scattered[h], 16 * STEP)
                ch = Chain(g, s.p_step, s.p_steps)
                g.memset(zero[:, :], 0.0)
                g.memset(v1[:, :, :, P:P + 1], 1.0)
                ch.then(g.memset(blockmask[:, :], 1.0))
                view = blockmask[:, :].rearrange("p (h e) -> p h e", e=DH)
                ch.then(g.affine_select(out=view, in_=view, compare_op=ALU.is_ge, fill=0.0, base=0,
                                        pattern=[[-DH, P // DH], [0, DH]], channel_multiplier=1))
                g.affine_select(out=view, in_=view, compare_op=ALU.is_ge, fill=0.0, base=DH - 1,
                                pattern=[[DH, P // DH], [0, DH]], channel_multiplier=-1).then_inc(const_ok, 1)
                with g.Fori(0, NS // 2) as k:
                    for h in range(2):
                        scatter(g, h, k)
                scatter(g, 0, NS // 2)
                g.wait_ge(rem_in, 16)
                g.wait_ge(rem_meta, 1)
                g.indirect_dma_start(out=s.sorted_d, out_offset=OFF(ap=rem_i[0:EREM, :], axis=0),
                                     in_=rem[0:EREM, :], in_offset=None).then_inc(rem_out, 16)
                g.wait_ge(rem_out, 16)
                for h in range(2):
                    g.wait_ge(scattered[h], 16 * STEP * (NS // 2 + 2 - h))

            @block.sync
            def _(sp):
                for h in range(2):
                    load_edges(sp, h, 0, True)
                for j in range(2):
                    sp.dma_start(xt[:, j, :], s.x_pad[j]).then_inc(xt_in[j], 16)
                    credit(s, sp, xn_st[j], 16)
                    credit(s, sp, qv_st[j], 32)
                    credit(s, sp, gh_st[j], 16)
                    credit(s, sp, qs_st[j], 16)
                    credit(s, sp, ot_st[j], 16)
                sp.dma_start(rem[0:EREM, 0:ED], a.edge_attr[EC * P:E, :]).then_inc(rem_in, 16)
                with sp.Fori(0, NT // 2) as i:
                    for j in range(2):
                        t = 2 * i + j
                        load_edges(sp, j, i + 1)
                        one = ds(t, 1)
                        sp.wait_ge(xn_ok, t + 3)
                        sp.dma_start(s.xn_d[one].rearrange("t p f -> p (t f)"), xn[:, j, :]).then_inc(xn_st[j], 16)
                        sp.dma_start(xt[:, j, :], s.x_pad[ds(t + 2, 1)].rearrange("t p f -> p (t f)")).then_inc(xt_in[j], 16)
                        sp.wait_ge(v_ok, t + 3)
                        sp.dma_start(s.q_tiles[one].rearrange("t p f -> p (t f)"), qt[:, j, :]).then_inc(qv_st[j], 16)
                        sp.dma_start(s.v_d[one].rearrange("t p f -> p (t f)"), vt[:, j, :]).then_inc(qv_st[j], 16)
                        sp.wait_ge(qs_ok, t + 3)
                        sp.dma_start(s.qs_d[one].rearrange("t p f -> p (t f)"), qs[:, j, :]).then_inc(qs_st[j], 16)
                        sp.wait_ge(gh_ok, t + 3)
                        sp.dma_start(s.gh_d[one].rearrange("t p f -> p (t f)"), gh[:, j, :]).then_inc(gh_st[j], 16)
                for j in range(2):
                    sp.wait_ge(qv_st[j], 16 * NT + 32)

                def load_v(i):
                    for j in range(2):
                        t = 2 * i + j
                        sp.wait_ge(ctx_mm, t + 1)
                        sp.dma_start(v1[:, j, :, 0:P],
                                     s.v_d[ds(t, 1)].rearrange("t p (c f) -> p (t c) f", c=2)).then_inc(v_in[j], 16)

                with sp.Fori(0, MID) as k:
                    for m in range(SPREAD):
                        if m < 2:
                            load_edges(sp, m, k + 1 + NT // 2)
                        load_v(SPREAD * k + m)
                for i in range(MID * SPREAD, NT // 2):
                    load_v(i)
                for j in range(2):
                    sp.wait_ge(qs_st[j], 8 * NT + 16)
                    sp.wait_ge(ctx_mm, NT + 2)

                def store_output(t, j):
                    sp.wait_ge(ot_ok, t + 3)
                    sp.dma_start(s.xm_d[ds(t, 1)].rearrange("t p f -> p (t f)"), ot[:, j, :]).then_inc(ot_st[j], 16)

                def load_q(i):
                    for j in range(2):
                        one = ds(2 * i + j, 1)
                        sp.wait_ge(qsT_ok, 2 * i + j + 1)
                        sp.dma_start(qsl[:, j, :], s.qs_d[one].rearrange("t p f -> p (t f)")).then_inc(qs_in[j], 16)

                def load_x(i, first=False):
                    for j in range(2):
                        if not first:
                            store_output(2 * i + j - 2, j)
                        sp.dma_start(xt[:, j, :], s.x_pad[ds(2 * i + j, 1)].rearrange("t p f -> p (t f)")).then_inc(xt_in[j], 16)

                def load_turn(k, first):
                    for m in range(SPREAD):
                        if m < 2:
                            load_edges(sp, m, k + 1 + NT // 2 + MID)
                        load_q(SPREAD * k + m + 1)
                        load_x(SPREAD * k + m, first and m == 0)

                load_q(0)
                load_turn(0, True)
                with sp.Fori(1, LATE) as k:
                    load_turn(k, False)
                load_edges(sp, 0, NS // 2)
                for i in range(LATE * SPREAD, NT // 2 - 1):
                    load_q(i + 1)
                    load_x(i)
                load_x(NT // 2 - 1)
                for j in range(2):
                    store_output(NT - 2 + j, j)
                for j in range(2):
                    sp.wait_ge(ot_st[j], 8 * NT + 16)
                for j in range(2):
                    sp.wait_ge(xn_st[j], 8 * NT + 16)
                    sp.wait_ge(gh_st[j], 8 * NT + 16)

            @block.tensor
            def _(pe):
                pe.sem_inc(x_tr, 2)
                pe.sem_inc(mm_k, 2)
                with pe.Fori(0, NT // 2) as i:
                    for j in range(2):
                        t = 2 * i + j
                        pe.wait_ge(xn_ok, t + 3)
                        pe.wait_ge(xnT_ok, t + 1)
                        for c in range(2):
                            last = nc.tensor.transpose(s.bank[j][:, c * P:(c + 1) * P],
                                                       xn[:, j, c * P:(c + 1) * P], s.ident[:, :])
                        last.then_inc(x_tr, 1)
                    for j in range(2):
                        t = 2 * i + j
                        pe.wait_ge(xnT_ok, t + 3)

                        def product(bank, right, free, value, signal):
                            pe.wait_ge(free, value)
                            for c in range(2):
                                last = nc.tensor.matmul(s.bank[bank][:, 0:right.shape[2]], xnT[:, j, c, :],
                                                        right[:, c, :], start=c == 0, stop=c == 1)
                            last.then_inc(signal, 1)

                        product(2, s.fused_w[:, :, 0:512], fr_pq, t + 1, mm_pq)
                        product(3, s.fused_w[:, :, 512:1024], v_ok, t + 2, mm_qv)
                        product(4, s.whhT[:, :, 0:512], fr_ga, t + 1, mm_ga)
                        product(5, s.whhT[:, :, 512:H3], fr_gb, t + 1, mm_gb)
                        pe.wait_ge(k_ok, t + 1)
                        for m in range(2):
                            for c in range(2):
                                last = nc.tensor.matmul(s.bank[6][:, m * P:(m + 1) * P], s.wk[:, c, m * P:(m + 1) * P],
                                                        xnT[:, j, c, :], start=c == 0, stop=c == 1)
                        last.then_inc(mm_k, 1)
                pe.sem_inc(ctx_mm, 2)
                pe.sem_inc(e_tr, 2)
                pe.wait_ge(const_ok, 1)
                pe.wait_ge(fr_pq, NT + 1)
                pe.wait_ge(v_ok, NT + 2)
                for m in range(2):
                    nc.tensor.matmul(s.bank[2 + m][:, 0:P + 1], zero[:, 0:P], zero[:, :], start=True, stop=True)
                with pe.Fori(0, NT // 2) as i:
                    for j in range(2):
                        t = 2 * i + j
                        pe.wait_ge(et_ok, t + 3)
                        pe.wait_ge(etok_ok, t + 1)
                        for m in range(2):
                            last = nc.tensor.transpose(s.bank[j][:, m * P:(m + 1) * P], et[:, j, m, :], s.ident[:, :])
                        last.then_inc(e_tr, 1)
                    for j in range(2):
                        t = 2 * i + j
                        pe.wait_ge(etok_ok, t + 3)
                        pe.wait_ge(v_in[j], 16 * i + 16)
                        for m in range(2):
                            last = nc.tensor.matmul(s.bank[2 + m][:, 0:P + 1], etok[:, j, m, :], v1[:, j, m, :],
                                                    start=False, stop=True, skip_group_check=True)
                        last.then_inc(ctx_mm, 1)
                pe.wait_ge(cx_ok, 1)
                for m in range(2):
                    last = nc.tensor.transpose(s.bank[4][:, m * P:(m + 1) * P], cx[:, m, :], s.ident[:, :])
                last.then_inc(cx_tr, 1)
                pe.wait_ge(cxT_ok, 1)
                for m in range(2):
                    last = nc.tensor.matmul(s.bank[5][:, m * H:(m + 1) * H], cxT[:, m, :], s.wout[:, m, :],
                                            start=True, stop=True)
                last.then_inc(m_mm, 1)
                pe.wait_ge(m_ok, 1)
                pe.sem_inc(qs_tr, 2)
                pe.sem_inc(o_mm, 2)
                with pe.Fori(0, NT // 2) as i:
                    for j in range(2):
                        t = 2 * i + j
                        pe.wait_ge(qs_in[j], 16 * i + 16)
                        pe.wait_ge(qsT_ok, t + 1)
                        for m in range(2):
                            last = nc.tensor.transpose(s.bank[j][:, m * P:(m + 1) * P], qsl[:, j, m * P:(m + 1) * P],
                                                       s.ident[:, :])
                        last.then_inc(qs_tr, 1)
                    for j in range(2):
                        t = 2 * i + j
                        pe.wait_ge(qsT_ok, t + 3)
                        pe.wait_ge(o_fr, t + 1)
                        for m in range(2):
                            last = nc.tensor.matmul(s.bank[6 + j][:, 0:H], qsT[:, j, m, :], mix[:, m, :],
                                                    start=m == 0, stop=m == 1)
                        last.then_inc(o_mm, 1)

            @block.scalar
            def _(act):
                act.wait_ge(varred, 1)
                nc.scalar.activation(s.rstd[:, :], pf[:, 0:NT], ACT.Sqrt).then_inc(rooted, 1)
                act.sem_inc(xnT_ok, 2)
                act.sem_inc(q_ok, 2)
                act.sem_inc(v_ok, 2)
                act.sem_inc(k_ok, 1)
                act.sem_inc(qexp, 1)
                with act.Fori(0, NT // 2) as i:
                    for j in range(2):
                        t = 2 * i + j
                        act.wait_ge(x_tr, t + 3)
                        act.wait_ge(mm_k, t + 1)
                        nc.scalar.copy(xnT[:, j, :, :], s.bank[j][:, 0:H].rearrange("p (c n) -> p c n", c=2)).then_inc(xnT_ok, 1)
                    for j in range(2):
                        t = 2 * i + j
                        act.wait_ge(mm_qv, t + 1)
                        act.wait_ge(qv_st[j], 32 * i + 32)
                        nc.scalar.copy(qt[:, j, :], s.bank[3][:, 0:H]).then_inc(q_ok, 1)
                        act.wait_ge(q_ok, t + 3)
                        nc.scalar.copy(vt[:, j, :], s.bank[3][:, H:2 * H]).then_inc(v_ok, 1)
                        act.wait_ge(qsub, t + 1)
                        nc.scalar.activation(qe[:, :], qe[:, :], ACT.Exp).then_inc(qexp, 1)
                        act.wait_ge(mm_k, t + 3)
                        nc.scalar.copy(kT[:, :, ds(t * P, P)], s.bank[6][:, 0:H].rearrange("p (c n) -> p c n", c=2)).then_inc(k_ok, 1)
                act.sem_inc(et_ok, 2)
                act.sem_inc(etok_ok, 2)
                act.wait_ge(kmax_ok, 1)
                for j in range(2):
                    act.wait_ge(qv_st[j], 16 * NT + 32)
                with act.Fori(0, NT // 2) as i:
                    for j in range(2):
                        t = 2 * i + j
                        act.wait_ge(e_tr, t + 1)
                        for m in range(2):
                            last = nc.scalar.activation(et[:, j, m, :], kT[:, m, ds(t * P, P)], ACT.Exp, bias=kmax[:, m:m + 1])
                        last.then_inc(et_ok, 1)
                    for j in range(2):
                        t = 2 * i + j
                        act.wait_ge(e_tr, t + 3)
                        act.wait_ge(ctx_mm, t + 1)
                        nc.scalar.copy(etok[:, j, :, :], s.bank[j][:, 0:H].rearrange("p (c n) -> p c n", c=2)).then_inc(etok_ok, 1)
                act.wait_ge(cx_tr, 1)
                nc.scalar.copy(cxT[:, :, :], s.bank[4][:, 0:H].rearrange("p (c n) -> p c n", c=2)).then_inc(cxT_ok, 1)
                act.wait_ge(m_mm, 1)
                nc.scalar.copy(mix[:, :, :], s.bank[5][:, :].rearrange("p (c n) -> p c n", c=2)).then_inc(m_ok, 1)
                act.sem_inc(qsT_ok, 2)
                with act.Fori(0, NT // 2) as i:
                    for j in range(2):
                        t = 2 * i + j
                        act.wait_ge(qs_tr, t + 3)
                        act.wait_ge(o_mm, t + 1)
                        nc.scalar.copy(qsT[:, j, :, :], s.bank[j][:, 0:H].rearrange("p (c n) -> p c n", c=2)).then_inc(qsT_ok, 1)
                    act.wait_ge(o_var, i + 1)
                    nc.scalar.activation(rs[:, :], rs[:, :], ACT.Sqrt).then_inc(o_root, 1)

            @block.vector
            def _(v):
                ch = Chain(v, s.v_step, s.v_steps)
                v.tensor_copy(rem[0:EREM, ED:ED + 1].bitcast(I32), s.dst_i[0:EREM, EC:EC + 1])
                v.tensor_copy(rem[0:EREM, ED + 1:EW], s.rowl[0:EREM, EC:EC + 1])
                v.tensor_copy(rem_i[0:EREM, :], s.pos[0:EREM, EC:EC + 1]).then_inc(rem_meta, 1)
                for h in range(2):
                    make_meta(v, h, 0)
                v.wait_ge(s.x_in, 16)
                base = ch.n
                with v.Fori(0, NT // 10) as i:
                    for k in range(10):
                        t = 10 * i + k
                        ch.mark(v.bn_stats(s.st2[:, ds(t, 1), :].rearrange("p a b -> p (a b)"), s.x1_all[:, ds(t * H, H)]))
                ch.n = base + NT
                ch.all_but(0)
                var, tmp = pf[:, 0:NT], rest[:, 0:NT]
                batch_norm_factors(v, ch, s.st2, s.mean[:, :], var, tmp)
                v.tensor_copy(tmp, var).then_inc(varred, 1)
                v.wait_ge(rooted, 1)
                ch.then(v.reciprocal(s.rstd[:, :], s.rstd[:, :]))
                v.sem_inc(xn_ok, 2)
                for k in (fr_pq, fr_ga, fr_gb):
                    v.sem_inc(k, 1)
                v.sem_inc(gh_ok, 2)
                v.sem_inc(qs_ok, 2)
                base = ch.n
                with v.Fori(0, NT // 2) as i:
                    for j in range(2):
                        t = 2 * i + j
                        v.wait_ge(xt_in[j], 16 * i + 16)
                        v.wait_ge(x_tr, t + 1)
                        v.wait_ge(xn_st[j], 16 * i + 16)
                        v.tensor_scalar(xn[:, j, :], xt[:, j, :], s.mean[:, ds(t, 1)], s.rstd[:, ds(t, 1)],
                                        ALU.subtract, ALU.mult).then_inc(xn_ok, 1)
                    for j in range(2):
                        t = 2 * i + j
                        make_meta(v, j, i + 1)
                        ch.n = base + t * 8
                        o = t * 2 * H
                        v.wait_ge(mm_pq, t + 1)
                        ch.then(v.tensor_tensor(pf[:, :], s.bank[2][:, 0:H], s.b1b[:, :], ALU.add))
                        q_ps = s.bank[2][:, H:2 * H].rearrange("p (h e) -> p h e", e=DH)
                        ch.then(v.tensor_reduce(qred[:, 0, :], q_ps, AX.X, ALU.max))
                        v.wait_ge(qs_ok, t + 2)
                        v.tensor_tensor(qe[:, :].rearrange("p (h e) -> p h e", e=DH), q_ps,
                                        qred[:, 0, :].unsqueeze(2).to_broadcast([P, HEADS, DH]), ALU.subtract).then_inc(qsub, 1)
                        v.wait_ge(qsub, t + 1)
                        v.sem_inc(fr_pq, 1)
                        ch.then(v.tensor_copy(s.big_p[:, ds(o, H)], pf[:, :]))
                        ch.then(v.tensor_tensor(rest[:, :], pf[:, :], s.big_p[:, ds(o, H)], ALU.subtract))
                        ch.then(v.tensor_copy(s.big_p[:, ds(o + H, H)], rest[:, :]))
                        v.tensor_tensor(s.p3[:, ds(t * H, H)], rest[:, :], s.big_p[:, ds(o + H, H)], ALU.subtract)
                        v.wait_ge(gh_st[j], 16 * i + 16)
                        v.wait_ge(mm_ga, t + 1)
                        v.tensor_tensor(gh[:, j, 0:512], s.bank[4][:, :], s.bhhb[:, 0:512], ALU.add).then_inc(fr_ga, 1)
                        v.wait_ge(mm_gb, t + 1)
                        v.tensor_tensor(gh[:, j, 512:H3], s.bank[5][:, 0:H], s.bhhb[:, 512:H3], ALU.add).then_inc(fr_gb, 1)
                        v.wait_ge(fr_gb, t + 2)
                        v.sem_inc(gh_ok, 1)
                        v.wait_ge(qexp, t + 2)
                        qe_v = qe[:, :].rearrange("p (h e) -> p h e", e=DH)
                        ch.then(v.tensor_reduce(qred[:, 1, :], qe_v, AX.X, ALU.add))
                        ch.then(v.reciprocal(qred[:, 1, :], qred[:, 1, :]))
                        ch.then(v.tensor_scalar(qred[:, 1, :], qred[:, 1, :], DH ** -0.5, None, ALU.mult))
                        v.wait_ge(qs_st[j], 16 * i + 16)
                        v.tensor_tensor(qs[:, j, :].rearrange("p (h e) -> p h e", e=DH), qe_v,
                                        qred[:, 1, :].unsqueeze(2).to_broadcast([P, HEADS, DH]), ALU.mult).then_inc(qs_ok, 1)
                ch.n = base + NT * 8
                v.wait_ge(k_ok, NT + 1)
                for m in range(2):
                    ch.then(v.tensor_reduce(kmax[:, m:m + 1], kT[:, m, 0:N], AX.X, ALU.max))
                v.memset(kT[:, :, N:NT * P], -1e30)
                v.tensor_scalar(kmax[:, :], kmax[:, :], -1.0, None, ALU.mult).then_inc(kmax_ok, 1)
                with v.Fori(0, MID) as i:
                    for h in range(2):
                        make_meta(v, h, i + 1 + NT // 2)
                v.wait_ge(ctx_mm, NT + 2)
                v.wait_ge(const_ok, 1)
                for m in range(2):
                    ch.then(v.reciprocal(den[:, m:m + 1], s.bank[2 + m][:, P:P + 1]))
                    ch.then(v.tensor_scalar(cx[:, m, :], s.bank[2 + m][:, 0:P], den[:, m:m + 1], None, ALU.mult))
                    last = v.tensor_tensor(cx[:, m, :], cx[:, m, :], blockmask[:, :], ALU.mult)
                last.then_inc(cx_ok, 1)
                for j in range(2):
                    v.wait_ge(qs_st[j], 8 * NT + 16)
                v.sem_inc(o_fr, 2)
                v.sem_inc(ot_ok, 2)
                base = ch.n

                def output(i):
                    ch.n = base + i * 10
                    for j in range(2):
                        v.wait_ge(o_mm, 2 * i + j + 3)
                        ch.mark(v.bn_stats(st[:, j, :], s.bank[6 + j][:, 0:H]))
                    for j in range(2):
                        ch.all_but(1)
                        apart(s, v)
                        ch.mark(v.bn_aggr(mvt[:, j, :], st[:, j, :]))
                    ch.all_but(0)
                    ch.mark(v.tensor_scalar(rs[:, :], mvt[:, :, 1:2].rearrange("p a b -> p (a b)"), EPS, None, ALU.add))
                    ch.all_but(0)
                    v.sem_inc(o_var, 1)
                    for j in range(2):
                        v.wait_ge(ot_st[j], 16 * i + 16)
                        ch.mark(v.scalar_tensor_tensor(out=ot[:, j, :], in0=s.bank[6 + j][:, 0:H], scalar=mvt[:, j, 0:1],
                                                       in1=s.gammab[:, :], op0=ALU.subtract, op1=ALU.mult))
                    ch.all_but(0)
                    v.sem_inc(o_fr, 2)
                    v.wait_ge(o_root, i + 1)
                    ch.mark(v.reciprocal(rs[:, :], rs[:, :]))
                    ch.all_but(0)
                    for j in range(2):
                        v.wait_ge(xt_in[j], 16 * (NT // 2 + 1) + 16 * i + 16)
                        ch.mark(v.scalar_tensor_tensor(out=ot[:, j, :], in0=ot[:, j, :], scalar=rs[:, j:j + 1],
                                                       in1=xt[:, j, :], op0=ALU.mult, op1=ALU.add))
                    ch.all_but(0)
                    v.sem_inc(ot_ok, 2)

                with v.Fori(0, LATE) as k:
                    for m in range(SPREAD):
                        if m < 2:
                            make_meta(v, m, k + 1 + NT // 2 + MID)
                        output(SPREAD * k + m)
                make_meta(v, 0, NS // 2)
                for i in range(LATE * SPREAD, NT // 2):
                    output(i)
                ch.n = base + (NT // 2) * 10
                s.v_steps = ch.n


def edges(nc, s, a):
    with ExitStack() as ctx:
        def sb(name, shape, dt=F32):
            return ctx.enter_context(nc.sbuf_tensor(name, shape, dt))

        sem = s.sem

        LOAD = RING // 2
        eb = sb("eb", [P, 2, LOAD, 2, EW])
        qg = sb("qg", [P, 4, 2, H])
        onehots = sb("onehots", [P, RING, 2, P], F32R)
        ident_r = sb("ident_r", [P, P], F32R)
        eaT = sb("eaT", [P, 4, 2 * P], F32R)
        w1c_high = sb("w1c_high", [P, H], F32R)
        w1c_low = sb("w1c_low", [P, H], F32R)
        ohT = sb("ohT", [P, 4, 2, P], BF16)
        hq = sb("hq", [P, 4, 2, H])
        r_high = sb("r_high", [P, 4, SW + 1], F32R)
        r_low = sb("r_low", [P, 4, H], F32R)
        r_full = sb("r_full", [P, 4, SW])
        edge_one = sb("edge_one", [P, 2])

        eb_in, gathered = sem("eb_in", 2), sem("gathered", 4)
        oh_ok, t_tr, t_ok, h_mm, h_ok, r_ok, s_mm, s_ok, r_one = (
            sem("onehot_made"), sem("transposed"), sem("transposes_evacuated"), sem("h_mm"), sem("h_summed"),
            sem("relu_made"), sem("s_mm"), sem("s_added"), sem("ones_made"))
        low_ok, rl_ok = sem("low_parts_made"), sem("relu_low_made")

        s.spent = ((t_tr, NG + 8), (t_ok, NG + 2), (low_ok, NG + 4), (rl_ok, NG), (h_mm, NG + 4), (h_ok, NG + 4),
                   (s_mm, NG + 8), (oh_ok, NG + 8))
        TR_BANKS = (0, 1, 4, 5)
        src_v = s.sorted_d.rearrange("(k g p j) w -> k p g (j w)", g=LOAD, p=P, j=2)

        with nc.Block() as block:
            @block.sync
            def _(sp):
                def load(i, c, first):
                    g = RING * i + LOAD * c
                    if not first:
                        for q in range(4):
                            sp.wait_ge(gathered[q], 64 * i + 32 * (c - 1))
                        apart(s, sp)
                        sp.wait_ge(t_tr, g + LOAD)
                        sp.wait_ge(oh_ok, g + LOAD)
                    sp.dma_start(eb[:, c, :, :, :].rearrange("p g j w -> p g (j w)"),
                                 src_v[ds(2 * i + c, 1)].rearrange("k p g w -> p (k g) w")).then_inc(eb_in[c], 16)

                for c in range(2):
                    load(0, c, True)
                with sp.Fori(1, NG // RING) as i:
                    for c in range(2):
                        load(i, c, False)

            @block.gpsimd
            def _(g):
                with g.Fori(0, NG // RING) as i:
                    for n in range(RING):
                        c, q = n // LOAD, n % 4
                        pair = RING * i + n
                        if n % LOAD == 0:
                            g.wait_ge(eb_in[c], 16 * i + 16)
                        g.wait_ge(h_ok, pair + 1)
                        apart(s, g)
                        for j in range(2):
                            g.indirect_dma_start(out=qg[:, q, j, :], out_offset=None, in_=s.q_tab,
                                                 in_offset=OFF(ap=eb[:, c, n % LOAD, j, ED:ED + 1].bitcast(I32), axis=0)
                                                 ).then_inc(gathered[q], 16)

            @block.tensor
            def _(pe):
                pe.sem_inc(t_tr, 8)
                pe.sem_inc(h_mm, 4)
                pe.sem_inc(s_mm, 8)

                def transposes(pair, n):
                    c, bank = n // LOAD % 2, s.bank[TR_BANKS[n % 4]]
                    pe.wait_ge(oh_ok, pair + 9)
                    pe.wait_ge(low_ok, pair + 1)
                    for j in range(2):
                        nc.tensor.transpose(bank[:, (2 + j) * P:(3 + j) * P].bitcast(F32R), onehots[:, n, j, :], ident_r[:, :])
                        last = nc.tensor.transpose(bank[0:ED, j * P:(j + 1) * P], eb[:, c, n % LOAD, j, 0:ED], s.ident[:, :])
                    last.then_inc(t_tr, 1)

                def hidden(pair, n, block_of):
                    q, b = n % 4, n % 2
                    pe.wait_ge(low_ok, pair + 5)
                    pe.wait_ge(h_ok, pair + 3)
                    for j in range(2):
                        into = s.bank[2 + b][:, j * H:(j + 1) * H]
                        both = eaT[:, q, j * P:(j + 1) * P]
                        nc.tensor.matmul(into, both, w1c_high[:, :], start=True, stop=False)
                        nc.tensor.matmul(into, both, w1c_low[:, :], start=False, stop=False)
                        for part in range(2):
                            nc.tensor.matmul(into, ohT[:, q, j, :], s.big_p[:, ds(block_of * 2 * H + part * H, H)],
                                             start=False, stop=False)
                        last = nc.tensor.matmul(into, ohT[:, q, j, :], s.p3[:, ds(block_of * H, H)],
                                                start=False, stop=True)
                    last.then_inc(h_mm, 1)

                def summed(pair, n):
                    b = n % 2
                    pe.wait_ge(rl_ok, pair + 1)
                    pe.wait_ge(s_ok, pair + 1)
                    into = s.bank[6 + b]
                    nc.tensor.matmul(into[:, 0:SW + 1], onehots[:, n, 0, :], r_high[:, n % 4, :], start=True, stop=False)
                    nc.tensor.matmul(into[:, 0:H], onehots[:, n, 0, :], r_low[:, n % 4, :], start=False, stop=False)
                    last = nc.tensor.matmul(into[:, 0:SW], onehots[:, n, 1, :].bitcast(F32), r_full[:, n % 4, :],
                                            start=False, stop=True)
                    last.then_inc(s_mm, 1)

                def turn(i, first, last):
                    _, blk = nc.values_load_multi_w_load_instructions(
                        s.blk_i[0:1, ds(RING * i, RING)], engines=(mybir.EngineType.PE,), min_val=0, max_val=NB - 1,
                        skip_runtime_bounds_check_because="the table is capped at the last block")
                    for n in range(RING):
                        pair = RING * i + n
                        if not (last and n >= RING - 2):
                            transposes(pair + 2, (n + 2) % RING)
                        hidden(pair, n, blk[n])
                        if not (first and n < 2):
                            summed(pair - 2, (n - 2) % RING)

                transposes(0, 0)
                transposes(1, 1)
                turn(0, True, False)
                with pe.Fori(1, NG // RING - 1) as i:
                    turn(i, False, False)
                turn(NG // RING - 1, False, True)
                summed(NG - 2, RING - 2)
                summed(NG - 1, RING - 1)

            @block.scalar
            def _(act):
                act.sem_inc(t_ok, 2)
                act.sem_inc(r_ok, 2)

                def evacuate(pair, n):
                    q, bank = n % 4, s.bank[TR_BANKS[n % 4]]
                    act.wait_ge(t_tr, pair + 9)
                    act.wait_ge(h_mm, pair + 1)
                    nc.scalar.copy(ohT[:, q, :, :], bank[:, 2 * P:4 * P].rearrange("p (j n) -> p j n", j=2))
                    nc.scalar.copy(eaT[0:ED, q, :], bank[0:ED, 0:2 * P]).then_inc(t_ok, 1)

                def relu(pair, n):
                    b = n % 2
                    act.wait_ge(h_ok, pair + 5)
                    act.wait_ge(s_mm, pair + 5)
                    nc.scalar.activation(r_high[:, n % 4, 0:H], hq[:, n % 4, 0, :], ACT.Relu)
                    nc.scalar.activation(r_full[:, n % 4, 0:H], hq[:, n % 4, 1, :], ACT.Relu).then_inc(r_ok, 1)

                act.wait_ge(r_one, 2)
                evacuate(0, 0)
                evacuate(1, 1)
                with act.Fori(0, NG // RING - 1) as i:
                    for n in range(RING):
                        evacuate(RING * i + n + 2, (n + 2) % RING)
                        relu(RING * i + n, n)
                for n in range(RING):
                    pair = NG - RING + n
                    if n < RING - 2:
                        evacuate(pair + 2, n + 2)
                    relu(pair, n)

            @block.vector
            def _(v):
                v.sem_inc(h_ok, 4)
                v.sem_inc(s_ok, 2)
                v.sem_inc(oh_ok, 8)
                v.sem_inc(low_ok, 4)
                v.memset(s.big_s[:, :], 0.0)
                v.tensor_copy(w1c_high[:, :], s.w1c[:, :])
                v.tensor_copy(ident_r[:, :], s.ident[:, :])
                v.memset(edge_one[:, 0:1], 1.0)
                v.memset(edge_one[:, 1:2], 0.0)
                v.memset(r_full[:, :, H:SW], 1.0).then_inc(r_one, 1)
                v.wait_ge(r_one, 1)
                for q in range(4):
                    last = v.tensor_copy(r_high[:, q, H:SW + 1], edge_one[:, :])
                last.then_inc(r_one, 1)
                v.tensor_tensor(w1c_low[:, :], s.w1c[:, :], w1c_high[:, :].bitcast(F32), ALU.subtract)

                def onehot(pair, n, load):
                    c = n // LOAD
                    v.wait_ge(eb_in[c], load)
                    v.wait_ge(s_mm, pair + 1)
                    rows = eb[:, c, n % LOAD, :, ED + 1:EW].to_broadcast([P, 2, P])
                    v.tensor_tensor(onehots[:, n, :, :], s.iota_f[:, :].unsqueeze(1).to_broadcast([P, 2, P]), rows,
                                    ALU.is_equal).then_inc(oh_ok, 1)

                def low_parts(pair, n):
                    q = n % 4
                    v.wait_ge(t_ok, pair + 3)
                    v.tensor_tensor(eaT[ED:P, q, :], s.bank[TR_BANKS[q]][0:ED, 0:2 * P], eaT[0:ED, q, :].bitcast(F32),
                                    ALU.subtract).then_inc(low_ok, 1)

                def add_q(pair, n, uses):
                    b, q = n % 2, n % 4
                    v.wait_ge(h_mm, pair + 5)
                    v.wait_ge(gathered[q], uses)
                    v.wait_ge(r_ok, pair + 1)
                    v.tensor_tensor(hq[:, n % 4, :, :].rearrange("p j f -> p (j f)"), s.bank[2 + b][:, :],
                                    qg[:, q, :, :].rearrange("p j f -> p (j f)"), ALU.add).then_inc(h_ok, 1)

                def relu_low(pair, n):
                    b = n % 2
                    v.wait_ge(r_ok, pair + 3)
                    v.scalar_tensor_tensor(out=r_low[:, n % 4, :], in0=hq[:, n % 4, 0, :], scalar=0.0,
                                           in1=r_high[:, n % 4, 0:H].bitcast(F32), op0=ALU.max,
                                           op1=ALU.subtract).then_inc(rl_ok, 1)

                def add_s(pair, n, block_of):
                    b = n % 2
                    v.wait_ge(s_mm, pair + 9)
                    v.wait_ge(s_ok, pair + 2)
                    rows = s.big_s[:, ds(block_of * SW, SW)]
                    v.tensor_tensor(rows, rows, s.bank[6 + b][:, 0:SW], ALU.add).then_inc(s_ok, 1)

                def load_blocks(at, count):
                    _, blk = nc.values_load_multi_w_load_instructions(
                        s.blk_i[0:1, ds(at, count)], engines=(mybir.EngineType.DVE,), min_val=0, max_val=NB - 1,
                        skip_runtime_bounds_check_because="the table is capped at the last block")
                    return blk

                def turn(i, first, last):
                    blk = load_blocks(RING * i, RING) if first else load_blocks(RING * i - 2, RING)
                    for n in range(RING):
                        pair = RING * i + n
                        add_q(pair, n, 64 * i + 32 * (n // 4) + 32)
                        if not (last and n >= RING - 2):
                            low_parts(pair + 2, (n + 2) % RING)
                        if not (last and n >= RING - 4):
                            onehot(pair + 4, (n + 4) % RING, 16 * (i + (n + 4) // RING) + 16)
                        if not (first and n == 0):
                            relu_low(pair - 1, (n - 1) % RING)
                        if not (first and n < 2):
                            add_s(pair - 2, (n - 2) % RING, blk[n - 2] if first else blk[n])

                for n in range(4):
                    onehot(n, n, 16)
                low_parts(0, 0)
                low_parts(1, 1)
                turn(0, True, False)
                with v.Fori(1, NG // RING - 1) as i:
                    turn(i, False, False)
                turn(NG // RING - 1, False, True)
                relu_low(NG - 1, RING - 1)
                blk = load_blocks(NG - 2, 2)
                for k in range(2):
                    add_s(NG - 2 + k, RING - 2 + k, blk[k])


def gru(nc, s, a):
    with ExitStack() as ctx:
        def sb(name, shape, dt=F32):
            return ctx.enter_context(nc.sbuf_tensor(name, shape, dt))

        sem = s.sem

        sums = sb("sums", [P, 2, SW])
        sT = sb("sT", [P, 2, 2, P])
        degT = sb("degT", [2, 2, P])
        ght = sb("ght", [P, 2, H3])
        xnt = sb("xnt", [P, 2, H])
        xmt = sb("xmt", [P, 2, H])
        rz = sb("rz", [P, 2, 2 * H])
        cand = sb("cand", [P, 2, H])

        gh_in, x_in = sem("gh_in", 2), sem("xn_and_xm_in", 2)
        s_cp, s_tr, s_ok, rz_mm, n_mm = sem("sums_copied"), sem("sums_transposed"), sem("sT_made"), sem("rz_mm"), sem("n_mm")
        rz_in, rz_ok, c_in, c_ok, done, deg_one = (sem("rz_summed"), sem("rz_made"), sem("cand_summed"), sem("cand_made"),
                                                   sem("tile_done"), sem("deg_ones"))

        with nc.Block() as block:
            @block.sync
            def _(sp):
                with sp.Fori(0, NT // 2) as i:
                    for j in range(2):
                        one = ds(2 * i + j, 1)
                        sp.wait_ge(c_in, 2 * i + j + 1)
                        sp.dma_start(ght[:, j, :], s.gh_d[one].rearrange("t p f -> p (t f)")).then_inc(gh_in[j], 16)
                        sp.wait_ge(done, 2 * i + j + 1)
                        sp.dma_start(xnt[:, j, :], s.xn_d[one].rearrange("t p f -> p (t f)")).then_inc(x_in[j], 16)
                        sp.dma_start(xmt[:, j, :], s.xm_d[one].rearrange("t p f -> p (t f)")).then_inc(x_in[j], 16)

            @block.tensor
            def _(pe):
                pe.sem_inc(s_tr, 2)
                pe.sem_inc(n_mm, 2)

                def transposes(t, j):
                    pe.wait_ge(s_cp, t + 1)
                    pe.wait_ge(s_ok, t + 1)
                    for c in range(2):
                        nc.tensor.transpose(s.bank[j][:, c * P:(c + 1) * P], sums[:, j, c * P:(c + 1) * P], s.ident[:, :])
                    nc.tensor.transpose(s.bank[j][0:1, 2 * P:3 * P], sums[:, j, H:SW], s.ident[:, :]).then_inc(s_tr, 1)

                def products(t, j):
                    pe.wait_ge(s_ok, t + 3)
                    pe.wait_ge(c_in, t + 1)
                    for bank, lo, hi, signal in ((2 + j, 0, 512, rz_mm), (4 + j, 512, H3, n_mm)):
                        for c in range(2):
                            nc.tensor.matmul(s.bank[bank][:, 0:hi - lo], sT[:, j, c, :], s.wg[:, c, lo:hi],
                                             start=c == 0, stop=False)
                        nc.tensor.matmul(s.bank[bank][:, 0:hi - lo], degT[:, j, :], s.bg[:, lo:hi],
                                         start=False, stop=True).then_inc(signal, 1)

                transposes(0, 0)
                with pe.Fori(0, NT // 2 - 1) as i:
                    for j in range(2):
                        transposes(2 * i + j + 1, 1 - j)
                        products(2 * i + j, j)
                transposes(NT - 1, 1)
                products(NT - 2, 0)
                products(NT - 1, 1)

            @block.scalar
            def _(act):
                act.sem_inc(s_ok, 2)
                act.wait_ge(deg_one, 1)

                def copy_sums(t, j):
                    act.wait_ge(s_tr, t + 1)
                    nc.scalar.copy(sums[:, j, :], s.big_s[:, ds(t * SW, SW)]).then_inc(s_cp, 1)

                def evacuate(t, j):
                    act.wait_ge(s_tr, t + 3)
                    act.wait_ge(n_mm, t + 1)
                    nc.scalar.copy(degT[0:1, j, :], s.bank[j][0:1, 2 * P:3 * P])
                    nc.scalar.copy(sT[:, j, :, :], s.bank[j][:, 0:H].rearrange("p (c n) -> p c n", c=2)).then_inc(s_ok, 1)

                def gates(t, j):
                    act.wait_ge(rz_in, t + 1)
                    nc.scalar.activation(rz[:, j, :], rz[:, j, :], ACT.Sigmoid).then_inc(rz_ok, 1)
                    act.wait_ge(c_in, t + 3)
                    nc.scalar.activation(cand[:, j, :], cand[:, j, :], ACT.Tanh).then_inc(c_ok, 1)

                copy_sums(0, 0)
                copy_sums(1, 1)
                evacuate(0, 0)
                with act.Fori(0, NT // 2 - 1) as i:
                    for j in range(2):
                        evacuate(2 * i + j + 1, 1 - j)
                        copy_sums(2 * i + j + 2, j)
                        gates(2 * i + j, j)
                evacuate(NT - 1, 1)
                gates(NT - 2, 0)
                gates(NT - 1, 1)

            @block.vector
            def _(v):
                ch = Chain(v, s.v_step, s.v_steps)
                v.sem_inc(done, 2)
                v.sem_inc(c_in, 2)
                v.memset(degT[:, :, :], 1.0).then_inc(deg_one, 1)
                base = ch.n

                def gate_sums(t, j, turn):
                    v.wait_ge(rz_mm, t + 1)
                    v.wait_ge(gh_in[j], 16 * turn + 16)
                    v.tensor_tensor(rz[:, j, :], s.bank[2 + j][:, :], ght[:, j, 0:512], ALU.add).then_inc(rz_in, 1)

                def candidate(t, j):
                    ch.n = base + 6 * t
                    v.wait_ge(rz_ok, t + 1)
                    v.wait_ge(n_mm, t + 3)
                    ch.then(v.tensor_tensor(cand[:, j, :], rz[:, j, 0:H], ght[:, j, 512:H3], ALU.mult))
                    v.tensor_tensor(cand[:, j, :], cand[:, j, :], s.bank[4 + j][:, 0:H], ALU.add).then_inc(c_in, 1)

                def update(t, j, turn):
                    ch.n = base + 6 * t + 1
                    v.wait_ge(c_ok, t + 1)
                    v.wait_ge(x_in[j], 32 * turn + 32)
                    x1 = s.x1_all[:, ds(t * H, H)]
                    ch.mark(v.tensor_tensor(xnt[:, j, :], xnt[:, j, :], cand[:, j, :], ALU.subtract))
                    ch.mark(v.tensor_tensor(xmt[:, j, :], xmt[:, j, :], cand[:, j, :], ALU.add))
                    ch.all_but(1)
                    ch.mark(v.tensor_tensor(xnt[:, j, :], xnt[:, j, :], rz[:, j, H:2 * H], ALU.mult))
                    ch.all_but(0)
                    ch.mark(v.tensor_tensor(x1, xmt[:, j, :], xnt[:, j, :], ALU.add))
                    ch.all_but(0)
                    v.sem_inc(done, 1)
                    ch.mark(v.bn_stats(s.st2[:, ds(t, 1), :].rearrange("p a b -> p (a b)"), x1))

                gate_sums(0, 0, 0)
                candidate(0, 0)
                gate_sums(1, 1, 0)
                update(0, 0, 0)
                candidate(1, 1)
                with v.Fori(1, NT // 2) as i:
                    gate_sums(2 * i, 0, i)
                    update(2 * i - 1, 1, i - 1)
                    candidate(2 * i, 0)
                    gate_sums(2 * i + 1, 1, i)
                    update(2 * i, 0, i)
                    candidate(2 * i + 1, 1)
                update(NT - 1, 1, NT // 2 - 1)
                s.v_steps = base + NT * 6


def routing(nc, s, a):
    with ExitStack() as ctx:
        def sb(name, shape, dt=F32):
            return ctx.enter_context(nc.sbuf_tensor(name, shape, dt))

        sem = s.sem

        W = NT * NX
        var, tmp = sb("var2", [P, NT]), sb("tmp2", [P, NT])
        mean, rstd = sb("mean2", [P, NT]), sb("rstd2", [P, NT])
        xl = sb("xl", [P, 2, H])
        xlT = sb("xlT", [P, 2, 2, P])
        lg, pr, t1, t2, t3 = (sb(n, [P, NT, NX]) for n in ("lg", "pr", "t1", "t2", "t3"))
        keyv = sb("keyv", [P, NX])
        basev = sb("basev", [P, NX])
        m1, m2, valid, gate = (sb(n, [P, NT]) for n in ("m1", "m2", "valid", "gate"))
        RR = 4
        xr = sb("xr", [P, RR, XW])
        xi = sb("xi", [P, RR], I32)
        zrow = sb("zrow2", [P, 8, XW])

        var_ok, root_ok = sem("var2_made"), sem("root2_made")
        xl_ok, xl_tr, xlT_ok, lg_mm, lg_ok = sem("xl_made"), sem("xl_transposed"), sem("xlT_made"), sem("lg_mm"), sem("lg_made")
        sh_ok, ex_ok, oh_ok, rank_mm = sem("shifted"), sem("exp_made"), sem("onehot2_made"), sem("rank_mm")
        z_ok, z_out, xr_ok, xr_out = sem("zeros_made"), s.pad_out, sem("xr_made"), sem("xr_out", RR)

        def flat(x):
            return x[:, :, :].rearrange("p t e -> p (t e)")

        def over(x, t=NT):
            return x.unsqueeze(2).to_broadcast([P, t, NX])

        with nc.Block() as block:
            @block.sync
            def _(sp):
                sp.wait_ge(z_ok, 1)
                rows, step = NX * CAP, P * 8
                n = 0
                for at in range(0, rows - step + 1, step):
                    sp.dma_start(s.routed_d[at:at + step, :].rearrange("(p r) w -> p r w", r=8), zrow[:, :, :]).then_inc(z_out, 16)
                    n += 1
                rest = rows - n * step
                if rest >= P:
                    k = rest // P
                    sp.dma_start(s.routed_d[rows - rest:rows - rest + k * P, :].rearrange("(p r) w -> p r w", r=k),
                                 zrow[:, 0:k, :]).then_inc(z_out, 16)
                    n += 1
                    rest -= k * P
                if rest:
                    sp.dma_start(s.routed_d[rows - rest:rows, :], zrow[0:rest, 0, :]).then_inc(z_out, 16)
                    n += 1
                assert n == ZERO_DMAS
                sp.wait_ge(z_out, 16 * (s.pads + n))

            @block.gpsimd
            def _(g):
                g.memset(zrow[:, :, :], 0.0).then_inc(z_ok, 1)
                for q in range(RR):
                    credit(s, g, xr_out[q], 16)
                g.wait_ge(z_out, 16 * (s.pads + ZERO_DMAS))

                def scatter(t, q):
                    g.wait_ge(xr_ok, t + 1)
                    apart(s, g)
                    g.indirect_dma_start(out=s.routed_d, out_offset=OFF(ap=xi[:, q:q + 1], axis=0),
                                         in_=xr[:, q, :], in_offset=None, bounds_check=NX * CAP - 1,
                                         oob_is_err=False).then_inc(xr_out[q], 16)

                with g.Fori(0, NT // RR) as i:
                    for q in range(RR):
                        scatter(RR * i + q, q)
                for t in range(NT // RR * RR, NT):
                    scatter(t, t % RR)
                for q in range(RR):
                    g.wait_ge(xr_out[q], 16 * (-(-(NT - q) // RR) + 1))

            @block.tensor
            def _(pe):
                pe.sem_inc(xl_tr, 2)
                pe.sem_inc(lg_mm, 2)

                def transposes(t, j):
                    pe.wait_ge(xl_ok, t + 1)
                    pe.wait_ge(xlT_ok, t + 1)
                    for c in range(2):
                        last = nc.tensor.transpose(s.bank[j][:, c * P:(c + 1) * P], xl[:, j, c * P:(c + 1) * P], s.ident[:, :])
                    last.then_inc(xl_tr, 1)

                def logits(t, j):
                    pe.wait_ge(xlT_ok, t + 3)
                    pe.wait_ge(lg_ok, t + 1)
                    for c in range(2):
                        last = nc.tensor.matmul(s.bank[2 + j][:, 0:NX], xlT[:, j, c, :], s.gatew[:, c, :],
                                                start=c == 0, stop=c == 1)
                    last.then_inc(lg_mm, 1)

                transposes(0, 0)
                with pe.Fori(0, NT // 2 - 1) as i:
                    for j in range(2):
                        transposes(2 * i + j + 1, 1 - j)
                        logits(2 * i + j, j)
                transposes(NT - 1, 1)
                logits(NT - 2, 0)
                logits(NT - 1, 1)
                pe.wait_ge(oh_ok, 1)
                nc.tensor.matmul(s.bank[4][:, 0:W], s.upper[:, :], flat(t1), start=True, stop=True)
                nc.tensor.matmul(s.bank[5][:, 0:W], s.ones[:, :], flat(t1), start=True, stop=True).then_inc(rank_mm, 1)

            @block.scalar
            def _(act):
                act.wait_ge(var_ok, 1)
                nc.scalar.activation(rstd[:, :], var[:, :], ACT.Sqrt).then_inc(root_ok, 1)
                act.sem_inc(xlT_ok, 2)
                with act.Fori(0, NT // 2) as i:
                    for j in range(2):
                        t = 2 * i + j
                        act.wait_ge(xl_tr, t + 3)
                        act.wait_ge(lg_mm, t + 1)
                        nc.scalar.copy(xlT[:, j, :, :], s.bank[j][:, 0:H].rearrange("p (c n) -> p c n", c=2)).then_inc(xlT_ok, 1)
                act.wait_ge(sh_ok, 1)
                nc.scalar.activation(flat(lg), flat(lg), ACT.Exp).then_inc(ex_ok, 1)

            @block.vector
            def _(v):
                ch = Chain(v, s.v_step, s.v_steps)
                batch_norm_factors(v, ch, s.st2, mean[:, :], var[:, :], tmp[:, :])
                v.tensor_copy(tmp[:, :], var[:, :]).then_inc(var_ok, 1)
                v.wait_ge(root_ok, 1)
                ch.then(v.reciprocal(rstd[:, :], rstd[:, :]))
                v.sem_inc(lg_ok, 2)

                def normed(t, j):
                    v.wait_ge(xl_tr, t + 1)
                    v.tensor_scalar(xl[:, j, :], s.x1_all[:, ds(t * H, H)], mean[:, ds(t, 1)], rstd[:, ds(t, 1)],
                                    ALU.subtract, ALU.mult).then_inc(xl_ok, 1)

                def biased(t, j):
                    v.wait_ge(lg_mm, t + 3)
                    v.tensor_tensor(lg[:, ds(t, 1), :].rearrange("p a e -> p (a e)"), s.bank[2 + j][:, 0:NX],
                                    s.gateb[:, :], ALU.add).then_inc(lg_ok, 1)

                normed(0, 0)
                normed(1, 1)
                with v.Fori(0, NT // 2 - 1) as i:
                    for j in range(2):
                        normed(2 * i + j + 2, j)
                        biased(2 * i + j, j)
                for j in range(2):
                    biased(NT - 2 + j, j)
                v.wait_ge(lg_ok, NT + 2)
                ch.then(v.tensor_reduce(m1[:, :], lg[:, :, :], AX.X, ALU.max))
                v.tensor_tensor(lg[:, :, :], lg[:, :, :], over(m1[:, :]), ALU.subtract).then_inc(sh_ok, 1)
                v.wait_ge(ex_ok, 1)
                ch.then(v.tensor_reduce(m1[:, :], lg[:, :, :], AX.X, ALU.add))
                ch.then(v.reciprocal(m1[:, :], m1[:, :]))
                ch.then(v.tensor_tensor(pr[:, :, :], lg[:, :, :], over(m1[:, :]), ALU.mult))
                ch.then(v.tensor_reduce(gate[:, :], pr[:, :, :], AX.X, ALU.max))
                ch.then(v.tensor_scalar(keyv[:, :], s.iota_f[:, 0:NX], -1.0, float(NX), ALU.mult, ALU.add))
                ch.then(v.tensor_tensor(t1[:, :, :], pr[:, :, :], over(gate[:, :]), ALU.is_equal))
                ch.then(v.tensor_tensor(t1[:, :, :], t1[:, :, :], keyv[:, :].unsqueeze(1).to_broadcast([P, NT, NX]), ALU.mult))
                ch.then(v.tensor_reduce(m1[:, :], t1[:, :, :], AX.X, ALU.max))
                ch.then(v.tensor_tensor(t1[:, :, :], t1[:, :, :], over(m1[:, :]), ALU.is_equal))
                ch.then(v.tensor_scalar(valid[:, :], s.node_f[:, :], float(N), None, ALU.is_lt))
                v.tensor_tensor(t1[:, :, :], t1[:, :, :], over(valid[:, :]), ALU.mult).then_inc(oh_ok, 1)
                v.wait_ge(rank_mm, 1)
                ch.then(v.tensor_copy(flat(t2), s.bank[5][:, 0:W]))
                for e in range(NX):
                    last = v.tensor_tensor_scan(t3[:, :, e], s.ones[:, 0:NT], t2[:, :, e], 0.0, ALU.mult, ALU.add)
                ch.then(last)
                ch.then(v.tensor_tensor(flat(t3), flat(t3), flat(t2), ALU.subtract))
                ch.then(v.tensor_tensor(flat(t3), flat(t3), s.bank[4][:, 0:W], ALU.add))
                ch.then(v.tensor_tensor(flat(t2), flat(t3), flat(t1), ALU.mult))
                ch.then(v.tensor_reduce(m1[:, :], t2[:, :, :], AX.X, ALU.add))
                ch.then(v.tensor_scalar(s.kept[:, :], m1[:, :], float(CAP), None, ALU.is_lt))
                ch.then(v.tensor_tensor(s.kept[:, :], s.kept[:, :], valid[:, :], ALU.mult))
                ch.then(v.tensor_scalar(basev[:, :], s.iota_f[:, 0:NX], float(CAP), None, ALU.mult))
                ch.then(v.tensor_tensor(t2[:, :, :], t1[:, :, :], basev[:, :].unsqueeze(1).to_broadcast([P, NT, NX]), ALU.mult))
                ch.then(v.tensor_reduce(m2[:, :], t2[:, :, :], AX.X, ALU.add))
                ch.then(v.tensor_tensor(m1[:, :], m1[:, :], m2[:, :], ALU.add))
                ch.then(v.tensor_tensor(m1[:, :], m1[:, :], s.kept[:, :], ALU.mult))
                ch.then(v.tensor_copy(s.place[:, :], m1[:, :]))
                ch.then(v.tensor_scalar(m2[:, :], s.kept[:, :], -float(2 * NX * CAP), float(2 * NX * CAP), ALU.mult, ALU.add))
                ch.then(v.tensor_tensor(m1[:, :], m1[:, :], m2[:, :], ALU.add))
                s.v_steps = ch.n

                def row(t, q, turn):
                    v.wait_ge(xr_out[q], 16 * turn + 16)
                    v.tensor_scalar(xr[:, q, 0:H], s.x1_all[:, ds(t * H, H)], mean[:, ds(t, 1)], rstd[:, ds(t, 1)],
                                    ALU.subtract, ALU.mult)
                    v.tensor_copy(xr[:, q, H:XW], gate[:, ds(t, 1)])
                    v.tensor_copy(xi[:, q:q + 1], m1[:, ds(t, 1)]).then_inc(xr_ok, 1)

                with v.Fori(0, NT // RR) as i:
                    for q in range(RR):
                        row(RR * i + q, q, i)
                for t in range(NT // RR * RR, NT):
                    row(t, t % RR, t // RR)


def experts(nc, s, a):
    with ExitStack() as ctx:
        def sb(name, shape, dt=F32):
            return ctx.enter_context(nc.sbuf_tensor(name, shape, dt))

        sem = s.sem

        FT = FF // P
        Q = 2 * FT
        EVEN = CAP + CAP % 2
        CUT = -(-EVEN // 4) * 2
        HALVES = ((0, CUT), (CUT, EVEN))
        w1, w2 = sb("w1", [P, 2, FF]), sb("w2", [P, FT, H])
        w1_high, w1_low = sb("w1_high", [P, 2, FF], F32R), sb("w1_low", [P, 2, FF], F32R)
        w2_high, w2_low = sb("w2_high", [P, FT, H], F32R), sb("w2_low", [P, FT, H], F32R)
        xT_high, xT_low = sb("xT_high", [P, 2, EVEN], F32R), sb("xT_low", [P, 2, EVEN], F32R)
        hT_high, hT_low = sb("hT_high", [P, FT, EVEN], F32R), sb("hT_low", [P, FT, EVEN], F32R)
        hid = sb("hid", [P, 3, HALVES[0][1]])
        b1T = sb("b1T", [P, NX * FT])
        b1e = sb("b1e", [P, 2, FT])
        b2b = sb("b2b", [P, 2, H])
        xg = sb("xg", [P, 2, CT, XW])
        y = sb("y", [P, 2, H])
        b1raw = y[0:NX * FT, 0, 0:P]
        fix = sb("fix", [P, 2])
        mask = sb("mask", [P, 3, H], BF16)

        b1_in, b1_tr, b1_ok = sem("b1_in"), sem("b1_tr"), sem("b1_made")
        w1_in, w2_in, x_in = sem("w1_in"), sem("w2_in"), sem("x_in6", 2)
        x_tr, x_ok, h_mm, h_ok, y_mm, y_st, y_ok = (sem("x_tr6"), sem("xT_made"), sem("h_mm6"), sem("hidden_made"), sem("y_mm"),
                                                    sem("y_stored", 2), sem("y_made"))
        ((w1h_ok, W1H), (w1l_ok, W1L), (w2h_ok, W2H), (w2l_ok, W2L), (xl_ok, XL), (hh_ok, HH), (hl_ok, HL),
         (yg_ok, YG)) = s.spent
        w1_v = a.fw1.rearrange("e (c p) f -> e p c f", p=P)
        w2_v = a.fw2.rearrange("e (k p) d -> e p k d", p=P)
        rows_v = s.routed_d.rearrange("(e c) w -> e c w", e=NX)
        y_v = s.y_d.rearrange("(e c) w -> e c w", e=NX)
        FULL = (CT - 1) * P

        def rows_of(t):
            return P if t < CT - 1 else CLAST

        def next_tiles(t, last):
            return () if last else range(min(2 * t, CT), min(2 * t + 2, CT))

        def step(q):
            return q % FT, HALVES[q // FT]

        def turns(eng, expert):
            with eng.Fori(0, NX // 2 - 1) as i:
                for j in range(2):
                    expert(2 * i + j, j, i, False)
            expert(NX - 2, 0, NX // 2 - 1, False)
            expert(NX - 1, 1, NX // 2 - 1, True)

        with nc.Block() as block:
            @block.sync
            def _(sp):
                sp.dma_start(b1raw, a.fb1.rearrange("e (k p) -> (e k) p", p=P)).then_inc(b1_in, 16)

                def load(e, j, first):
                    one = ds(e, 1)
                    sp.wait_ge(w1l_ok, W1L + e)
                    sp.dma_start(w1[:, :, :], w1_v[one].rearrange("e p c f -> p (e c) f")).then_inc(w1_in, 16)
                    if not first:
                        sp.wait_ge(y_ok, (e - 1) * CT + 2)
                    sp.dma_start(xg[:, j, 0:CT - 1, :], rows_v[one, 0:FULL, :].rearrange("e (t p) w -> p (e t) w", p=P)).then_inc(x_in[j], 16)
                    sp.dma_start(xg[0:CLAST, j, CT - 1, :], rows_v[one, FULL:CAP, :].rearrange("e p w -> p (e w)")).then_inc(x_in[j], 16)
                    sp.dma_start(b2b[:, j, :], a.fb2[one].rearrange("e d -> (e d)").partition_broadcast(P)).then_inc(x_in[j], 16)
                    sp.wait_ge(w2l_ok, W2L + e)
                    sp.dma_start(w2[:, :, :], w2_v[one].rearrange("e p k d -> p (e k) d")).then_inc(w2_in, 16)

                for j in range(2):
                    load(j, j, True)
                with sp.Fori(1, NX // 2) as i:
                    for j in range(2):
                        load(2 * i + j, j, False)

            @block.tensor
            def _(pe):
                pe.wait_ge(b1_in, 16)
                nc.tensor.transpose(s.bank[0][:, 0:NX * FT], b1raw, s.ident[0:NX * FT, 0:NX * FT]).then_inc(b1_tr, 1)
                pe.wait_ge(b1_ok, 1)
                pe.sem_inc(y_mm, 2)

                def transposes(e, j, t):
                    rows = rows_of(t)
                    pe.wait_ge(xl_ok, XL + e * CT + t + 1)
                    for c in range(2):
                        last = nc.tensor.transpose(s.bank[t % 2][:, c * P:c * P + rows], xg[0:rows, j, t, c * P:(c + 1) * P],
                                                   s.ident[0:rows, 0:rows])
                    last.then_inc(x_tr, 1)

                def three(into, terms, signal):
                    for n, ((lh, ll), (rh, rl)) in enumerate(terms):
                        nc.tensor.matmul(into, lh, rh, start=n == 0, stop=False)
                        nc.tensor.matmul(into, lh, rl, start=False, stop=False)
                        last = nc.tensor.matmul(into, ll, rh, start=False, stop=n == len(terms) - 1)
                    last.then_inc(signal, 1)

                def expert(e, j, turn, last):
                    pe.wait_ge(xl_ok, XL + (e + 1) * CT + 2)
                    pe.wait_ge(w1l_ok, W1L + e + 1)
                    for q in range(Q):
                        f, (lo, hi) = step(q)
                        part = slice(f * P, (f + 1) * P)
                        pe.wait_ge(h_ok, e * Q + q + 1)
                        three(s.bank[2 + q % 4][:, 0:hi - lo],
                              [((w1_high[:, c, part], w1_low[:, c, part]), (xT_high[:, c, lo:hi], xT_low[:, c, lo:hi]))
                               for c in range(2)], h_mm)
                    pe.wait_ge(w2l_ok, W2L + e + 1)
                    if not last:
                        pe.wait_ge(x_in[1 - j], 48 * (turn + j) + 48)
                    for t in range(CT):
                        for u in next_tiles(t, last):
                            transposes(e + 1, 1 - j, u)
                        rows = rows_of(t)
                        part = slice(t * P, t * P + rows)
                        pe.wait_ge(hl_ok, HL + e * Q + 2 + (FT if t * P + rows <= CUT else Q))
                        pe.wait_ge(yg_ok, YG + e * CT + t + 1)
                        three(s.bank[6 + t % 2][0:rows, 0:H],
                              [((hT_high[:, f, part], hT_low[:, f, part]), (w2_high[:, f, :], w2_low[:, f, :]))
                               for f in range(FT)], y_mm)

                pe.wait_ge(x_in[0], 48)
                for t in range(CT):
                    transposes(0, 0, t)
                turns(pe, expert)

            @block.scalar
            def _(act):
                act.sem_inc(h_ok, 4)
                act.sem_inc(yg_ok, 2)
                act.wait_ge(b1_tr, 1)
                nc.scalar.copy(b1T[:, :], s.bank[0][:, 0:NX * FT]).then_inc(b1_ok, 1)
                act.wait_ge(b1_ok, 1)

                def x_high(e, t):
                    rows = rows_of(t)
                    act.wait_ge(x_tr, e * CT + t + 1)
                    nc.scalar.copy(xT_high[:, :, t * P:t * P + rows],
                                   s.bank[t % 2][:, 0:H].rearrange("p (c n) -> p c n", c=2)[:, :, 0:rows]).then_inc(x_ok, 1)

                def hidden_high(e, q):
                    f, (lo, hi) = step(q)
                    act.wait_ge(h_ok, e * Q + q + 5)
                    nc.scalar.copy(hT_high[:, f, lo:hi], hid[:, q % 3, 0:hi - lo]).then_inc(hh_ok, 1)

                def expert(e, j, turn, last):
                    nc.scalar.copy(b1e[:, j, :], b1T[:, ds(e * FT, FT)]).then_inc(b1_ok, 1)
                    act.wait_ge(b1_ok, e + 2)
                    act.wait_ge(y_mm, e * CT + 2)
                    for q in range(Q):
                        f, (lo, hi) = step(q)
                        act.wait_ge(h_mm, e * Q + q + 1)
                        act.wait_ge(hl_ok, HL + e * Q + 2 + max(0, q - 2))
                        nc.scalar.activation(hid[:, q % 3, 0:hi - lo], s.bank[2 + q % 4][:, 0:hi - lo], ACT.Relu,
                                             bias=b1e[:, j, f:f + 1]).then_inc(h_ok, 1)
                        if q > 0:
                            hidden_high(e, q - 1)
                        if q == 3:
                            act.wait_ge(w2_in, 16 * e + 16)
                            nc.scalar.copy(w2_high[:, :, :], w2[:, :, :]).then_inc(w2h_ok, 1)
                    hidden_high(e, Q - 1)
                    if not last:
                        act.wait_ge(w1_in, 16 * e + 32)
                        nc.scalar.copy(w1_high[:, :, :], w1[:, :, :]).then_inc(w1h_ok, 1)
                    for t in range(CT):
                        for u in next_tiles(t, last):
                            x_high(e + 1, u)
                        rows = rows_of(t)
                        act.wait_ge(y_mm, e * CT + t + 3)
                        act.wait_ge(y_st[t % 2], 16 * (e * (CT // 2) + t // 2) + 16)
                        nc.scalar.mul(y[0:rows, t % 2, :], s.bank[6 + t % 2][0:rows, 0:H],
                                      xg[0:rows, j, t, H:XW]).then_inc(yg_ok, 1)

                act.wait_ge(w1_in, 16)
                nc.scalar.copy(w1_high[:, :, :], w1[:, :, :]).then_inc(w1h_ok, 1)
                act.wait_ge(x_in[0], 48)
                for t in range(CT):
                    x_high(0, t)
                turns(act, expert)

            @block.vector
            def _(v):
                ch = Chain(v, s.v_step, s.v_steps)
                if EVEN > CAP:
                    for to in (xT_high, xT_low):
                        v.tensor_copy(to[:, :, CAP:EVEN].rearrange("p c a -> p (c a)"), s.zerob[:, :])
                v.sem_inc(xl_ok, 2)
                v.sem_inc(hl_ok, 2)
                v.sem_inc(y_ok, 2)
                ch.then(v.memset(fix[:, 0:1], 1e4))
                ch.then(v.memset(fix[:, 1:2], -1e4))
                base = ch.n

                def x_low(e, t):
                    rows = rows_of(t)
                    to = slice(t * P, t * P + rows)
                    v.wait_ge(x_ok, e * CT + t + 1)
                    v.tensor_tensor(xT_low[:, :, to], s.bank[t % 2][:, 0:H].rearrange("p (c n) -> p c n", c=2)[:, :, 0:rows],
                                    xT_high[:, :, to].bitcast(F32), ALU.subtract).then_inc(xl_ok, 1)

                def expert(e, j, turn, last):
                    for q in range(Q):
                        f, (lo, hi) = step(q)
                        v.wait_ge(hh_ok, HH + e * Q + q + 1)
                        v.tensor_tensor(hT_low[:, f, lo:hi], hid[:, q % 3, 0:hi - lo], hT_high[:, f, lo:hi].bitcast(F32),
                                        ALU.subtract).then_inc(hl_ok, 1)
                    v.wait_ge(x_in[j], 48 * turn + 48)
                    for t in range(CT):
                        for u in next_tiles(t, last):
                            x_low(e + 1, u)
                        rows = rows_of(t)
                        ch.n = base + (e * CT + t) * 4
                        yt = y[0:rows, t % 2, :]
                        v.wait_ge(yg_ok, YG + e * CT + t + 3)
                        ch.then(v.scalar_tensor_tensor(out=yt, in0=b2b[0:rows, j, :], scalar=xg[0:rows, j, t, H:XW], in1=yt,
                                                       op0=ALU.mult, op1=ALU.add))
                        v.tensor_tensor(mask[0:rows, 0, :], yt, yt, ALU.not_equal)
                        v.tensor_scalar(mask[0:rows, 1, :], yt, FMAX, None, ALU.is_gt)
                        ch.then(v.tensor_scalar(mask[0:rows, 2, :], yt, -FMAX, None, ALU.is_lt))
                        apart(s, v)
                        ch.then(v.copy_predicated(yt, mask[0:rows, 0, :].bitcast(U16), s.zerob[0:rows, 0:1].to_broadcast([rows, H])))
                        apart(s, v)
                        ch.then(v.copy_predicated(yt, mask[0:rows, 1, :].bitcast(U16), fix[0:rows, 0:1].to_broadcast([rows, H])))
                        apart(s, v)
                        v.copy_predicated(yt, mask[0:rows, 2, :].bitcast(U16), fix[0:rows, 1:2].to_broadcast([rows, H])).then_inc(y_ok, 1)

                for t in range(CT):
                    x_low(0, t)
                turns(v, expert)

            @block.gpsimd
            def _(g):
                for j in range(2):
                    credit(s, g, y_st[j], 16)

                def expert(e, j, turn, last):
                    g.wait_ge(w2h_ok, W2H + e + 1)
                    g.tensor_tensor(w2_low[:, :, :], w2[:, :, :], w2_high[:, :, :].bitcast(F32), ALU.subtract).then_inc(w2l_ok, 1)
                    if not last:
                        g.wait_ge(w1h_ok, W1H + e + 2)
                        g.tensor_tensor(w1_low[:, :, :], w1[:, :, :], w1_high[:, :, :].bitcast(F32), ALU.subtract).then_inc(w1l_ok, 1)
                    for t in range(CT):
                        rows = rows_of(t)
                        g.wait_ge(y_ok, e * CT + t + 3)
                        g.dma_start(y_v[ds(e, 1), t * P:t * P + rows, :].rearrange("e p w -> p (e w)"),
                                    y[0:rows, t % 2, :]).then_inc(y_st[t % 2], 16)

                g.wait_ge(w1h_ok, W1H + 1)
                g.tensor_tensor(w1_low[:, :, :], w1[:, :, :], w1_high[:, :, :].bitcast(F32), ALU.subtract).then_inc(w1l_ok, 1)
                turns(g, expert)
                for j in range(2):
                    g.wait_ge(y_st[j], 16 * NX * CT // 2 + 16)


def combine(nc, s, a):
    with ExitStack() as ctx:
        def sb(name, shape, dt=F32):
            return ctx.enter_context(nc.sbuf_tensor(name, shape, dt))

        sem = s.sem

        RC = 4
        yg = sb("yg", [P, RC, H])
        gi = sb("gi", [P, RC], I32)
        ot = sb("ot7", [P, RC, H])
        gi_ok = sem("place_copied")
        o_ok = sem("o_made")
        y_in, o_st = sem("y_in", RC), sem("o_stored", RC)
        full = REAL - 1
        assert full % RC == 0
        out_v = a.out[0:full * P, :].rearrange("(t p) f -> t p f", p=P)

        with nc.Block() as block:
            @block.gpsimd
            def _(g):
                def gather(q, n):
                    g.wait_ge(gi_ok, n + 1)
                    apart(s, g)
                    g.indirect_dma_start(out=yg[:, q, :], out_offset=None, in_=s.y_d,
                                         in_offset=OFF(ap=gi[:, q:q + 1], axis=0)).then_inc(y_in[q], 16)

                with g.Fori(0, full // RC) as i:
                    for q in range(RC):
                        gather(q, RC * i + q)
                gather(0, full)

            @block.vector
            def _(v):
                v.sem_inc(o_ok, RC)

                def place(q, t):
                    v.tensor_copy(gi[:, q:q + 1], s.place[:, ds(t, 1)]).then_inc(gi_ok, 1)

                def add(q, t, turns):
                    v.wait_ge(y_in[q], 16 * turns + 16)
                    v.wait_ge(o_st[q], 16 * turns + 16)
                    v.scalar_tensor_tensor(out=ot[:, q, :], in0=yg[:, q, :], scalar=s.kept[:, ds(t, 1)],
                                           in1=s.x1_all[:, ds(t * H, H)], op0=ALU.mult, op1=ALU.add).then_inc(o_ok, 1)
                    v.wait_ge(o_ok, t + RC + 1)

                for q in range(RC):
                    place(q, q)
                with v.Fori(0, full // RC - 1) as i:
                    for q in range(RC):
                        add(q, RC * i + q, i)
                        place(q, RC * i + q + RC)
                for q in range(RC):
                    add(q, full - RC + q, full // RC - 1)
                    if q == 0:
                        place(0, full)
                add(0, full, full // RC)

            @block.sync
            def _(sp):
                for q in range(RC):
                    credit(s, sp, o_st[q], 16)
                with sp.Fori(0, full // RC) as i:
                    for q in range(RC):
                        sp.wait_ge(o_ok, RC * i + q + RC + 1)
                        sp.dma_start(out_v[ds(RC * i + q, 1)].rearrange("t p f -> p (t f)"), ot[:, q, :]).then_inc(o_st[q], 16)
                sp.wait_ge(o_ok, full + RC + 1)
                sp.dma_start(a.out[full * P:N, :], ot[0:TAIL, 0, :]).then_inc(o_st[0], 16)
                for q in range(RC):
                    sp.wait_ge(o_st[q], 16 * (full // RC + 1 + (q == 0)))


def build(nc, a):
    with ExitStack() as ctx:
        def sb(name, shape, dt=F32):
            return ctx.enter_context(nc.sbuf_tensor(name, shape, dt))

        def dram(name, shape):
            return nc.dram_tensor(name, shape, F32).ap()

        def sem(name, n=None):
            if n is None:
                return ctx.enter_context(nc.semaphore(name))
            return [ctx.enter_context(nc.semaphore(f"{name}{k}")) for k in range(n)]

        s = Shared()
        s.sem = sem
        s.carried = sem("waits_carried")
        s.x_in = sem("x_in")
        s.pad_out, s.pads = sem("padding_out"), 0
        s.p_step, s.p_steps = sem("p_step"), 0
        s.v_step, s.v_steps = sem("v_step"), 0
        s.bank = [ctx.enter_context(nc.psum_tensor(f"bank{k}", [P, 512], F32)) for k in range(8)]
        s.x_pad = dram("x_pad", [NTX, P, H])
        s.xn_d = dram("xn_d", [NT, P, H])
        s.q_tab = dram("q_tab", [NT * P, H])
        s.q_tiles = s.q_tab.rearrange("(t p) f -> t p f", p=P)
        s.v_d = dram("v_d", [NT, P, H])
        s.qs_d = dram("qs_d", [NT, P, H])
        s.gh_d = dram("gh_d", [NT, P, H3])
        s.xm_d = dram("xm_d", [NT, P, H])
        s.sorted_d = dram("sorted_d", [SLOTS, EW])
        s.routed_d = dram("routed_d", [NX * CAP, XW])
        s.y_d = dram("y_d", [NX * CAP, H])
        s.credit_d, s.credits = dram("credit_d", [32, 2]), 0
        s.big_p = sb("big_p", [P, NT * 2 * H], BF16)
        s.x1_all = s.big_p[:, :].bitcast(F32)
        s.ident = sb("ident", [P, P])
        s.iota_f = sb("iota_f", [P, P])
        s.node_f = sb("node_f", [P, NT])
        s.ones = sb("ones", [P, P])
        s.upper = sb("upper", [P, P])
        s.zerob = sb("zerob", [P, 2])
        s.gatew = sb("gatew", [P, 2, NX])
        s.gateb = sb("gateb", [P, NX])
        s.st2 = sb("st2_all", [P, NT, 6])
        s.kept = sb("kept", [P, NT])
        s.place = sb("place", [P, NT], I32)
        with ExitStack() as graph:
            s.big_s = graph.enter_context(nc.sbuf_tensor("big_s", [P, NT * SW], F32))
            s.p3 = graph.enter_context(nc.sbuf_tensor("p3", [P, NT * H], BF16))
            s.blk_i = graph.enter_context(nc.sbuf_tensor("blk_i", [1, NG], I32))
            s.w1c = graph.enter_context(nc.sbuf_tensor("w1c", [P, H], F32))
            s.wg = graph.enter_context(nc.sbuf_tensor("wg", [P, 2, H3], F32))
            s.bg = graph.enter_context(nc.sbuf_tensor("bg", [2, H3], F32))
            with ExitStack() as early:
                def eb(name, shape, dt=F32):
                    return early.enter_context(nc.sbuf_tensor(name, shape, dt))

                s.fused_w = eb("fused_w", [P, 2, 4 * H])
                s.whhT = eb("whhT", [P, 2, H3])
                s.wk = eb("wk", [P, 2, H])
                s.wout = eb("wout", [P, 2, H])
                s.b1b = eb("b1b", [P, H])
                s.bhhb = eb("bhhb", [P, H3])
                s.gammab = eb("gammab", [P, H])
                s.dst_i = eb("dst_i", [P, EC + 1], I32)
                s.pos = eb("pos", [P, EC + 1])
                s.rowl = eb("rowl", [P, EC + 1], BF16)
                s.mean = eb("mean", [P, NT])
                s.rstd = eb("rstd", [P, NT])
                prepare(nc, s, a)
                nodes(nc, s, a)
            edges(nc, s, a)
            gru(nc, s, a)
        routing(nc, s, a)
        experts(nc, s, a)
        combine(nc, s, a)


_NAMES = {"x": "x", "src": "src", "dst": "dst", "edge_attr_64": "edge_attr", "L0_gnn_W1": "W1", "L0_gnn_b1": "b1",
          "L0_gnn_W2": "W2", "L0_gnn_b2": "b2", "L0_gnn_W_ih": "W_ih", "L0_gnn_b_ih": "b_ih",
          "L0_gnn_W_hh": "W_hh", "L0_gnn_b_hh": "b_hh", "L0_mix_Wqkv": "Wqkv", "L0_mix_Wout": "Wout",
          "L0_mix_gamma": "gamma", "L0_ffn_gate_w": "gate_w", "L0_ffn_gate_b": "gate_b", "L0_ffn_w1": "fw1",
          "L0_ffn_b1": "fb1", "L0_ffn_w2": "fw2", "L0_ffn_b2": "fb2"}


def kernel(**inputs):
    import numpy as _np
    import concourse.bacc as _bacc
    from concourse import mybir as _mybir
    from concourse.bass_utils import run_bass_kernel_spmd as _run

    nc = _bacc.Bacc("TRN2", target_bir_lowering=False, num_devices=1)
    arrays, args = {}, {}
    for name, short in _NAMES.items():
        arr = _np.ascontiguousarray(inputs[name])
        arrays[f"in_{name}"] = arr
        args[short] = nc.dram_tensor(f"in_{name}", arr.shape, _mybir.dt.from_np(arr.dtype), kind="ExternalInput").ap()
    args["out"] = nc.dram_tensor("out_dram", (N, H), F32, kind="ExternalOutput").ap()
    build(nc, Arrays(**args))
    r = _run(nc, [arrays], core_ids=[0])
    return r.results[0]["out_dram"]
```
